# Optimizing a Trainium2 kernel written in Bass

```python
import numpy as np
import jax
import jax.numpy as jnp

def _softmax(x, axis=-1):
    return jax.nn.softmax(x, axis=axis)

def _gelu(x):
    return jax.nn.gelu(x, approximate=True)

def _silu(x):
    return jax.nn.silu(x)

def _sigmoid(x):
    return jax.nn.sigmoid(x)

def _layernorm(x, axis=-1, eps=1e-05):
    m = jnp.mean(x, axis=axis, keepdims=True)
    v = jnp.var(x, axis=axis, keepdims=True)
    return (x - m) / jnp.sqrt(v + eps)

def _scatter_add(tgt, idx, src, axis=0):
    return tgt.at[idx].add(src)

def _segment_sum(src, seg, n):
    return jax.ops.segment_sum(src, seg, n)
kernel_name = 'mk_xattn_seq_d4_seqx_r8_04a61a'

def setup_inputs(seed: int=0):
    np.random.seed(seed)
    _w = jnp.asarray

    def _rec_inputs():
        import jax
        import jax.numpy as jnp
        _rk = jax.random.key(seed)
        x = -0.0005207 + 1.001 * jax.random.normal(jax.random.fold_in(_rk, 1), (16, 128, 256), jnp.float32)
        _lenS = 128 - jax.random.randint(jax.random.fold_in(_rk, 7), (16,), 0, max(1, 128 // 4) + 1, jnp.int32)
        _lenS2 = 128 - jax.random.randint(jax.random.fold_in(_rk, 8), (16,), 0, max(1, 128 // 4) + 1, jnp.int32)
        _ctx_2048P = jax.random.normal(jax.random.fold_in(_rk, 11), (16, 16, 256), jnp.float32)
        _ctx_2048c = jax.random.dirichlet(jax.random.fold_in(_rk, 511), 0.3 * jnp.ones((16,), jnp.float32), (16, 128))
        _ctx_2048t = jnp.einsum('bsk,bkd->bsd', _ctx_2048c, _ctx_2048P)
        _ctx_2048t = _ctx_2048t * jax.lax.rsqrt(jnp.mean(jnp.square(_ctx_2048t)) + 1e-12) * 0.953939
        ctx_2048 = 2.81802e-05 + 1.00001 * (_ctx_2048t + 0.3 * jax.random.normal(jax.random.fold_in(_rk, 611), (16, 128, 256), jnp.float32))
        _validS = jnp.arange(128)[None, :] < _lenS[:, None]
        _validS2 = jnp.arange(128)[None, :] < _lenS2[:, None]
        _causal = jnp.tril(jnp.ones((128, 128), dtype=bool))
        mask_Bx1x2048_bf1 = jnp.ones((16, 1, 256), dtype=bool)
        mask_1x1xSxS2_fc1 = jnp.where(jnp.broadcast_to(_validS2[0:1, None, None, :], (1, 1, 128, 128)), 1.0, 0.0).astype(jnp.float32)
        mask_Bx1xSxS2_ff1 = jnp.where(jnp.ones((16, 1, 128, 128), dtype=bool), 1.0, 0.0).astype(jnp.float32)
        return (x, ctx_2048, mask_Bx1x2048_bf1, mask_1x1xSxS2_fc1, mask_Bx1xSxS2_ff1)
    x, ctx_2048, mask_Bx1x2048_bf1, mask_1x1xSxS2_fc1, mask_Bx1xSxS2_ff1 = _rec_inputs()

    def _L0_xattn_setup():
        import jax, jax.numpy as jnp
        import numpy as np
        B, Q, S1, S2 = (4, 32, 256, 256)
        D, H, K, F = (256, 16, 128, 1024)
        LN_EPS = 1e-05

        def _layer_norm(x, scale, offset):
            mu = jnp.mean(x, axis=-1, keepdims=True)
            var = jnp.var(x, axis=-1, keepdims=True)
            return (x - mu) * jax.lax.rsqrt(var + LN_EPS) * scale + offset

        def _cross_attention(q_in, kv_in, wq, bq, wk, bk, wv, bv, wo, bo, bias_k, bias_v):
            b, q_len, _ = q_in.shape
            t = kv_in.shape[1]
            qh = (q_in @ wq + bq).reshape(b, q_len, H, K)
            kh = (kv_in @ wk + bk).reshape(b, t, H, K)
            vh = (kv_in @ wv + bv).reshape(b, t, H, K)
            kh = jnp.concatenate([kh, jnp.broadcast_to(bias_k, (b, 1, H, K))], axis=1)
            vh = jnp.concatenate([vh, jnp.broadcast_to(bias_v, (b, 1, H, K))], axis=1)
            scale = jnp.sqrt(jnp.asarray(K, q_in.dtype))
            logits = jnp.einsum('bqhk,bthk->bhqt', qh, kh) / scale
            weights = jax.nn.softmax(logits, axis=-1)
            ctx = jnp.einsum('bhqt,bthk->bqhk', weights, vh).reshape(b, q_len, H * K)
            return ctx @ wo + bo

        def _forward(x, xf_1, xf_2, ln1_scale, ln1_offset, wq1, bq1, wk1, bk1, wv1, bv1, wo1, bo1, bias_k1, bias_v1, ln2_scale, ln2_offset, wq2, bq2, wk2, bk2, wv2, bv2, wo2, bo2, bias_k2, bias_v2, ln_mlp_scale, ln_mlp_offset, w_fc1, b_fc1, w_fc2, b_fc2):
            res = x
            h = _layer_norm(x, ln1_scale, ln1_offset)
            x = res + _cross_attention(h, xf_1, wq1, bq1, wk1, bk1, wv1, bv1, wo1, bo1, bias_k1, bias_v1)
            res = x
            h = _layer_norm(x, ln2_scale, ln2_offset)
            x = res + _cross_attention(h, xf_2, wq2, bq2, wk2, bk2, wv2, bv2, wo2, bo2, bias_k2, bias_v2)
            h = _layer_norm(x, ln_mlp_scale, ln_mlp_offset)
            h = jax.nn.gelu(h @ w_fc1 + b_fc1, approximate=False) @ w_fc2 + b_fc2
            return x + h
        key = jax.random.key(seed)
        ks = iter(jax.random.split(key, 64))

        def rn(shape, s=0.02):
            return jax.random.normal(next(ks), shape, jnp.float32) * s
        inp = {'x': rn((B, Q, D), 1.0), 'xf_1': rn((B, S1, D), 1.0), 'xf_2': rn((B, S2, D), 1.0)}
        for i in (1, 2):
            inp[f'ln{i}_scale'] = jnp.ones((D,), jnp.float32)
            inp[f'ln{i}_offset'] = jnp.zeros((D,), jnp.float32)
            inp[f'wq{i}'] = rn((D, H * K))
            inp[f'bq{i}'] = jnp.zeros((H * K,), jnp.float32)
            inp[f'wk{i}'] = rn((D, H * K))
            inp[f'bk{i}'] = jnp.zeros((H * K,), jnp.float32)
            inp[f'wv{i}'] = rn((D, H * K))
            inp[f'bv{i}'] = jnp.zeros((H * K,), jnp.float32)
            inp[f'wo{i}'] = rn((H * K, D))
            inp[f'bo{i}'] = jnp.zeros((D,), jnp.float32)
            inp[f'bias_k{i}'] = rn((1, 1, H, K))
            inp[f'bias_v{i}'] = rn((1, 1, H, K))
        inp['ln_mlp_scale'] = jnp.ones((D,), jnp.float32)
        inp['ln_mlp_offset'] = jnp.zeros((D,), jnp.float32)
        inp['w_fc1'] = rn((D, F))
        inp['b_fc1'] = jnp.zeros((F,), jnp.float32)
        inp['w_fc2'] = rn((F, D))
        inp['b_fc2'] = jnp.zeros((D,), jnp.float32)
        return inp
    _L0_xattn_all = _L0_xattn_setup()
    _L0_xattn_in = {k: v for k, v in _L0_xattn_all.items() if k in ('ln1_scale', 'ln1_offset', 'wq1', 'bq1', 'wk1', 'bk1', 'wv1', 'bv1', 'wo1', 'bo1', 'bias_k1', 'bias_v1', 'ln2_scale', 'ln2_offset', 'wq2', 'bq2', 'wk2', 'bk2', 'wv2', 'bv2', 'wo2', 'bo2', 'bias_k2', 'bias_v2', 'ln_mlp_scale', 'ln_mlp_offset', 'w_fc1', 'b_fc1', 'w_fc2', 'b_fc2')}
    del _L0_xattn_all

    def _L1_xattn_setup():
        import jax, jax.numpy as jnp
        import numpy as np
        import math
        N_HEADS = 16
        EPS = 1e-05

        def _masked_instance_norm(x, mask):
            m = mask.astype(x.dtype)
            x = x * m
            n_valid = jnp.sum(m, axis=-1, keepdims=True)
            mean = jnp.sum(x, axis=-1, keepdims=True) / n_valid
            var = jnp.sum(x * x, axis=-1, keepdims=True) / n_valid - mean * mean
            x = (x - mean) / jnp.sqrt(jax.nn.relu(var) + EPS)
            return x * m
        key = jax.random.key(seed)
        ks = jax.random.split(key, 8)
        bs, c, t1, t2 = (2, 128, 256, 256)
        s = 1.0 / math.sqrt(c)
        return {'x': jax.random.normal(ks[0], (bs, c, t1), jnp.float32), 'mask': jnp.ones((bs, 1, t1), jnp.bool_), 'kv': jax.random.normal(ks[1], (bs, c, t2), jnp.float32), 'kv_mask': jnp.ones((bs, 1, t2), jnp.bool_), 'Wq': jax.random.normal(ks[2], (c, c), jnp.float32) * s, 'bq': jnp.zeros((c,), jnp.float32), 'Wk': jax.random.normal(ks[3], (c, c), jnp.float32) * s, 'bk': jnp.zeros((c,), jnp.float32), 'Wv': jax.random.normal(ks[4], (c, c), jnp.float32) * s, 'bv': jnp.zeros((c,), jnp.float32)}
    _L1_xattn_all = _L1_xattn_setup()
    _L1_xattn_in = {k: v for k, v in _L1_xattn_all.items() if k in ('Wq', 'bq', 'Wk', 'bk', 'Wv', 'bv')}
    del _L1_xattn_all

    def _L2_xattn_setup():
        import jax, jax.numpy as jnp
        import numpy as np
        H = 256
        NH = 16
        HD = H // NH
        EPS = 1e-05

        def gelu(x):
            return 0.5 * x * (1.0 + jnp.tanh(0.7978845608028654 * x * (1.0 + 0.044715 * x * x)))

        def layernorm(x, scale, bias):
            m = jnp.mean(x, axis=-1, keepdims=True)
            v = jnp.mean(jnp.square(x - m), axis=-1, keepdims=True)
            return (x - m) * jax.lax.rsqrt(v + EPS) * scale + bias

        def split_heads(x):
            b, s, _ = x.shape
            return x.reshape(b, s, NH, HD).transpose(0, 2, 1, 3)

        def merge_heads(x):
            b, nh, s, hd = x.shape
            return x.transpose(0, 2, 1, 3).reshape(b, s, nh * hd)

        def attention(q, k, v, mask):
            scores = jnp.einsum('bhqd,bhkd->bhqk', q, k) / jnp.sqrt(jnp.float32(HD))
            scores = scores * mask - 10000.0 * (1.0 - mask)
            probs = jax.nn.softmax(scores, axis=-1)
            return jnp.einsum('bhqk,bhkd->bhqd', probs, v)
        key = jax.random.key(seed)
        ks = jax.random.split(key, 16)
        b, s, t = (2, 128, 128)
        w = lambda k, i, o: jax.random.normal(k, (i, o), jnp.float32) * 0.02
        inp = {'hidden_states': jax.random.normal(ks[0], (b, s, H), jnp.float32), 'encoder_states': jax.random.normal(ks[1], (b, t, H), jnp.float32), 'ltor_mask': jnp.tril(jnp.ones((1, 1, s, s), jnp.float32)), 'cross_mask': jnp.ones((b, 1, s, t), jnp.float32), 'ln1_s': jnp.ones((H,), jnp.float32), 'ln1_b': jnp.zeros((H,), jnp.float32), 'w_qkv': w(ks[2], H, 3 * H), 'b_qkv': jnp.zeros((3 * H,), jnp.float32), 'w_ao': w(ks[3], H, H), 'b_ao': jnp.zeros((H,), jnp.float32), 'ln2_s': jnp.ones((H,), jnp.float32), 'ln2_b': jnp.zeros((H,), jnp.float32), 'w_q': w(ks[4], H, H), 'b_q': jnp.zeros((H,), jnp.float32), 'w_kv': w(ks[5], H, 2 * H), 'b_kv': jnp.zeros((2 * H,), jnp.float32), 'w_co': w(ks[6], H, H), 'b_co': jnp.zeros((H,), jnp.float32), 'ln3_s': jnp.ones((H,), jnp.float32), 'ln3_b': jnp.zeros((H,), jnp.float32), 'w1': w(ks[7], H, 4 * H), 'b1': jnp.zeros((4 * H,), jnp.float32), 'w2': w(ks[8], 4 * H, H), 'b2': jnp.zeros((H,), jnp.float32)}
        return inp
    _L2_xattn_all = _L2_xattn_setup()
    _L2_xattn_in = {k: v for k, v in _L2_xattn_all.items() if k in ('ln1_s', 'ln1_b', 'w_qkv', 'b_qkv', 'w_ao', 'b_ao', 'ln2_s', 'ln2_b', 'w_q', 'b_q', 'w_kv', 'b_kv', 'w_co', 'b_co', 'ln3_s', 'ln3_b', 'w1', 'b1', 'w2', 'b2')}
    del _L2_xattn_all

    def _L3_xattn_setup():
        import math
        import jax, jax.numpy as jnp
        import numpy as np
        C = 128
        H = 16
        DH = C // H
        EPS = 1e-05

        def pos_enc(c, T, dtype):
            pos = jnp.arange(T, dtype=jnp.float32)[:, None]
            div = jnp.exp(jnp.arange(0, c, 2, dtype=jnp.float32) * (-math.log(10000.0) / c))
            ang = pos * div
            pe = jnp.zeros((T, c), dtype=jnp.float32)
            pe = pe.at[:, 0::2].set(jnp.sin(ang)).at[:, 1::2].set(jnp.cos(ang))
            return pe.T.astype(dtype)

        def layer_norm(x, g, b):
            mu = jnp.mean(x, axis=-1, keepdims=True)
            var = jnp.mean(jnp.square(x - mu), axis=-1, keepdims=True)
            return (x - mu) * jax.lax.rsqrt(var + EPS) * g + b
        key = jax.random.key(seed)
        ks = jax.random.split(key, 16)
        s = 1.0 / math.sqrt(C)
        inp = {'zt_prev': jax.random.normal(ks[0], (2, C, 256), jnp.float32), 'za': jax.random.normal(ks[1], (2, C, 256), jnp.float32), 'Wq': jax.random.normal(ks[2], (C, C), jnp.float32) * s, 'Wk': jax.random.normal(ks[3], (C, C), jnp.float32) * s, 'Wv': jax.random.normal(ks[4], (C, C), jnp.float32) * s, 'Wo': jax.random.normal(ks[5], (C, C), jnp.float32) * s, 'ln_q_g': jnp.ones((C,), jnp.float32), 'ln_q_b': jnp.zeros((C,), jnp.float32), 'ln_kv_g': jnp.ones((C,), jnp.float32), 'ln_kv_b': jnp.zeros((C,), jnp.float32), 'ffn_ln_g': jnp.ones((C,), jnp.float32), 'ffn_ln_b': jnp.zeros((C,), jnp.float32), 'W1': jax.random.normal(ks[6], (C, 2 * C), jnp.float32) * s, 'b1': jnp.zeros((2 * C,), jnp.float32), 'W2': jax.random.normal(ks[7], (2 * C, C), jnp.float32) * (1.0 / math.sqrt(2 * C)), 'b2': jnp.zeros((C,), jnp.float32)}
        return inp
    _L3_xattn_all = _L3_xattn_setup()
    _L3_xattn_in = {k: v for k, v in _L3_xattn_all.items() if k in ('Wq', 'Wk', 'Wv', 'Wo', 'ln_q_g', 'ln_q_b', 'ln_kv_g', 'ln_kv_b', 'ffn_ln_g', 'ffn_ln_b', 'W1', 'b1', 'W2', 'b2')}
    del _L3_xattn_all
    return {'x': x, 'ctx_2048': ctx_2048, 'mask_Bx1x2048_bf1': mask_Bx1x2048_bf1, 'mask_1x1xSxS2_fc1': mask_1x1xSxS2_fc1, 'mask_Bx1xSxS2_ff1': mask_Bx1xSxS2_ff1, 'L0_xattn_ln1_scale': _L0_xattn_in['ln1_scale'], 'L0_xattn_ln1_offset': _L0_xattn_in['ln1_offset'], 'L0_xattn_wq1': _L0_xattn_in['wq1'], 'L0_xattn_bq1': _L0_xattn_in['bq1'], 'L0_xattn_wk1': _L0_xattn_in['wk1'], 'L0_xattn_bk1': _L0_xattn_in['bk1'], 'L0_xattn_wv1': _L0_xattn_in['wv1'], 'L0_xattn_bv1': _L0_xattn_in['bv1'], 'L0_xattn_wo1': _L0_xattn_in['wo1'], 'L0_xattn_bo1': _L0_xattn_in['bo1'], 'L0_xattn_bias_k1': _L0_xattn_in['bias_k1'], 'L0_xattn_bias_v1': _L0_xattn_in['bias_v1'], 'L0_xattn_ln2_scale': _L0_xattn_in['ln2_scale'], 'L0_xattn_ln2_offset': _L0_xattn_in['ln2_offset'], 'L0_xattn_wq2': _L0_xattn_in['wq2'], 'L0_xattn_bq2': _L0_xattn_in['bq2'], 'L0_xattn_wk2': _L0_xattn_in['wk2'], 'L0_xattn_bk2': _L0_xattn_in['bk2'], 'L0_xattn_wv2': _L0_xattn_in['wv2'], 'L0_xattn_bv2': _L0_xattn_in['bv2'], 'L0_xattn_wo2': _L0_xattn_in['wo2'], 'L0_xattn_bo2': _L0_xattn_in['bo2'], 'L0_xattn_bias_k2': _L0_xattn_in['bias_k2'], 'L0_xattn_bias_v2': _L0_xattn_in['bias_v2'], 'L0_xattn_ln_mlp_scale': _L0_xattn_in['ln_mlp_scale'], 'L0_xattn_ln_mlp_offset': _L0_xattn_in['ln_mlp_offset'], 'L0_xattn_w_fc1': _L0_xattn_in['w_fc1'], 'L0_xattn_b_fc1': _L0_xattn_in['b_fc1'], 'L0_xattn_w_fc2': _L0_xattn_in['w_fc2'], 'L0_xattn_b_fc2': _L0_xattn_in['b_fc2'], 'L1_xattn_Wq': _L1_xattn_in['Wq'], 'L1_xattn_bq': _L1_xattn_in['bq'], 'L1_xattn_Wk': _L1_xattn_in['Wk'], 'L1_xattn_bk': _L1_xattn_in['bk'], 'L1_xattn_Wv': _L1_xattn_in['Wv'], 'L1_xattn_bv': _L1_xattn_in['bv'], 'L2_xattn_ln1_s': _L2_xattn_in['ln1_s'], 'L2_xattn_ln1_b': _L2_xattn_in['ln1_b'], 'L2_xattn_w_qkv': _L2_xattn_in['w_qkv'], 'L2_xattn_b_qkv': _L2_xattn_in['b_qkv'], 'L2_xattn_w_ao': _L2_xattn_in['w_ao'], 'L2_xattn_b_ao': _L2_xattn_in['b_ao'], 'L2_xattn_ln2_s': _L2_xattn_in['ln2_s'], 'L2_xattn_ln2_b': _L2_xattn_in['ln2_b'], 'L2_xattn_w_q': _L2_xattn_in['w_q'], 'L2_xattn_b_q': _L2_xattn_in['b_q'], 'L2_xattn_w_kv': _L2_xattn_in['w_kv'], 'L2_xattn_b_kv': _L2_xattn_in['b_kv'], 'L2_xattn_w_co': _L2_xattn_in['w_co'], 'L2_xattn_b_co': _L2_xattn_in['b_co'], 'L2_xattn_ln3_s': _L2_xattn_in['ln3_s'], 'L2_xattn_ln3_b': _L2_xattn_in['ln3_b'], 'L2_xattn_w1': _L2_xattn_in['w1'], 'L2_xattn_b1': _L2_xattn_in['b1'], 'L2_xattn_w2': _L2_xattn_in['w2'], 'L2_xattn_b2': _L2_xattn_in['b2'], 'L3_xattn_Wq': _L3_xattn_in['Wq'], 'L3_xattn_Wk': _L3_xattn_in['Wk'], 'L3_xattn_Wv': _L3_xattn_in['Wv'], 'L3_xattn_Wo': _L3_xattn_in['Wo'], 'L3_xattn_ln_q_g': _L3_xattn_in['ln_q_g'], 'L3_xattn_ln_q_b': _L3_xattn_in['ln_q_b'], 'L3_xattn_ln_kv_g': _L3_xattn_in['ln_kv_g'], 'L3_xattn_ln_kv_b': _L3_xattn_in['ln_kv_b'], 'L3_xattn_ffn_ln_g': _L3_xattn_in['ffn_ln_g'], 'L3_xattn_ffn_ln_b': _L3_xattn_in['ffn_ln_b'], 'L3_xattn_W1': _L3_xattn_in['W1'], 'L3_xattn_b1': _L3_xattn_in['b1'], 'L3_xattn_W2': _L3_xattn_in['W2'], 'L3_xattn_b2': _L3_xattn_in['b2']}

def reference(x, ctx_2048, mask_Bx1x2048_bf1, mask_1x1xSxS2_fc1, mask_Bx1xSxS2_ff1, L0_xattn_ln1_scale, L0_xattn_ln1_offset, L0_xattn_wq1, L0_xattn_bq1, L0_xattn_wk1, L0_xattn_bk1, L0_xattn_wv1, L0_xattn_bv1, L0_xattn_wo1, L0_xattn_bo1, L0_xattn_bias_k1, L0_xattn_bias_v1, L0_xattn_ln2_scale, L0_xattn_ln2_offset, L0_xattn_wq2, L0_xattn_bq2, L0_xattn_wk2, L0_xattn_bk2, L0_xattn_wv2, L0_xattn_bv2, L0_xattn_wo2, L0_xattn_bo2, L0_xattn_bias_k2, L0_xattn_bias_v2, L0_xattn_ln_mlp_scale, L0_xattn_ln_mlp_offset, L0_xattn_w_fc1, L0_xattn_b_fc1, L0_xattn_w_fc2, L0_xattn_b_fc2, L1_xattn_Wq, L1_xattn_bq, L1_xattn_Wk, L1_xattn_bk, L1_xattn_Wv, L1_xattn_bv, L2_xattn_ln1_s, L2_xattn_ln1_b, L2_xattn_w_qkv, L2_xattn_b_qkv, L2_xattn_w_ao, L2_xattn_b_ao, L2_xattn_ln2_s, L2_xattn_ln2_b, L2_xattn_w_q, L2_xattn_b_q, L2_xattn_w_kv, L2_xattn_b_kv, L2_xattn_w_co, L2_xattn_b_co, L2_xattn_ln3_s, L2_xattn_ln3_b, L2_xattn_w1, L2_xattn_b1, L2_xattn_w2, L2_xattn_b2, L3_xattn_Wq, L3_xattn_Wk, L3_xattn_Wv, L3_xattn_Wo, L3_xattn_ln_q_g, L3_xattn_ln_q_b, L3_xattn_ln_kv_g, L3_xattn_ln_kv_b, L3_xattn_ffn_ln_g, L3_xattn_ffn_ln_b, L3_xattn_W1, L3_xattn_b1, L3_xattn_W2, L3_xattn_b2):
    import jax
    import jax.numpy as jnp

    def _L0_xattn_ref(x, xf_1, xf_2, ln1_scale, ln1_offset, wq1, bq1, wk1, bk1, wv1, bv1, wo1, bo1, bias_k1, bias_v1, ln2_scale, ln2_offset, wq2, bq2, wk2, bk2, wv2, bv2, wo2, bo2, bias_k2, bias_v2, ln_mlp_scale, ln_mlp_offset, w_fc1, b_fc1, w_fc2, b_fc2):
        import jax, jax.numpy as jnp
        import numpy as np
        B, Q, S1, S2 = (4, 32, 256, 256)
        D, H, K, F = (256, 16, 128, 1024)
        LN_EPS = 1e-05

        def _layer_norm(x, scale, offset):
            mu = jnp.mean(x, axis=-1, keepdims=True)
            var = jnp.var(x, axis=-1, keepdims=True)
            return (x - mu) * jax.lax.rsqrt(var + LN_EPS) * scale + offset

        def _cross_attention(q_in, kv_in, wq, bq, wk, bk, wv, bv, wo, bo, bias_k, bias_v):
            b, q_len, _ = q_in.shape
            t = kv_in.shape[1]
            qh = (q_in @ wq + bq).reshape(b, q_len, H, K)
            kh = (kv_in @ wk + bk).reshape(b, t, H, K)
            vh = (kv_in @ wv + bv).reshape(b, t, H, K)
            kh = jnp.concatenate([kh, jnp.broadcast_to(bias_k, (b, 1, H, K))], axis=1)
            vh = jnp.concatenate([vh, jnp.broadcast_to(bias_v, (b, 1, H, K))], axis=1)
            scale = jnp.sqrt(jnp.asarray(K, q_in.dtype))
            logits = jnp.einsum('bqhk,bthk->bhqt', qh, kh) / scale
            weights = jax.nn.softmax(logits, axis=-1)
            ctx = jnp.einsum('bhqt,bthk->bqhk', weights, vh).reshape(b, q_len, H * K)
            return ctx @ wo + bo

        def _forward(x, xf_1, xf_2, ln1_scale, ln1_offset, wq1, bq1, wk1, bk1, wv1, bv1, wo1, bo1, bias_k1, bias_v1, ln2_scale, ln2_offset, wq2, bq2, wk2, bk2, wv2, bv2, wo2, bo2, bias_k2, bias_v2, ln_mlp_scale, ln_mlp_offset, w_fc1, b_fc1, w_fc2, b_fc2):
            res = x
            h = _layer_norm(x, ln1_scale, ln1_offset)
            x = res + _cross_attention(h, xf_1, wq1, bq1, wk1, bk1, wv1, bv1, wo1, bo1, bias_k1, bias_v1)
            res = x
            h = _layer_norm(x, ln2_scale, ln2_offset)
            x = res + _cross_attention(h, xf_2, wq2, bq2, wk2, bk2, wv2, bv2, wo2, bo2, bias_k2, bias_v2)
            h = _layer_norm(x, ln_mlp_scale, ln_mlp_offset)
            h = jax.nn.gelu(h @ w_fc1 + b_fc1, approximate=False) @ w_fc2 + b_fc2
            return x + h
        return _forward(x, xf_1, xf_2, ln1_scale, ln1_offset, wq1, bq1, wk1, bk1, wv1, bv1, wo1, bo1, bias_k1, bias_v1, ln2_scale, ln2_offset, wq2, bq2, wk2, bk2, wv2, bv2, wo2, bo2, bias_k2, bias_v2, ln_mlp_scale, ln_mlp_offset, w_fc1, b_fc1, w_fc2, b_fc2)

    def _L1_xattn_ref(x, mask, kv, kv_mask, Wq, bq, Wk, bk, Wv, bv):
        import jax, jax.numpy as jnp
        import numpy as np
        import math
        N_HEADS = 16
        EPS = 1e-05

        def _masked_instance_norm(x, mask):
            m = mask.astype(x.dtype)
            x = x * m
            n_valid = jnp.sum(m, axis=-1, keepdims=True)
            mean = jnp.sum(x, axis=-1, keepdims=True) / n_valid
            var = jnp.sum(x * x, axis=-1, keepdims=True) / n_valid - mean * mean
            x = (x - mean) / jnp.sqrt(jax.nn.relu(var) + EPS)
            return x * m
        bs, c, t1 = x.shape
        h = N_HEADS
        d = c // h
        scale = 1.0 / math.sqrt(d)
        q = jnp.einsum('oc,bct->bot', Wq, x) + bq[None, :, None]
        k = jnp.einsum('oc,bct->bot', Wk, kv) + bk[None, :, None]
        v = jnp.einsum('oc,bct->bot', Wv, kv) + bv[None, :, None]
        q = q.reshape(bs, h, d, t1).transpose(0, 1, 3, 2)
        k = k.reshape(bs, h, d, -1)
        v = v.reshape(bs, h, d, -1).transpose(0, 1, 3, 2)
        attn = jnp.einsum('bhqd,bhdk->bhqk', q * scale, k)
        attn = jnp.where(kv_mask[:, :, None, :], attn, -jnp.inf)
        attn = jax.nn.softmax(attn, axis=-1)
        mean = jnp.einsum('bhqk,bhkd->bhqd', attn, v)
        ex2 = jnp.einsum('bhqk,bhkd->bhqd', attn, v * v)
        std = jnp.sqrt(jax.nn.relu(ex2 - mean * mean))
        mean = mean.transpose(0, 1, 3, 2).reshape(bs, c, t1)
        std = std.transpose(0, 1, 3, 2).reshape(bs, c, t1)
        xn = _masked_instance_norm(x, mask)
        out = (xn * std + mean) * mask.astype(x.dtype)
        return out

    def _L2_xattn_ref(hidden_states, encoder_states, ltor_mask, cross_mask, ln1_s, ln1_b, w_qkv, b_qkv, w_ao, b_ao, ln2_s, ln2_b, w_q, b_q, w_kv, b_kv, w_co, b_co, ln3_s, ln3_b, w1, b1, w2, b2):
        import jax, jax.numpy as jnp
        import numpy as np
        H = 256
        NH = 16
        HD = H // NH
        EPS = 1e-05

        def gelu(x):
            return 0.5 * x * (1.0 + jnp.tanh(0.7978845608028654 * x * (1.0 + 0.044715 * x * x)))

        def layernorm(x, scale, bias):
            m = jnp.mean(x, axis=-1, keepdims=True)
            v = jnp.mean(jnp.square(x - m), axis=-1, keepdims=True)
            return (x - m) * jax.lax.rsqrt(v + EPS) * scale + bias

        def split_heads(x):
            b, s, _ = x.shape
            return x.reshape(b, s, NH, HD).transpose(0, 2, 1, 3)

        def merge_heads(x):
            b, nh, s, hd = x.shape
            return x.transpose(0, 2, 1, 3).reshape(b, s, nh * hd)

        def attention(q, k, v, mask):
            scores = jnp.einsum('bhqd,bhkd->bhqk', q, k) / jnp.sqrt(jnp.float32(HD))
            scores = scores * mask - 10000.0 * (1.0 - mask)
            probs = jax.nn.softmax(scores, axis=-1)
            return jnp.einsum('bhqk,bhkd->bhqd', probs, v)
        ln_out = layernorm(hidden_states, ln1_s, ln1_b)
        qkv = ln_out @ w_qkv + b_qkv
        q, k, v = jnp.split(qkv, 3, axis=-1)
        ctx = merge_heads(attention(split_heads(q), split_heads(k), split_heads(v), ltor_mask))
        attn_out = ctx @ w_ao + b_ao
        x = hidden_states + attn_out
        ln_out = layernorm(x, ln2_s, ln2_b)
        q = ln_out @ w_q + b_q
        kv = encoder_states @ w_kv + b_kv
        k, v = jnp.split(kv, 2, axis=-1)
        ctx = merge_heads(attention(split_heads(q), split_heads(k), split_heads(v), cross_mask))
        cross_out = ctx @ w_co + b_co
        x = x + cross_out
        ln_out = layernorm(x, ln3_s, ln3_b)
        mlp_out = gelu(ln_out @ w1 + b1) @ w2 + b2
        return x + mlp_out

    def _L3_xattn_ref(zt_prev, za, Wq, Wk, Wv, Wo, ln_q_g, ln_q_b, ln_kv_g, ln_kv_b, ffn_ln_g, ffn_ln_b, W1, b1, W2, b2):
        import math
        import jax, jax.numpy as jnp
        import numpy as np
        C = 128
        H = 16
        DH = C // H
        EPS = 1e-05

        def pos_enc(c, T, dtype):
            pos = jnp.arange(T, dtype=jnp.float32)[:, None]
            div = jnp.exp(jnp.arange(0, c, 2, dtype=jnp.float32) * (-math.log(10000.0) / c))
            ang = pos * div
            pe = jnp.zeros((T, c), dtype=jnp.float32)
            pe = pe.at[:, 0::2].set(jnp.sin(ang)).at[:, 1::2].set(jnp.cos(ang))
            return pe.T.astype(dtype)

        def layer_norm(x, g, b):
            mu = jnp.mean(x, axis=-1, keepdims=True)
            var = jnp.mean(jnp.square(x - mu), axis=-1, keepdims=True)
            return (x - mu) * jax.lax.rsqrt(var + EPS) * g + b
        B, _, Tq = zt_prev.shape
        Tk = za.shape[-1]
        q = jnp.transpose(zt_prev + pos_enc(C, Tq, zt_prev.dtype)[None], (0, 2, 1))
        kv = jnp.transpose(za + pos_enc(C, Tk, za.dtype)[None], (0, 2, 1))
        q = layer_norm(q, ln_q_g, ln_q_b)
        kv = layer_norm(kv, ln_kv_g, ln_kv_b)

        def split(x):
            Bt, T, _ = x.shape
            return jnp.transpose(x.reshape(Bt, T, H, DH), (0, 2, 1, 3))
        Q = split(q @ Wq)
        K = split(kv @ Wk)
        V = split(kv @ Wv)
        attn = jnp.einsum('bhqd,bhkd->bhqk', Q, K) / math.sqrt(DH)
        ctx = jnp.einsum('bhqk,bhkd->bhqd', jax.nn.softmax(attn, axis=-1), V)
        ctx = jnp.transpose(ctx, (0, 2, 1, 3)).reshape(B, Tq, C)
        y = ctx @ Wo
        r = y + q
        h = layer_norm(r, ffn_ln_g, ffn_ln_b)
        h = jax.nn.gelu(h @ W1 + b1, approximate=False) @ W2 + b2
        out = h + r
        return jnp.transpose(out, (0, 2, 1))
    x = _L0_xattn_ref(x, ctx_2048, ctx_2048, L0_xattn_ln1_scale, L0_xattn_ln1_offset, L0_xattn_wq1, L0_xattn_bq1, L0_xattn_wk1, L0_xattn_bk1, L0_xattn_wv1, L0_xattn_bv1, L0_xattn_wo1, L0_xattn_bo1, L0_xattn_bias_k1, L0_xattn_bias_v1, L0_xattn_ln2_scale, L0_xattn_ln2_offset, L0_xattn_wq2, L0_xattn_bq2, L0_xattn_wk2, L0_xattn_bk2, L0_xattn_wv2, L0_xattn_bv2, L0_xattn_wo2, L0_xattn_bo2, L0_xattn_bias_k2, L0_xattn_bias_v2, L0_xattn_ln_mlp_scale, L0_xattn_ln_mlp_offset, L0_xattn_w_fc1, L0_xattn_b_fc1, L0_xattn_w_fc2, L0_xattn_b_fc2)
    x = _L1_xattn_ref(x, mask_Bx1x2048_bf1, ctx_2048, mask_Bx1x2048_bf1, L1_xattn_Wq, L1_xattn_bq, L1_xattn_Wk, L1_xattn_bk, L1_xattn_Wv, L1_xattn_bv)
    x = _L2_xattn_ref(x, ctx_2048, mask_1x1xSxS2_fc1, mask_Bx1xSxS2_ff1, L2_xattn_ln1_s, L2_xattn_ln1_b, L2_xattn_w_qkv, L2_xattn_b_qkv, L2_xattn_w_ao, L2_xattn_b_ao, L2_xattn_ln2_s, L2_xattn_ln2_b, L2_xattn_w_q, L2_xattn_b_q, L2_xattn_w_kv, L2_xattn_b_kv, L2_xattn_w_co, L2_xattn_b_co, L2_xattn_ln3_s, L2_xattn_ln3_b, L2_xattn_w1, L2_xattn_b1, L2_xattn_w2, L2_xattn_b2)
    x = _L3_xattn_ref(x, ctx_2048, L3_xattn_Wq, L3_xattn_Wk, L3_xattn_Wv, L3_xattn_Wo, L3_xattn_ln_q_g, L3_xattn_ln_q_b, L3_xattn_ln_kv_g, L3_xattn_ln_kv_b, L3_xattn_ffn_ln_g, L3_xattn_ffn_ln_b, L3_xattn_W1, L3_xattn_b1, L3_xattn_W2, L3_xattn_b2)
    return x

_drawn_inputs = setup_inputs


def setup_inputs(seed=0):
    import zlib

    import numpy as np

    out = dict(_drawn_inputs(seed))
    spreads = {'L0_xattn_ln1_scale': (1.0, 0.6),
     'L0_xattn_ln1_offset': (0.0, 0.8),
     'L0_xattn_bq1': (0.0, 0.8),
     'L0_xattn_bk1': (0.0, 2.0),
     'L0_xattn_bv1': (0.0, 0.272),
     'L0_xattn_bo1': (0.0, 0.275),
     'L0_xattn_ln2_scale': (1.0, 0.6),
     'L0_xattn_ln2_offset': (0.0, 0.8),
     'L0_xattn_bq2': (0.0, 0.8),
     'L0_xattn_bk2': (0.0, 2.0),
     'L0_xattn_bv2': (0.0, 0.289),
     'L0_xattn_bo2': (0.0, 0.1),
     'L0_xattn_ln_mlp_scale': (1.0, 0.6),
     'L0_xattn_ln_mlp_offset': (0.0, 0.8),
     'L0_xattn_b_fc1': (0.0, 0.512),
     'L0_xattn_b_fc2': (0.0, 0.1),
     'L1_xattn_bq': (0.0, 0.267),
     'L1_xattn_bk': (0.0, 2.0),
     'L1_xattn_bv': (0.0, 0.1),
     'L2_xattn_ln1_s': (1.0, 0.6),
     'L2_xattn_ln1_b': (0.0, 2.0),
     'L2_xattn_b_qkv': (0.0, 2.0),
     'L2_xattn_b_ao': (0.0, 2.0),
     'L2_xattn_ln2_s': (1.0, 0.6),
     'L2_xattn_ln2_b': (0.0, 2.0),
     'L2_xattn_b_q': (0.0, 2.0),
     'L2_xattn_b_kv': (0.0, 2.0),
     'L2_xattn_b_co': (0.0, 2.0),
     'L2_xattn_ln3_s': (1.0, 0.6),
     'L2_xattn_ln3_b': (0.0, 2.0),
     'L2_xattn_b1': (0.0, 2.0),
     'L2_xattn_b2': (0.0, 2.0),
     'L3_xattn_ln_q_g': (1.0, 0.2),
     'L3_xattn_ln_q_b': (0.0, 0.1),
     'L3_xattn_ln_kv_g': (1.0, 0.2),
     'L3_xattn_ln_kv_b': (0.0, 0.1),
     'L3_xattn_ffn_ln_g': (1.0, 0.2),
     'L3_xattn_ffn_ln_b': (0.0, 0.1),
     'L3_xattn_b1': (0.0, 0.1),
     'L3_xattn_b2': (0.0, 0.1)}
    factors = {'L0_xattn_wq1': 8.0,
     'L0_xattn_wk1': 8.0,
     'L0_xattn_bias_k1': 64.0,
     'L0_xattn_bias_v1': 64.0,
     'L0_xattn_wq2': 8.0,
     'L0_xattn_wk2': 8.0,
     'L0_xattn_bias_k2': 64.0,
     'L0_xattn_bias_v2': 64.0,
     'L2_xattn_w_q': 200.0}
    for name, (base, spread) in spreads.items():
        noise = np.random.default_rng([zlib.crc32(name.encode()), seed]).standard_normal(out[name].shape)
        drawn = base * np.exp(spread * noise) if base else spread * noise
        out[name] = jnp.asarray(drawn.astype(out[name].dtype))
    for name, factor in factors.items():
        out[name] = (out[name] * factor).astype(out[name].dtype)
    return out
```

```python
from contextlib import ExitStack

import numpy as np

import concourse.bass as bass
from concourse import mybir
from concourse.alu_op_type import AluOpType as ALU

F32 = mybir.dt.float32
F32R = mybir.dt.float32r
I32 = mybir.dt.int32
U8 = mybir.dt.uint8
ACT = mybir.ActivationFunctionType
X_AXIS = mybir.AxisListType.X

P = 128
B = 16
D = 256
DC = D // P
EPS = 1e-5
BANK = 512

H0 = 16
PAIRS = H0 // 2
GROUP = 4
GROUPS = B // GROUP
TOK = GROUP * P
KEYS0 = P + 1
F0 = 1024
SCALE0 = 1.0 / float(np.sqrt(np.float32(P)))
ADD_CREDIT = 9
PAIR_LOADS = 10

SLOTS = 2
ROUNDS = B // SLOTS
HN = 16
NEG_BIG = 10000.0
SCALE1 = float(np.float32(1.0 / np.sqrt(8.0)))
SCALE2 = 0.25


ds = bass.ds


class Statistics:

    def __init__(self, sums, mean_var, rstd, shifted, work):
        self.sums, self.mean_var, self.rstd, self.shifted, self.work = sums, mean_var, rstd, shifted, work


class FeedForward:

    def __init__(self, sem):
        self.chain = sem("ff_chain")
        self.rows_normed = sem("ff_rows_normed")
        self.turned = sem("ff_turned")
        self.in_ready = sem("ff_in_ready")
        self.up_ready = sem("ff_up_ready")
        self.hidden_ready = sem("ff_hidden_ready")
        self.down_ready = sem("ff_down_ready")
        self.x_added = sem("ff_x_added")


class FeedForward3:

    def __init__(self, sem):
        self.chain = sem("ff3_chain")
        self.x_copied = sem("ff3_x_copied")
        self.turned = sem("ff3_turned")
        self.rows_normed = sem("ff3_rows_normed")
        self.turned_back = sem("ff3_turned_back")
        self.in_ready = sem("ff3_in_ready")
        self.up_ready = sem("ff3_up_ready")
        self.hidden_ready = sem("ff3_hidden_ready")
        self.down_ready = sem("ff3_down_ready")


class Narrow:

    def __init__(self, sem, name, loads, around):
        self.chain = sem(f"{name}_chain")
        self.projected = sem(f"{name}_projected")
        self.values = sem(f"{name}_values")
        self.q_ready = sem(f"{name}_q_ready")
        self.k_ready = sem(f"{name}_k_ready")
        self.spread = sem(f"{name}_spread")
        self.v_ready = sem(f"{name}_v_ready")
        self.scores = sem(f"{name}_scores")
        self.max_ready = sem(f"{name}_max_ready")
        self.exp_ready = sem(f"{name}_exp_ready")
        self.probs_turned = sem(f"{name}_probs_turned")
        self.probs_copied = sem(f"{name}_probs_copied")
        self.heads = sem(f"{name}_heads")
        self.heads_taken = sem(f"{name}_heads_taken")
        self.result = sem(f"{name}_result")
        self.x_added = sem(f"{name}_x_added")
        if loads:
            self.loaded0 = sem(f"{name}_loaded0")
            self.loaded1 = sem(f"{name}_loaded1")
        if around:
            self.setup = sem(f"{name}_setup")
            self.rows_normed = sem(f"{name}_rows_normed")
            self.turned = sem(f"{name}_turned")
            self.in_ready = sem(f"{name}_in_ready")
            self.heads_turned = sem(f"{name}_heads_turned")
            self.heads_copied = sem(f"{name}_heads_copied")


class Attention:

    def __init__(self, sems, units, heads, keys, width, mask):
        self.s, self.units, self.heads, self.keys, self.width, self.mask = sems, units, heads, keys, width, mask
        self.blocks = keys // P
        self.steps = HN // heads
        self.per_slot = units * self.steps
        self.per_round = SLOTS * self.per_slot
        self.all_units = SLOTS * units


class Chain:

    def __init__(self, engine, sem, base=0):
        self.engine, self.sem, self.base, self.steps = engine, sem, base, 0

    def mark(self, instruction):
        self.steps += 1
        instruction.then_inc(self.sem, 1)

    def join(self):
        self.engine.wait_ge(self.sem, self.base + self.steps)

    def link(self, instruction):
        self.mark(instruction)
        self.join()


def inverse_root(dve, chain, out, var, shifted, work):
    chain.link(dve.tensor_scalar(shifted, var, EPS, None, ALU.add))
    chain.link(dve.tensor_scalar(out.bitcast(I32), shifted.bitcast(I32), -0.5, 1597463007.0,
                                 ALU.mult, ALU.add))
    for _ in range(3):
        chain.link(dve.scalar_tensor_tensor(work, out, -0.5, out, ALU.mult, ALU.mult))
        chain.link(dve.tensor_tensor(work, work, shifted, ALU.mult))
        chain.link(dve.scalar_tensor_tensor(out, work, 1.5, out, ALU.add, ALU.mult))


def row_statistics(dve, chain, rows, stats, idle):
    n = len(rows)
    for k, row in enumerate(rows):
        chain.mark(dve.bn_stats(stats.sums[:, k, :], row))
    chain.join()
    dve.sem_inc(idle, 1)
    for k in range(n):
        chain.mark(dve.bn_aggr(stats.mean_var[:, k, :], stats.sums[:, k, :]))
    chain.join()
    inverse_root(dve, chain, stats.rstd[:, 0:n], stats.mean_var[:, 0:n, 1], stats.shifted[:, 0:n],
                 stats.work[:, 0:n])


def statistics_steps(n):
    return 2 * n + 11


def build(nc, t, out):
    with ExitStack() as outer:
        program(nc, t, out, outer)


def program(nc, t, out, outer):
    def sem(name):
        return outer.enter_context(nc.semaphore(name))

    def sbuf(scope, name, shape, dtype=F32):
        return scope.enter_context(nc.sbuf_tensor(name, shape, dtype))

    bank = [outer.enter_context(nc.psum_tensor(f"bank{k}", [P, BANK], F32)) for k in range(8)]

    x = sbuf(outer, "x", [P, B, D])
    zero = sbuf(outer, "zero", [P, 1])
    ident = sbuf(outer, "ident", [P, P])
    norm_rows = sbuf(outer, "norm_rows", [P, SLOTS, D])
    stats = Statistics(
        sums=sbuf(outer, "stat_sums", [P, 4, 6]), mean_var=sbuf(outer, "mean_var", [P, 4, 2]),
        rstd=sbuf(outer, "rstd", [P, 4]), shifted=sbuf(outer, "stat_shifted", [P, 4]),
        work=sbuf(outer, "stat_work", [P, 4]))
    norms = ["L0_xattn_ln1", "L0_xattn_ln2", "L0_xattn_ln_mlp", "L2_xattn_ln1", "L2_xattn_ln2", "L2_xattn_ln3"]
    norm_scale = sbuf(outer, "norm_scale", [P, len(norms), DC])
    norm_offset = sbuf(outer, "norm_offset", [P, len(norms), DC])
    row_biases = ["L0_xattn_bo1", "L0_xattn_bo2", "L0_xattn_b_fc2", "L2_xattn_b_ao", "L2_xattn_b_co", "L2_xattn_b2"]
    row_bias = sbuf(outer, "row_bias", [P, len(row_biases), D])
    w_up = sbuf(outer, "w_up", [P, DC, F0])
    w_down = sbuf(outer, "w_down", [P, F0 // P, D])
    b_up = sbuf(outer, "b_up", [P, 2, F0 // P])
    hidden_in = sbuf(outer, "hidden_in", [P, DC, SLOTS * P])
    hidden = sbuf(outer, "hidden", [P, F0 // P, SLOTS * P])

    with ExitStack() as scope0:
        normed_high = sbuf(scope0, "wide_normed_high", [P, DC, B * P], F32R)
        normed_low = sbuf(scope0, "wide_normed_low", [P, DC, B * P], F32R)
        ctx_high = sbuf(scope0, "wide_ctx_high", [P, DC, B * P], F32R)
        ctx_low = sbuf(scope0, "wide_ctx_low", [P, DC, B * P], F32R)
        ctx_rows = sbuf(scope0, "wide_ctx_rows", [P, 2, GROUP, D])
        normed = sbuf(scope0, "wide_normed", [P, DC, SLOTS * P])
        pair_weights = sbuf(scope0, "wide_pair_weights", [P, 4, DC * D])
        pair_columns = sbuf(scope0, "wide_pair_columns", [P, 4, 2])
        pair_rows = sbuf(scope0, "wide_pair_rows", [P, 2, D])
        weights_high = [sbuf(scope0, f"wide_weights_high{k}", [P, 4, DC * D], F32R) for k in range(2)]
        weights_low = [sbuf(scope0, f"wide_weights_low{k}", [P, 4, DC * D], F32R) for k in range(2)]
        columns = [sbuf(scope0, f"wide_columns{k}", [P, 4, 2]) for k in range(2)]
        value_bias = [sbuf(scope0, f"wide_value_bias{k}", [P, 1, D]) for k in range(2)]
        q0 = sbuf(scope0, "wide_q0", [P, 2, TOK])
        k0 = sbuf(scope0, "wide_k0", [P, 2, GROUP, KEYS0])
        v0 = sbuf(scope0, "wide_v0", [P, GROUP, D])
        neg_max0 = sbuf(scope0, "wide_neg_max0", [P, GROUP, 2])
        sums0 = sbuf(scope0, "wide_sums0", [P, GROUP, 2])
        inverse0 = sbuf(scope0, "wide_inverse0", [P, GROUP, 2])
        probs0 = sbuf(scope0, "wide_probs0", [P, GROUP, 2, KEYS0])
        probs_t0 = sbuf(scope0, "wide_probs_t0", [P, GROUP, 2, P])
        heads_high = sbuf(scope0, "wide_heads_high", [P, 2, GROUP, P], F32R)
        heads_low = sbuf(scope0, "wide_heads_low", [P, 2, GROUP, P], F32R)

    with ExitStack() as scope1:
        head_of_8 = sbuf(scope1, "head_of_8", [P, HN])
        head_of_16 = sbuf(scope1, "head_of_16", [P, HN // 2])
        qn = [sbuf(scope1, f"qn{u}", [P, D]) for u in range(SLOTS)]
        kn = [sbuf(scope1, f"kn{u}", [P, D]) for u in range(SLOTS)]
        km = [sbuf(scope1, f"km{u}", [P, HN * D]) for u in range(SLOTS)]
        vn = [sbuf(scope1, f"vn{u}", [P, 2, HN, 17]) for u in range(SLOTS)]
        cn = [sbuf(scope1, f"cn{u}", [P, D]) for u in range(SLOTS)]
        scores_masked = [sbuf(scope1, f"scores_masked{k}", [P, BANK]) for k in range(2)]
        neg_max = [sbuf(scope1, f"neg_max{k}", [P, 4]) for k in range(2)]
        probs = [sbuf(scope1, f"probs{k}", [P, BANK]) for k in range(2)]
        probs_t = [sbuf(scope1, f"probs_t{k}", [P, BANK]) for k in range(2)]
        ones = sbuf(scope1, "ones", [P, HN])
        inverse = sbuf(scope1, "inverse", [P, 2, HN])
        heads_out = [sbuf(scope1, f"heads_out{k}", [P, D]) for k in range(4)]
        heads_t = [sbuf(scope1, f"heads_t{u}", [P, D]) for u in range(SLOTS)]
        wq1 = sbuf(scope1, "wq1", [P, P])
        wk1 = sbuf(scope1, "wk1", [P, P])
        wv1 = sbuf(scope1, "wv1", [P, P])
        w_rows1 = sbuf(scope1, "w_rows1", [P, 3, P])
        bias1 = sbuf(scope1, "bias1", [P, 2])
        bq1 = sbuf(scope1, "bq1", [P, 1])
        bv1 = sbuf(scope1, "bv1", [P, 1, P])
        mask_own_bytes = sbuf(scope1, "mask_own_bytes", [B, D], U8)
        mask_own = sbuf(scope1, "mask_own", [B, D])
        mask_keys = sbuf(scope1, "mask_keys", [P, B, 2])
        valid = sbuf(scope1, "valid", [P, B])
        key_mean = sbuf(scope1, "key_mean", [P, SLOTS])
        row_sums = sbuf(scope1, "row_sums", [P, 6, B])
        w_qkv = sbuf(scope1, "w_qkv", [P, 2, DC, 3 * D])
        b_qk2 = sbuf(scope1, "b_qk2", [P, 2, 2, DC])
        b_q2 = sbuf(scope1, "b_q2", [P, 2, DC])
        b_v2 = sbuf(scope1, "b_v2", [P, 2, D])
        w_out2 = sbuf(scope1, "w_out2", [P, 2, DC, D])
        self_mask = sbuf(scope1, "self_mask", [P, 2, P])
        cross_mask = [sbuf(scope1, f"cross_mask{u}", [P, 2, P]) for u in range(SLOTS)]
        rows_t = [sbuf(scope1, f"rows_t{u}", [P, DC, P]) for u in range(SLOTS)]
        cn_t = [sbuf(scope1, f"cn_t{u}", [P, DC, P]) for u in range(SLOTS)]
        positions = sbuf(scope1, "positions", [P, D])
        w3 = sbuf(scope1, "w3", [P, 4, P])
        ln3 = sbuf(scope1, "ln3", [P, 6])
        w3_up = sbuf(scope1, "w3_up", [P, D])
        w3_down = sbuf(scope1, "w3_down", [P, 2, P])
        b3_up = sbuf(scope1, "b3_up", [P, 2])
        b3_down = sbuf(scope1, "b3_down", [P, 1])
        with ExitStack() as scope_early:
            mask_bytes = sbuf(scope_early, "mask_bytes", [P, B, D], U8)
            mask_rows = sbuf(scope_early, "mask_rows", [P, B, D])
            mean_t = sbuf(scope_early, "mean_t", [P, B, D])
            std_t = sbuf(scope_early, "std_t", [P, B, D])
        with ExitStack() as scope_late:
            placed = [sbuf(scope_late, f"placed{u}", [P, 2, D]) for u in range(SLOTS)]
            norm3 = [sbuf(scope_late, f"norm3{u}", [P, 2, D]) for u in range(SLOTS)]
            ln_t3 = [sbuf(scope_late, f"ln_t3{u}", [P, 2, D]) for u in range(SLOTS)]
            hidden3 = [sbuf(scope_late, f"hidden3{u}", [P, 2, D]) for u in range(SLOTS)]
            result = [sbuf(scope_late, f"result{u}", [P, D]) for u in range(SLOTS)]

    idle = sem("idle")
    x_loaded = sem("x_loaded")
    small_loaded = sem("small_loaded")
    weights0_loaded = sem("weights0_loaded")
    heads_known = sem("heads_known")
    ident_ready = sem("ident_ready")
    rows_loaded = [sem(f"rows_loaded{k}") for k in range(2)]
    rows_turned = sem("rows_turned")
    ctx_high_ready = sem("ctx_high_ready")
    ctx_low_ready = sem("ctx_low_ready")
    split_chain = sem("split_chain")
    rows_normed = sem("rows_normed")
    normed_turned = sem("normed_turned")
    normed_ready = sem("normed_ready")
    normed_high_ready = sem("normed_high_ready")
    normed_low_ready = sem("normed_low_ready")
    pair_loaded = sem("pair_loaded")
    split_steps = sem("split_steps")
    weights_split = sem("weights_split")
    qk_ready = sem("qk_ready")
    q_copied = sem("q_copied")
    k_copied = sem("k_copied")
    scores_ready = sem("scores_ready")
    v_ready = sem("v_ready")
    v_copied = sem("v_copied")
    max_ready = sem("max_ready")
    exp_ready = sem("exp_ready")
    softmax_chain = sem("softmax_chain")
    probs_ready = sem("probs_ready")
    probs_turned = sem("probs_turned")
    probs_copied = sem("probs_copied")
    heads_ready = sem("heads_ready")
    heads_high_ready = sem("heads_high_ready")
    heads_split = sem("heads_split")
    out_ready = sem("out_ready")
    x_added = sem("x_added")

    later_loaded = sem("later_loaded")
    weights2_loaded = sem("weights2_loaded")
    masks_ready = sem("masks_ready")
    masks_turned = sem("masks_turned")
    head_steps = sem("head_steps")
    masks_chain = sem("masks_chain")
    std_chain = sem("std_chain")
    std_ready = sem("std_ready")
    out_stored = [sem(f"out_stored{u}") for u in range(SLOTS)]
    result_ready = sem("result_ready")
    ff = FeedForward(sem)
    ff3 = FeedForward3(sem)
    n1 = Narrow(sem, "n1", True, False)
    n2 = Narrow(sem, "n2", True, True)
    n2.cross_chain = sem("n2_cross_chain")
    n3 = Narrow(sem, "n3", True, True)
    n3.ctx_ready = sem("n3_ctx_ready")
    n3.turned_back = sem("n3_turned_back")

    a1 = Attention(n1, units=2, heads=2, keys=D, width=17, mask=False)
    a2s = Attention(n2, units=1, heads=4, keys=P, width=17, mask=True)
    a2c = Attention(n2, units=1, heads=4, keys=P, width=17, mask=True)
    a3 = Attention(n3, units=2, heads=2, keys=D, width=9, mask=False)

    q_bank = [bank[6], bank[7]]
    v_bank = [bank[4], bank[5]]
    score_bank = [bank[0], bank[1]]
    turn_bank = [bank[2], bank[3]]


    def column(name):
        return t[name].rearrange("(c p) -> p c", p=P)

    small_loads = []
    for k, name in enumerate(norms):
        part = ("_scale", "_offset") if name.startswith("L0") else ("_s", "_b")
        small_loads += [(norm_scale[:, k, :], column(name + part[0])), (norm_offset[:, k, :], column(name + part[1]))]
    for k, name in enumerate(row_biases):
        small_loads.append((row_bias[:, k, :], t[name].partition_broadcast(P)))
    small_loads += [(b_up[:, 0, :], column("L0_xattn_b_fc1")), (b_up[:, 1, :], column("L2_xattn_b1"))]
    small_count = 16 * len(small_loads)

    def rows(name):
        return t[name].rearrange("(c p) n -> p c n", p=P)

    def row(name):
        return t[name].partition_broadcast(P)

    later_loads = [(w_rows1[:, k, :], t[f"L1_xattn_W{n}"]) for k, n in enumerate("qkv")]
    later_loads += [(bias1[:, k:k + 1], column(f"L1_xattn_b{n}")) for k, n in enumerate("qk")]
    later_loads += [
        (bv1[:, 0, :], row("L1_xattn_bv")),
        (mask_own_bytes[:, :], t["mask_Bx1x2048_bf1"].rearrange("b a k -> (b a) k")),
        (mask_bytes[:, :, :].rearrange("p b k -> p (b k)"), t["mask_Bx1x2048_bf1"].rearrange("b a k -> (b a k)").partition_broadcast(P)),
        (w_qkv[:, 0, :, :], rows("L2_xattn_w_qkv")),
        (w_qkv[:, 1, :, 0:D], rows("L2_xattn_w_q")),
        (w_qkv[:, 1, :, D:3 * D], rows("L2_xattn_w_kv")),
        (w_out2[:, 0, :, :], rows("L2_xattn_w_ao")),
        (w_out2[:, 1, :, :], rows("L2_xattn_w_co")),
        (b_qk2[:, 0, :, :].rearrange("p a c -> p (a c)"), column("L2_xattn_b_qkv")[:, 0:2 * DC]),
        (b_qk2[:, 1, 0, :], column("L2_xattn_b_q")),
        (b_qk2[:, 1, 1, :], column("L2_xattn_b_kv")[:, 0:DC]),
        (b_v2[:, 0, :], t["L2_xattn_b_qkv"][2 * D:3 * D].partition_broadcast(P)),
        (b_v2[:, 1, :], t["L2_xattn_b_kv"][D:2 * D].partition_broadcast(P)),
        (self_mask[:, 0, :], t["mask_1x1xSxS2_fc1"].rearrange("a b q k -> (a b q) k")),
        (positions[:, :], t["positions"]),
        (w3_up[:, :], t["L3_xattn_W1"]),
        (w3_down[:, :, :], rows("L3_xattn_W2")),
        (b3_up[:, :], column("L3_xattn_b1")),
        (b3_down[:, :], column("L3_xattn_b2")),
    ]
    later_loads += [(w3[:, k, :], t[f"L3_xattn_W{n}"]) for k, n in enumerate("qkvo")]
    later_loads += [(ln3[:, k:k + 1], column(f"L3_xattn_{n}")) for k, n in enumerate(
        ("ln_q_g", "ln_q_b", "ln_kv_g", "ln_kv_b", "ffn_ln_g", "ffn_ln_b"))]
    later_count = 16 * len(later_loads)


    block = outer.enter_context(nc.Block())

    @block.tensor
    def _(pe):
        def product3(acc, wh, wl, mh, ml, start, stop):
            pe.matmul(acc, wh, mh, start=start, stop=False)
            pe.matmul(acc, wh, ml, start=False, stop=False)
            return pe.matmul(acc, wl, mh, start=False, stop=stop)

        def turn_context():
            pe.wait_ge(ident_ready, 3)
            for g in range(GROUPS):
                pe.wait_ge(rows_loaded[g % 2], 16 * (g // 2 + 1))
                if g >= 2:
                    pe.wait_ge(ctx_low_ready, DC * (g - 1))
                for c in range(DC):
                    for b in range(GROUP):
                        last = pe.transpose(bank[2 * (g % 2) + c][:, b * P:(b + 1) * P],
                                            ctx_rows[:, g % 2, b, c * P:(c + 1) * P], ident[:, :])
                    last.then_inc(rows_turned, 1)

        def turn_normed(layer):
            with pe.Fori(0, ROUNDS) as i:
                r = ROUNDS * layer + i
                pe.wait_ge(rows_normed, SLOTS * (r + 1))
                for c in range(DC):
                    for u in range(SLOTS):
                        last = pe.transpose(bank[4][:, (SLOTS * c + u) * P:(SLOTS * c + u + 1) * P],
                                            norm_rows[:, u, c * P:(c + 1) * P], ident[:, :])
                last.then_inc(normed_turned, 1)

        def pairs(layer):
            pe.wait_ge(normed_low_ready, DC * ROUNDS * (layer + 1))
            if layer == 0:
                pe.wait_ge(ctx_low_ready, DC * GROUPS)
            with pe.Fori(0, PAIRS // 2) as i:
                for slot in range(2):
                    pair(PAIRS * layer + 2 * i + slot, slot)

        def pair(p, slot):
            wh, wl = weights_high[slot], weights_low[slot]

            def out_product(n):
                pe.wait_ge(heads_split, GROUP * (GROUPS * p + n) + 2 * GROUP)
                if n == GROUPS - 1:
                    pe.wait_ge(x_added, 8 * p + 2 * n + ADD_CREDIT)
                for b in range(GROUP):
                    acc = bank[b // 2][:, (b % 2) * D:(b % 2 + 1) * D]
                    for h in range(2):
                        w = slice(h * D, (h + 1) * D)
                        last = product3(acc, heads_high[:, h, b, :], heads_low[:, h, b, :],
                                        wh[:, 3, w], wl[:, 3, w], h == 0, h == 1)
                    if b % 2:
                        last.then_inc(out_ready, 1)

            pe.wait_ge(weights_split, p + 2)
            for n in range(GROUPS):
                g = GROUPS * p + n
                tok = slice(n * TOK, (n + 1) * TOK)
                for m in range(4):
                    kind, h = m // 2, m % 2
                    if m < 2 and n == 0:
                        pe.wait_ge(x_added, 8 * (p - 1) + 7 + m + ADD_CREDIT)
                    elif m < 2 and n == 1:
                        pe.wait_ge(k_copied, 2 * g - 1 + m)
                    elif m < 2:
                        pe.wait_ge(x_added, 8 * p + 2 * (n - 2) + 1 + m + ADD_CREDIT)
                    else:
                        pe.wait_ge(q_copied, 2 * g + 1 + h)
                    mh, ml = ((normed_high, normed_low), (ctx_high, ctx_low))[kind]
                    for c in range(DC):
                        w = slice(c * D + h * P, c * D + (h + 1) * P)
                        last = product3(bank[h][:, :], wh[:, kind, w], wl[:, kind, w],
                                        mh[:, c, tok], ml[:, c, tok], c == 0, c == DC - 1)
                    last.then_inc(qk_ready, 1)

                def scores(b):
                    if b >= 2:
                        pe.wait_ge(exp_ready, GROUP * g + b - 1)
                    for h in range(2):
                        last = pe.matmul(bank[4 + b % 2][:, h * KEYS0:(h + 1) * KEYS0],
                                         q0[:, h, b * P:(b + 1) * P], k0[:, h, b, :], start=True, stop=True)
                    last.then_inc(scores_ready, 1)

                def turn_probs(b):
                    pe.wait_ge(probs_ready, GROUP * g + b + 1)
                    if b >= 2:
                        pe.wait_ge(probs_copied, GROUP * g + b - 1)
                    for h in range(2):
                        last = pe.transpose(bank[6 + b % 2][:, h * P:(h + 1) * P], probs0[:, b, h, 0:P], ident[:, :])
                    last.then_inc(probs_turned, 1)

                def sum_values(b):
                    pe.wait_ge(probs_copied, GROUP * g + b + 1)
                    if b < 2:
                        pe.wait_ge(v_copied, 2 * g + b + 1)
                    else:
                        pe.wait_ge(heads_split, GROUP * g + b - 1 + GROUP)
                    for h in range(2):
                        last = pe.matmul(bank[2 + b % 2][:, h * P:(h + 1) * P], v0[:, b, h * P:(h + 1) * P],
                                         probs_t0[:, b, h, :], start=True, stop=True)
                    last.then_inc(heads_ready, 1)

                pe.wait_ge(q_copied, 2 * g + 2)
                pe.wait_ge(k_copied, 2 * g + 2)
                scores(0)
                scores(1)
                for half in range(2):
                    pe.wait_ge(heads_split, GROUP * (g - 1) + 3 + half + GROUP)
                    for k in range(2):
                        b = 2 * half + k
                        keys = slice(n * TOK + b * P, n * TOK + (b + 1) * P)
                        for c in range(DC):
                            w = slice(c * D, (c + 1) * D)
                            last = product3(bank[2 + half][:, k * D:(k + 1) * D], ctx_high[:, c, keys], ctx_low[:, c, keys],
                                            wh[:, 2, w], wl[:, 2, w], c == 0, c == DC - 1)
                    last.then_inc(v_ready, 1)
                if n:
                    out_product(n - 1)
                for b in range(GROUP + 1):
                    if b < GROUP:
                        turn_probs(b)
                    if b + 2 < GROUP:
                        scores(b + 2)
                    if b:
                        sum_values(b - 1)
            out_product(GROUPS - 1)

        def feed_forward(which, weights_loaded):
            s = ff
            pe.wait_ge(weights_loaded, 32)
            with pe.Fori(0, ROUNDS) as i:
                r = i + ROUNDS * (which == 2)
                pe.wait_ge(s.rows_normed, SLOTS * (r + 1))
                for c in range(DC):
                    for u in range(SLOTS):
                        last = pe.transpose(bank[0][:, (SLOTS * c + u) * P:(SLOTS * c + u + 1) * P],
                                            norm_rows[:, u, c * P:(c + 1) * P], ident[:, :])
                last.then_inc(s.turned, 1)
                pe.wait_ge(s.in_ready, DC * (r + 1))
                for f in range(F0 // P):
                    for c in range(DC):
                        last = pe.matmul(bank[1 + f // 2][:, (f % 2) * D:(f % 2 + 1) * D], w_up[:, c, f * P:(f + 1) * P],
                                         hidden_in[:, c, :], start=c == 0, stop=c == DC - 1)
                    if f % 2:
                        last.then_inc(s.up_ready, 1)
                for u in range(SLOTS):
                    for f in range(F0 // P):
                        if u == 0:
                            pe.wait_ge(s.hidden_ready, F0 // P * r + f + 1)
                        last = pe.matmul(bank[5][:, u * D:(u + 1) * D], hidden[:, f, u * P:(u + 1) * P],
                                         w_down[:, f, :], start=f == 0, stop=f == F0 // P - 1)
                last.then_inc(s.down_ready, 1)

        def narrow_attention(a, i, q_of, k_of):
            s = a.s
            for j in range(a.per_round + 2):
                if j < a.per_round:
                    u, unit, step = j // a.per_slot, j // a.steps % a.units, j % a.steps
                    if j % a.per_slot == 0:
                        pe.wait_ge(s.spread, SLOTS * i + u + 1)
                        pe.wait_ge(s.q_ready, SLOTS * i + u + 1)
                    if j >= 2:
                        pe.wait_ge(s.exp_ready, a.per_round * i + j - 1)
                    pe.matmul(score_bank[j % 2][:, :], q_of(u, unit, step), k_of(u, step),
                              start=True, stop=True).then_inc(s.scores, 1)
                if 1 <= j <= a.per_round:
                    k = j - 1
                    pe.wait_ge(s.exp_ready, a.per_round * i + k + 1)
                    if k >= 2:
                        pe.wait_ge(s.probs_copied, a.per_round * i + k - 1)
                    for n in range(BANK // P):
                        last = pe.transpose(turn_bank[k % 2][:, n * P:(n + 1) * P],
                                            probs[k % 2][:, n * P:(n + 1) * P], ident[:, :])
                    last.then_inc(s.probs_turned, 1)
                if j >= 2:
                    k = j - 2
                    u, w, step = k // a.per_slot, k // a.steps, k % a.steps
                    pe.wait_ge(s.probs_copied, a.per_round * i + k + 1)
                    if k % a.per_slot == 0:
                        pe.wait_ge(s.v_ready, SLOTS * i + u + 1)
                    if w >= 2 and step == 0:
                        pe.wait_ge(s.heads_taken, a.all_units * i + w - 1)
                    for n in range(a.heads):
                        h = step * a.heads + n
                        for c in range(a.blocks):
                            m = n * a.blocks + c
                            last = pe.matmul(v_bank[w % 2][:, h * a.width:(h + 1) * a.width],
                                             probs_t[k % 2][:, m * P:(m + 1) * P], vn[u][:, c, h, 0:a.width],
                                             start=c == 0, stop=c == a.blocks - 1)
                    last.then_inc(s.heads, 1)

        def layer1():
            s = n1
            pe.wait_ge(later_loaded, later_count)
            pe.wait_ge(masks_ready, 1)
            for k in range(3):
                pe.transpose(bank[0][:, k * P:(k + 1) * P], w_rows1[:, k, :], ident[:, :])
            for c in range(2):
                last = pe.transpose(bank[1][:, c * B:(c + 1) * B], mask_own[:, c * P:(c + 1) * P], ident[0:B, 0:B])
            last.then_inc(masks_turned, 1)
            pe.wait_ge(masks_ready, 3)
            with pe.Fori(0, ROUNDS) as i:
                for u in range(SLOTS):
                    b = SLOTS * i + u
                    pe.wait_ge((s.loaded0, s.loaded1)[u], 16 * (i + 1))
                    pe.wait_ge(s.x_added, b + 1)
                    pe.matmul(q_bank[u][:, 0:D], wq1[:, :], x[:, ds(b, 1), :].rearrange("p a d -> p (a d)"), start=True, stop=True)
                    pe.matmul(q_bank[u][:, D:2 * D], wk1[:, :], cn[u][:, :], start=True, stop=True).then_inc(s.projected, 1)
                    for c in range(2):
                        last = pe.matmul(v_bank[u][:, c * P:(c + 1) * P], cn[u][:, c * P:(c + 1) * P], wv1[:, :],
                                         start=True, stop=True)
                    last.then_inc(s.values, 1)
                narrow_attention(a1, i, lambda u, unit, step: qn[u][:, unit * P:(unit + 1) * P],
                                 lambda u, step: km[u][:, step * BANK:(step + 1) * BANK])
                for w in range(a1.all_units):
                    u, unit = w // 2, w % 2
                    pe.wait_ge(s.heads_taken, a1.all_units * i + w + 1)
                    for n in range(2):
                        last = pe.transpose(q_bank[u][:, (2 * n + unit) * P:(2 * n + unit + 1) * P],
                                            heads_out[w][:, n * P:(n + 1) * P], ident[:, :])
                    if unit:
                        last.then_inc(s.result, 1)

        def layer2(a, cross):
            s = a.s
            with pe.Fori(0, ROUNDS) as i:
                r = i + ROUNDS * int(cross)
                for u in range(SLOTS):
                    pe.wait_ge(s.rows_normed, SLOTS * r + u + 1)
                    if cross:
                        pe.wait_ge((s.loaded0, s.loaded1)[u], 32 * (i + 1))
                    for c in range(DC):
                        last = pe.transpose(q_bank[u][:, c * P:(c + 1) * P], norm_rows[:, u, c * P:(c + 1) * P], ident[:, :])
                    if cross:
                        for c in range(DC):
                            last = pe.transpose(q_bank[u][:, (DC + c) * P:(DC + c + 1) * P], cn[u][:, c * P:(c + 1) * P],
                                                ident[:, :])
                    last.then_inc(s.turned, 1)
                for u in range(SLOTS):
                    pe.wait_ge(s.in_ready, SLOTS * r + u + 1)
                    keys_in = cn_t[u] if cross else rows_t[u]
                    for m in range(4):
                        src = rows_t[u] if m < 2 else keys_in
                        for c in range(DC):
                            last = pe.matmul(q_bank[u][:, m * P:(m + 1) * P], w_qkv[:, int(cross), c, m * P:(m + 1) * P],
                                             src[:, c, :], start=c == 0, stop=c == DC - 1)
                    last.then_inc(s.projected, 1)
                    for c in range(DC):
                        last = pe.matmul(v_bank[u][:, 0:D], keys_in[:, c, :], w_qkv[:, int(cross), c, 2 * D:3 * D],
                                         start=c == 0, stop=c == DC - 1)
                    last.then_inc(s.values, 1)
                narrow_attention(a, r, lambda u, unit, step: qn[u][:, step // 2 * P:(step // 2 + 1) * P],
                                 lambda u, step: km[u][:, step * BANK:(step + 1) * BANK])
                for u in range(SLOTS):
                    pe.wait_ge(s.heads_taken, SLOTS * r + u + 1)
                    for c in range(DC):
                        last = pe.transpose(q_bank[u][:, c * P:(c + 1) * P], heads_out[u][:, c * P:(c + 1) * P], ident[:, :])
                    last.then_inc(s.heads_turned, 1)
                for u in range(SLOTS):
                    pe.wait_ge(s.heads_copied, SLOTS * r + u + 1)
                    for c in range(DC):
                        last = pe.matmul(q_bank[u][:, D:2 * D], heads_t[u][:, c * P:(c + 1) * P], w_out2[:, int(cross), c, :],
                                         start=c == 0, stop=c == DC - 1)
                    last.then_inc(s.result, 1)

        def layer3():
            s = n3
            with pe.Fori(0, ROUNDS) as i:
                for u in range(SLOTS):
                    pe.wait_ge(s.ctx_ready, SLOTS * i + u + 1)
                    for n in range(4):
                        last = pe.transpose(q_bank[u][:, n * P:(n + 1) * P], placed[u][:, n // 2, n % 2 * P:(n % 2 + 1) * P],
                                            ident[:, :])
                    last.then_inc(s.turned, 1)
                for u in range(SLOTS):
                    pe.wait_ge(s.rows_normed, SLOTS * i + u + 1)
                    for n in range(4):
                        last = pe.transpose(v_bank[u][:, n * P:(n + 1) * P], norm3[u][:, n // 2, n % 2 * P:(n % 2 + 1) * P],
                                            ident[:, :])
                    last.then_inc(s.turned_back, 1)
                for u in range(SLOTS):
                    pe.wait_ge(s.in_ready, SLOTS * i + u + 1)
                    for n in range(2):
                        last = pe.matmul(q_bank[u][:, n * D:(n + 1) * D], w3[:, n, :], ln_t3[u][:, n, :], start=True, stop=True)
                    last.then_inc(s.projected, 1)
                    for c in range(2):
                        last = pe.matmul(v_bank[u][:, c * P:(c + 1) * P], ln_t3[u][:, 1, c * P:(c + 1) * P], w3[:, 2, :],
                                         start=True, stop=True)
                    last.then_inc(s.values, 1)
                narrow_attention(a3, i, lambda u, unit, step: qn[u][:, unit * P:(unit + 1) * P],
                                 lambda u, step: km[u][:, step * BANK:(step + 1) * BANK])
                for u in range(SLOTS):
                    pe.wait_ge(s.heads_taken, a3.all_units * i + 2 * (u + 1))
                    for n in range(2):
                        last = pe.transpose(q_bank[u][:, n * P:(n + 1) * P], heads_out[2 * u + n][:, 0:P], ident[:, :])
                    last.then_inc(s.heads_turned, 1)
                for u in range(SLOTS):
                    pe.wait_ge(s.heads_copied, SLOTS * i + u + 1)
                    pe.matmul(q_bank[u][:, D:2 * D], w3[:, 3, :], heads_t[u][:, :], start=True, stop=True).then_inc(s.result, 1)

        def feed_forward3():
            s = ff3
            with pe.Fori(0, ROUNDS) as i:
                for u in range(SLOTS):
                    b = SLOTS * i + u
                    pe.wait_ge(s.x_copied, b + 1)
                    for n in range(2):
                        last = pe.transpose(bank[u][:, n * P:(n + 1) * P], placed[u][:, 0, n * P:(n + 1) * P], ident[:, :])
                    last.then_inc(s.turned, 1)
                for u in range(SLOTS):
                    b = SLOTS * i + u
                    pe.wait_ge(s.rows_normed, b + 1)
                    for n in range(2):
                        last = pe.transpose(bank[2 + u][:, n * P:(n + 1) * P], norm3[u][:, 0, n * P:(n + 1) * P], ident[:, :])
                    last.then_inc(s.turned_back, 1)
                for u in range(SLOTS):
                    b = SLOTS * i + u
                    pe.wait_ge(s.in_ready, b + 1)
                    for f in range(2):
                        last = pe.matmul(bank[4 + u][:, f * D:(f + 1) * D], w3_up[:, f * P:(f + 1) * P], ln_t3[u][:, 0, :],
                                         start=True, stop=True)
                    last.then_inc(s.up_ready, 1)
                for u in range(SLOTS):
                    b = SLOTS * i + u
                    pe.wait_ge(s.hidden_ready, 2 * (b + 1))
                    for f in range(2):
                        last = pe.matmul(bank[6 + u][:, 0:D], w3_down[:, f, :], hidden3[u][:, f, :], start=f == 0, stop=f == 1)
                    last.then_inc(s.down_ready, 1)

        turn_context()
        for layer in range(2):
            turn_normed(layer)
            pairs(layer)
        feed_forward(0, weights0_loaded)
        layer1()
        layer2(a2s, False)
        layer2(a2c, True)
        feed_forward(2, weights2_loaded)
        layer3()
        feed_forward3()

    @block.scalar
    def _(act):
        def split_context():
            for g in range(GROUPS):
                for c in range(DC):
                    act.wait_ge(rows_turned, DC * g + c + 1)
                    act.activation(ctx_high[:, c, g * TOK:(g + 1) * TOK], bank[2 * (g % 2) + c][:, :], ACT.Copy)\
                       .then_inc(ctx_high_ready, 1)

        def split_normed(layer):
            with act.Fori(0, ROUNDS) as i:
                for c in range(DC):
                    act.wait_ge(normed_ready, DC * (ROUNDS * layer + i) + c + 1)
                    act.sem_inc(idle, 1)
                    act.activation(normed_high[:, c, ds(i * SLOTS * P, SLOTS * P)], normed[:, c, :], ACT.Copy)\
                       .then_inc(normed_high_ready, 1)

        def pairs(layer):
            with act.Fori(0, PAIRS // 2) as i:
                for slot in range(2):
                    pair(PAIRS * layer + 2 * i + slot, slot)

        def pair(p, slot):
            act.wait_ge(weights_split, p + 2)
            for n in range(GROUPS):
                g = GROUPS * p + n
                for h in range(2):
                    act.wait_ge(qk_ready, 4 * g + 2 + h + 1)
                    if n == 0:
                        act.activation(k0[:, h, :, P:P + 1], columns[slot][:, 2:3, h:h + 1].broadcast_to([P, GROUP, 1]), ACT.Copy)
                    act.activation(k0[:, h, :, 0:P], bank[h][:, :].rearrange("p (b k) -> p b k", b=GROUP), ACT.Identity,
                                   bias=columns[slot][:, 1, h:h + 1]).then_inc(k_copied, 1)

                def exponentials(b):
                    act.wait_ge(max_ready, GROUP * g + b + 1)
                    for h in range(2):
                        last = act.activation(probs0[:, b, h, :], bank[4 + b % 2][:, h * KEYS0:(h + 1) * KEYS0], ACT.Exp,
                                              bias=neg_max0[:, b, h:h + 1], accum_out=sums0[:, b, h:h + 1])
                    last.then_inc(exp_ready, 1)

                def copy_probs(b):
                    act.wait_ge(probs_turned, GROUP * g + b + 1)
                    act.activation(probs_t0[:, b, :, :], bank[6 + b % 2][:, 0:2 * P].rearrange("p (h q) -> p h q", h=2), ACT.Copy)\
                       .then_inc(probs_copied, 1)

                def high_heads(b):
                    act.wait_ge(heads_ready, GROUP * g + b + 1)
                    for h in range(2):
                        last = act.activation(heads_high[:, h, b, :], bank[2 + b % 2][:, h * P:(h + 1) * P], ACT.Identity,
                                              bias=columns[slot][:, 3, h:h + 1])
                    last.then_inc(heads_high_ready, 1)

                exponentials(0)
                exponentials(1)
                for b in range(GROUP):
                    copy_probs(b)
                    if b + 2 < GROUP:
                        exponentials(b + 2)
                    if b:
                        high_heads(b - 1)
                high_heads(GROUP - 1)

        def feed_forward(which, norm, function):
            s = ff
            with act.Fori(0, ROUNDS) as i:
                r = i + ROUNDS * (which == 2)
                act.wait_ge(s.turned, r + 1)
                for c in range(DC):
                    act.activation(hidden_in[:, c, :], bank[0][:, c * D:(c + 1) * D], ACT.Identity, bias=norm_offset[:, norm, c:c + 1],
                                   scale=norm_scale[:, norm, c:c + 1]).then_inc(s.in_ready, 1)
                for f in range(F0 // P):
                    act.wait_ge(s.up_ready, F0 // P // 2 * r + f // 2 + 1)
                    act.activation(hidden[:, f, :], bank[1 + f // 2][:, (f % 2) * D:(f % 2 + 1) * D], function,
                                   bias=b_up[:, which // 2, f:f + 1]).then_inc(s.hidden_ready, 1)

        def narrow_attention(a, i):
            s = a.s
            for j in range(a.per_round + 1):
                if j < a.per_round:
                    act.wait_ge(s.max_ready, a.per_round * i + j + 1)
                    if j >= 2:
                        act.wait_ge(s.probs_turned, a.per_round * i + j - 1)
                    source = scores_masked[j % 2] if a.mask else score_bank[j % 2]
                    for h in range(a.heads):
                        part = slice(h * a.keys, (h + 1) * a.keys)
                        last = act.activation(probs[j % 2][:, part], source[:, part], ACT.Exp, bias=neg_max[j % 2][:, h:h + 1])
                    last.then_inc(s.exp_ready, 1)
                if j >= 1:
                    k = j - 1
                    act.wait_ge(s.probs_turned, a.per_round * i + k + 1)
                    if k >= 2:
                        act.wait_ge(s.heads, a.per_round * i + k - 1)
                    act.activation(probs_t[k % 2][:, :], turn_bank[k % 2][:, :], ACT.Copy).then_inc(s.probs_copied, 1)

        def layer1():
            s = n1
            act.wait_ge(masks_ready, 3)
            with act.Fori(0, ROUNDS) as i:
                for u in range(SLOTS):
                    act.wait_ge(s.projected, SLOTS * i + u + 1)
                    act.activation(qn[u][:, :], q_bank[u][:, 0:D], ACT.Identity, bias=bq1[:, 0:1], scale=SCALE1).then_inc(s.q_ready, 1)
                    act.activation(kn[u][:, :], q_bank[u][:, D:2 * D], ACT.Identity, bias=bias1[:, 1:2]).then_inc(s.k_ready, 1)
                narrow_attention(a1, i)
            act.wait_ge(s.x_added, B + SLOTS)
            act.activation(std_t[:, :, :], std_t[:, :, :], ACT.Sqrt).then_inc(std_ready, 1)

        def layer2(a, cross):
            s = a.s
            norm = 3 + int(cross)
            with act.Fori(0, ROUNDS) as i:
                r = i + ROUNDS * int(cross)
                for u in range(SLOTS):
                    act.wait_ge(s.turned, SLOTS * r + u + 1)
                    for c in range(DC):
                        last = act.activation(rows_t[u][:, c, :], q_bank[u][:, c * P:(c + 1) * P], ACT.Identity,
                                              bias=norm_offset[:, norm, c:c + 1], scale=norm_scale[:, norm, c:c + 1])
                    if cross:
                        last = act.activation(cn_t[u][:, :, :], q_bank[u][:, D:2 * D].rearrange("p (c k) -> p c k", c=DC), ACT.Copy)
                    last.then_inc(s.in_ready, 1)
                for u in range(SLOTS):
                    act.wait_ge(s.projected, SLOTS * r + u + 1)
                    for c in range(DC):
                        last = act.activation(qn[u][:, c * P:(c + 1) * P], q_bank[u][:, c * P:(c + 1) * P], ACT.Identity,
                                              bias=b_q2[:, int(cross), c:c + 1], scale=SCALE2)
                    last.then_inc(s.q_ready, 1)
                    for c in range(DC):
                        last = act.activation(kn[u][:, c * P:(c + 1) * P], q_bank[u][:, (DC + c) * P:(DC + c + 1) * P], ACT.Identity,
                                              bias=b_qk2[:, int(cross), 1, c:c + 1])
                    last.then_inc(s.k_ready, 1)
                narrow_attention(a, r)
                for u in range(SLOTS):
                    act.wait_ge(s.heads_turned, SLOTS * r + u + 1)
                    act.activation(heads_t[u][:, :], q_bank[u][:, 0:D], ACT.Copy).then_inc(s.heads_copied, 1)

        def layer3():
            s = n3
            with act.Fori(0, ROUNDS) as i:
                for u in range(SLOTS):
                    act.wait_ge(s.turned_back, SLOTS * i + u + 1)
                    for n in range(2):
                        last = act.activation(ln_t3[u][:, n, :], v_bank[u][:, n * D:(n + 1) * D], ACT.Identity,
                                              bias=ln3[:, 2 * n + 1:2 * n + 2], scale=ln3[:, 2 * n:2 * n + 1])
                    last.then_inc(s.in_ready, 1)
                for u in range(SLOTS):
                    act.wait_ge(s.projected, SLOTS * i + u + 1)
                    act.activation(qn[u][:, :], q_bank[u][:, 0:D], ACT.Copy, scale=SCALE1).then_inc(s.q_ready, 1)
                    act.activation(kn[u][:, :], q_bank[u][:, D:2 * D], ACT.Copy).then_inc(s.k_ready, 1)
                narrow_attention(a3, i)
                for u in range(SLOTS):
                    act.wait_ge(s.heads_turned, SLOTS * i + u + 1)
                    act.activation(heads_t[u][:, :], q_bank[u][:, 0:D], ACT.Copy).then_inc(s.heads_copied, 1)

        def feed_forward3():
            s = ff3
            with act.Fori(0, ROUNDS) as i:
                for u in range(SLOTS):
                    act.wait_ge(s.turned_back, SLOTS * i + u + 1)
                    act.activation(ln_t3[u][:, 0, :], bank[2 + u][:, 0:D], ACT.Identity, bias=ln3[:, 5:6], scale=ln3[:, 4:5])\
                       .then_inc(s.in_ready, 1)
                for u in range(SLOTS):
                    act.wait_ge(s.up_ready, SLOTS * i + u + 1)
                    for f in range(2):
                        act.activation(hidden3[u][:, f, :], bank[4 + u][:, f * D:(f + 1) * D], ACT.Gelu, bias=b3_up[:, f:f + 1])\
                           .then_inc(s.hidden_ready, 1)

        split_context()
        for layer in range(2):
            split_normed(layer)
            pairs(layer)
        feed_forward(0, 2, ACT.Gelu)
        layer1()
        layer2(a2s, False)
        layer2(a2c, True)
        feed_forward(2, 5, ACT.Gelu_apprx_tanh)
        layer3()
        feed_forward3()

    @block.vector
    def _(dve):
        def spread_over(tile, shape, axis):
            return tile.unsqueeze(axis).broadcast_to(shape)

        def split_context():
            for g in range(GROUPS):
                tok = slice(g * TOK, (g + 1) * TOK)
                for c in range(DC):
                    dve.wait_ge(ctx_high_ready, DC * g + c + 1)
                    dve.tensor_tensor(ctx_low[:, c, tok], bank[2 * (g % 2) + c][:, :], ctx_high[:, c, tok].bitcast(F32),
                                      ALU.subtract).then_inc(ctx_low_ready, 1)

        def norm_two(chain, i, sem_ready):
            for u in range(SLOTS):
                chain.mark(dve.bn_stats(stats.sums[:, u, :], x[:, ds(SLOTS * i + u, 1), :].rearrange("p a d -> p (a d)")))
            chain.join()
            dve.sem_inc(idle, 1)
            for u in range(SLOTS):
                chain.mark(dve.bn_aggr(stats.mean_var[:, u, :], stats.sums[:, u, :]))
            chain.join()
            inverse_root(dve, chain, stats.rstd[:, 0:SLOTS], stats.mean_var[:, 0:SLOTS, 1], stats.shifted[:, 0:SLOTS],
                         stats.work[:, 0:SLOTS])
            for u in range(SLOTS):
                dve.tensor_scalar(norm_rows[:, u, :], x[:, ds(SLOTS * i + u, 1), :].rearrange("p a d -> p (a d)"),
                                  stats.mean_var[:, u, 0:1], stats.rstd[:, u:u + 1], ALU.subtract, ALU.mult)\
                   .then_inc(sem_ready, 1)

        NORM_TWO = 2 * SLOTS + 11

        def add_row_bias(chain, i, bias):
            both = x[:, ds(SLOTS * i, SLOTS), :]
            chain.mark(dve.tensor_tensor(both, both, row_bias[:, bias:bias + 1, :].broadcast_to([P, SLOTS, D]), ALU.add))

        def norm_and_split(layer):
            with dve.Fori(0, ROUNDS) as i:
                r = ROUNDS * layer + i
                chain = Chain(dve, split_chain, (NORM_TWO + 1) * r)
                norm_two(chain, i, rows_normed)
                dve.wait_ge(rows_normed, SLOTS * (r + 1))
                add_row_bias(chain, i, layer)
                dve.wait_ge(normed_turned, r + 1)
                tok = ds(i * SLOTS * P, SLOTS * P)
                for c in range(DC):
                    dve.tensor_scalar(normed[:, c, :], bank[4][:, c * D:(c + 1) * D], norm_scale[:, layer, c:c + 1],
                                      norm_offset[:, layer, c:c + 1], ALU.mult, ALU.add).then_inc(normed_ready, 1)
                for c in range(DC):
                    dve.wait_ge(normed_high_ready, DC * r + c + 1)
                    dve.tensor_tensor(normed_low[:, c, tok], normed[:, c, :], normed_high[:, c, tok].bitcast(F32),
                                      ALU.subtract).then_inc(normed_low_ready, 1)
            dve.wait_ge(split_chain, (NORM_TWO + 1) * ROUNDS * (layer + 1))

        def pairs(layer):
            with dve.Fori(0, PAIRS // 2) as i:
                for slot in range(2):
                    pair(PAIRS * layer + 2 * i + slot, slot)
            dve.wait_ge(x_added, 8 * PAIRS * (layer + 1) + ADD_CREDIT)

        def pair(p, slot):
            def add_output(n):
                for half in range(2):
                    dve.wait_ge(out_ready, 8 * p + 2 * n + half + 1)
                    rows = x[:, GROUP * n + 2 * half:GROUP * n + 2 * half + 2, :]
                    dve.wait_ge(x_added, 8 * (p - 1) + 2 * n + half + 1 + ADD_CREDIT)
                    dve.tensor_tensor(rows, rows, bank[half][:, :].rearrange("p (b d) -> p b d", b=2), ALU.add)\
                       .then_inc(x_added, 1)

            dve.wait_ge(weights_split, p + 2)
            for n in range(GROUPS):
                g = GROUPS * p + n
                chain = Chain(dve, softmax_chain, GROUP * g)
                for h in range(2):
                    dve.wait_ge(qk_ready, 4 * g + h + 1)
                    dve.tensor_scalar(q0[:, h, :], bank[h][:, :], columns[slot][:, 0, h:h + 1], SCALE0, ALU.add, ALU.mult)\
                       .then_inc(q_copied, 1)

                def row_max(b):
                    dve.wait_ge(scores_ready, GROUP * g + b + 1)
                    dve.tensor_reduce(neg_max0[:, b, :], bank[4 + b % 2][:, 0:2 * KEYS0].rearrange("p (h k) -> p h k", h=2),
                                      X_AXIS, ALU.max, negate=True).then_inc(max_ready, 1)

                def normalise(b):
                    dve.wait_ge(exp_ready, GROUP * g + b + 1)
                    chain.link(dve.reciprocal(inverse0[:, b, :], sums0[:, b, :]))
                    for h in range(2):
                        last = dve.tensor_scalar(probs0[:, b, h, 0:P], probs0[:, b, h, 0:P], inverse0[:, b, h:h + 1], None,
                                                 ALU.mult)
                    last.then_inc(probs_ready, 1)

                def split_heads(b):
                    dve.wait_ge(heads_high_ready, GROUP * g + b + 1)
                    for h in range(2):
                        last = dve.scalar_tensor_tensor(heads_low[:, h, b, :], bank[2 + b % 2][:, h * P:(h + 1) * P],
                                                        columns[slot][:, 3, h:h + 1], heads_high[:, h, b, :].bitcast(F32),
                                                        ALU.add, ALU.subtract)
                    last.then_inc(heads_split, 1)

                row_max(0)
                row_max(1)
                for half in range(2):
                    dve.wait_ge(v_ready, 2 * g + half + 1)
                    dve.tensor_tensor(v0[:, 2 * half:2 * half + 2, :], bank[2 + half][:, :].rearrange("p (b d) -> p b d", b=2),
                                      value_bias[slot][:, :, :].broadcast_to([P, 2, D]), ALU.add).then_inc(v_copied, 1)
                if n:
                    add_output(n - 1)
                for b in range(GROUP):
                    normalise(b)
                    if b + 2 < GROUP:
                        row_max(b + 2)
                    if b:
                        split_heads(b - 1)
                split_heads(GROUP - 1)
            add_output(GROUPS - 1)

        def feed_forward(which, bias):
            s = ff
            steps = NORM_TWO + 1
            with dve.Fori(0, ROUNDS) as i:
                r = i + ROUNDS * (which == 2)
                chain = Chain(dve, s.chain, steps * r)
                norm_two(chain, i, s.rows_normed)
                dve.wait_ge(s.rows_normed, SLOTS * (r + 1))
                add_row_bias(chain, i, bias)
                dve.wait_ge(s.down_ready, r + 1)
                chain.join()
                both = x[:, ds(SLOTS * i, SLOTS), :]
                dve.tensor_tensor(both, both, bank[5][:, :].rearrange("p (u d) -> p u d", u=SLOTS), ALU.add)\
                   .then_inc(s.x_added, 1)
            dve.wait_ge(s.x_added, ROUNDS * (1 + which // 2))

        def narrow_attention(a, i, chain, masks, take_heads):
            s = a.s
            for j in range(a.per_round + 4):
                if j < a.per_round:
                    u = j // a.per_slot
                    source = score_bank[j % 2][:, :].rearrange("p (h k) -> p h k", h=a.heads)
                    dve.wait_ge(s.scores, a.per_round * i + j + 1)
                    if masks is not None:
                        masked = scores_masked[j % 2][:, :].rearrange("p (h k) -> p h k", h=a.heads)
                        mask = masks(u)
                        wide = [P, a.heads, a.keys]
                        chain.link(dve.tensor_tensor(masked, source, mask[:, 0:1, :].broadcast_to(wide), ALU.mult))
                        chain.link(dve.tensor_tensor(masked, masked, mask[:, 1:2, :].broadcast_to(wide), ALU.add))
                        source = masked
                    dve.tensor_reduce(neg_max[j % 2][:, 0:a.heads], source, X_AXIS, ALU.max, negate=True)\
                       .then_inc(s.max_ready, 1)
                if j > 3 and (j - 3) % a.steps == 0:
                    w = (j - 3) // a.steps - 1
                    dve.wait_ge(s.heads, a.per_round * i + (w + 1) * a.steps)
                    sums = v_bank[w % 2][:, 0:HN * a.width].rearrange("p (h e) -> p h e", h=HN)
                    chain.link(dve.reciprocal(inverse[:, w % 2, :].unsqueeze(2), sums[:, :, a.width - 1:a.width]))
                    take_heads(w, sums)

        def weighted(w, target, sums):
            return dve.tensor_tensor(target.rearrange("p (h e) -> p h e", h=HN), sums,
                                     inverse[:, w % 2, :].unsqueeze(2).broadcast_to([P, HN, sums.shape[2]]), ALU.mult)

        def layer1():
            s = n1
            dve.wait_ge(later_loaded, later_count)
            chain = Chain(dve, masks_chain)
            chain.mark(dve.tensor_copy(mask_own[:, :], mask_own_bytes[:, :]))
            chain.mark(dve.memset(ones[:, :], 1.0))
            chain.mark(dve.tensor_scalar(bq1[:, :], bias1[:, 0:1], SCALE1, None, ALU.mult))
            chain.mark(dve.tensor_scalar(b_q2[:, :, :], b_qk2[:, :, 0, :], SCALE2, None, ALU.mult))
            chain.mark(dve.tensor_scalar(self_mask[:, 1, :], self_mask[:, 0, :], NEG_BIG, -NEG_BIG, ALU.mult, ALU.add))
            chain.join()
            dve.tensor_copy(mask_rows[:, :, :], mask_bytes[:, :, :]).then_inc(masks_ready, 1)
            dve.wait_ge(masks_ready, 1)
            chain.link(dve.tensor_reduce(valid[:, :], mask_rows[:, :, :], X_AXIS, ALU.add))
            chain.link(dve.reciprocal(valid[:, :], valid[:, :]))
            dve.wait_ge(masks_turned, 1)
            for k, w in enumerate((wq1, wk1, wv1)):
                chain.mark(dve.tensor_copy(w[:, :], bank[0][:, k * P:(k + 1) * P]))
            chain.join()
            dve.tensor_copy(mask_keys[:, :, :].rearrange("p b c -> p c b"), bank[1][:, 0:2 * B].rearrange("p (c b) -> p c b", c=2))\
               .then_inc(masks_ready, 1)
            dve.wait_ge(masks_ready, 2)
            dve.wait_ge(heads_known, 3)
            dve.sem_inc(masks_ready, 1)

            def take_heads(chain, w, sums):
                mean, square = heads_out[w][:, 0:P], heads_out[w][:, P:2 * P]
                chain.mark(weighted(w, mean, sums[:, :, 0:8]))
                chain.link(weighted(w, square, sums[:, :, 8:16]))
                chain.link(dve.tensor_tensor(scores_masked[0][:, 0:P], mean, mean, ALU.mult))
                dve.tensor_tensor(square, square, scores_masked[0][:, 0:P], ALU.subtract).then_inc(s.heads_taken, 1)

            dve.sem_inc(s.x_added, SLOTS)
            steps = SLOTS * 12 + a1.all_units * 4
            with dve.Fori(0, ROUNDS) as i:
                chain = Chain(dve, s.chain, steps * i)
                for u in range(SLOTS):
                    b = SLOTS * i + u
                    mask = mask_rows[:, ds(b, 1), :].rearrange("p a d -> p (a d)")
                    dve.wait_ge(s.k_ready, b + 1)
                    scratch = scores_masked[u][:, 0:D]
                    chain.link(dve.tensor_tensor(scratch, kn[u][:, :], mask, ALU.mult))
                    chain.link(dve.tensor_reduce(key_mean[:, u:u + 1], scratch, X_AXIS, ALU.add))
                    chain.link(dve.tensor_tensor(key_mean[:, u:u + 1], key_mean[:, u:u + 1], valid[:, ds(b, 1)], ALU.mult))
                    chain.link(dve.scalar_tensor_tensor(scratch, kn[u][:, :], key_mean[:, u:u + 1], mask, ALU.subtract, ALU.mult))
                    chain.link(dve.tensor_scalar(kn[u][:, :], scratch, key_mean[:, u:u + 1], None, ALU.add))
                    dve.tensor_tensor(km[u][:, :].rearrange("p (h k) -> p h k", h=HN), spread_over(kn[u][:, :], [P, HN, D], 1),
                                      spread_over(head_of_8[:, :], [P, HN, D], 2), ALU.mult).then_inc(s.spread, 1)
                    dve.wait_ge(s.values, b + 1)
                    v = scratch.rearrange("p (c d) -> p c d", c=2)
                    chain.link(dve.tensor_tensor(v, v_bank[u][:, 0:D].rearrange("p (c d) -> p c d", c=2),
                                                 bv1[:, :, :].broadcast_to([P, 2, P]), ALU.add))
                    for c in range(2):
                        valid_key = mask_keys[:, ds(b, 1), c]
                        heads = v[:, c, :].rearrange("p (h e) -> p h e", h=HN)
                        chain.mark(dve.tensor_scalar(vn[u][:, c, :, 0:8], heads, valid_key, None, ALU.mult))
                        chain.mark(dve.scalar_tensor_tensor(vn[u][:, c, :, 8:16], heads, valid_key, heads, ALU.mult, ALU.mult))
                        ins = dve.tensor_scalar(vn[u][:, c, :, 16], ones[:, :], valid_key, None, ALU.mult)
                        if c:
                            ins.then_inc(s.v_ready, 1)
                        else:
                            chain.mark(ins)
                narrow_attention(a1, i, chain, None, lambda w, sums: take_heads(chain, w, sums))
                for u in range(SLOTS):
                    b = SLOTS * i + u
                    dve.wait_ge(s.result, b + 1)
                    chain.mark(dve.tensor_scalar(mean_t[:, ds(b, 1), :].rearrange("p a d -> p (a d)"), q_bank[u][:, 0:D], 1.0, None,
                                                 ALU.mult))
                    dve.tensor_scalar(std_t[:, ds(b, 1), :].rearrange("p a d -> p (a d)"), q_bank[u][:, D:2 * D], 0.0, None,
                                      ALU.max).then_inc(s.x_added, 1)
            assert chain.steps == steps, (chain.steps, steps)
            dve.wait_ge(s.chain, steps * ROUNDS)

            dve.wait_ge(s.x_added, B + SLOTS)
            chain = Chain(dve, std_chain)
            n, mean, var, rstd, shifted, work = (row_sums[:, k, :] for k in range(6))
            scratch = km[0][:, :].rearrange("p (b d) -> p b d", b=B)
            chain.link(dve.tensor_tensor(x[:, :, :], x[:, :, :], mask_rows[:, :, :], ALU.mult))
            chain.mark(dve.tensor_tensor(scratch, x[:, :, :], x[:, :, :], ALU.mult))
            chain.link(dve.tensor_reduce(mean, x[:, :, :], X_AXIS, ALU.add))
            chain.mark(dve.tensor_reduce(var, scratch, X_AXIS, ALU.add))
            chain.link(dve.tensor_tensor(mean, mean, valid[:, :], ALU.mult))
            chain.mark(dve.tensor_tensor(n, mean, mean, ALU.mult))
            chain.link(dve.tensor_tensor(var, var, valid[:, :], ALU.mult))
            chain.link(dve.tensor_tensor(var, var, n, ALU.subtract))
            chain.link(dve.tensor_scalar(var, var, 0.0, None, ALU.max))
            inverse_root(dve, chain, rstd, var, shifted, work)
            for b in range(B):
                chain.mark(dve.tensor_scalar(x[:, b, :], x[:, b, :], mean[:, b:b + 1], rstd[:, b:b + 1], ALU.subtract, ALU.mult))
            chain.join()
            dve.wait_ge(std_ready, 1)
            chain.link(dve.tensor_tensor(x[:, :, :], x[:, :, :], std_t[:, :, :], ALU.mult))
            chain.link(dve.tensor_tensor(x[:, :, :], x[:, :, :], mean_t[:, :, :], ALU.add))
            chain.link(dve.tensor_tensor(x[:, :, :], x[:, :, :], mask_rows[:, :, :], ALU.mult))

        def layer2(a, cross):
            s = a.s
            if not cross:
                chain = Chain(dve, s.setup)
                for u in range(SLOTS):
                    chain.mark(dve.memset(vn[u][:, 0, :, 16], 1.0))
                chain.join()

            def take_heads(w, sums):
                weighted(w, heads_out[w][:, :], sums[:, :, 0:16]).then_inc(s.heads_taken, 1)

            steps = NORM_TWO + 1 + SLOTS * (1 + int(cross)) + a.per_round * 2 + a.all_units
            with dve.Fori(0, ROUNDS) as i:
                r = i + ROUNDS * int(cross)
                chain = Chain(dve, s.cross_chain if cross else s.chain, steps * i)
                norm_two(chain, i, s.rows_normed)
                dve.wait_ge(s.rows_normed, SLOTS * (r + 1))
                add_row_bias(chain, i, 3 + int(cross))
                for u in range(SLOTS):
                    if cross:
                        dve.wait_ge((s.loaded0, s.loaded1)[u], 32 * (i + 1))
                        chain.mark(dve.tensor_scalar(cross_mask[u][:, 1, :], cross_mask[u][:, 0, :], NEG_BIG, -NEG_BIG,
                                                     ALU.mult, ALU.add))
                    dve.wait_ge(s.k_ready, SLOTS * r + u + 1)
                    for c in range(DC):
                        ins = dve.tensor_tensor(km[u][:, c * 8 * P:(c + 1) * 8 * P].rearrange("p (h k) -> p h k", h=8),
                                                spread_over(kn[u][:, c * P:(c + 1) * P], [P, 8, P], 1),
                                                spread_over(head_of_16[:, :], [P, 8, P], 2), ALU.mult)
                        if c:
                            ins.then_inc(s.spread, 1)
                        else:
                            chain.mark(ins)
                    dve.wait_ge(s.values, SLOTS * r + u + 1)
                    dve.tensor_tensor(vn[u][:, 0, :, 0:16], v_bank[u][:, 0:D].rearrange("p (h e) -> p h e", h=HN),
                                      b_v2[:, int(cross), :].rearrange("p (h e) -> p h e", h=HN), ALU.add).then_inc(s.v_ready, 1)
                chain.join()
                narrow_attention(a, r, chain, (lambda u: cross_mask[u]) if cross else (lambda u: self_mask), take_heads)
                for u in range(SLOTS):
                    dve.wait_ge(s.result, SLOTS * r + u + 1)
                    row = x[:, ds(SLOTS * i + u, 1), :].rearrange("p a d -> p (a d)")
                    dve.tensor_tensor(row, row, q_bank[u][:, D:2 * D], ALU.add).then_inc(s.x_added, 1)
            assert chain.steps == steps, (chain.steps, steps)
            dve.wait_ge(s.x_added, B * (1 + int(cross)))

        def norm_columns(chain, tiles, outs, sem_ready):
            row_statistics(dve, chain, tiles, stats, idle)
            for k, (tile, target) in enumerate(zip(tiles, outs)):
                ins = dve.tensor_scalar(target, tile, stats.mean_var[:, k, 0:1], stats.rstd[:, k:k + 1], ALU.subtract, ALU.mult)
                if k < len(tiles) - 1:
                    chain.mark(ins)
            ins.then_inc(sem_ready, 1)
            chain.join()

        def layer3():
            s = n3
            chain = Chain(dve, s.setup)
            for u in range(SLOTS):
                chain.mark(dve.memset(vn[u][:, :, :, 8], 1.0))
            chain.join()

            def take_heads(w, sums):
                weighted(w, heads_out[w][:, 0:P], sums[:, :, 0:8]).then_inc(s.heads_taken, 1)

            steps = SLOTS * (1 + statistics_steps(4) + 3) + a3.all_units
            with dve.Fori(0, ROUNDS) as i:
                chain = Chain(dve, s.chain, steps * i)
                for u in range(SLOTS):
                    b = SLOTS * i + u
                    chain.mark(dve.tensor_tensor(placed[u][:, 0, :], x[:, ds(b, 1), :].rearrange("p a d -> p (a d)"), positions[:, :],
                                                 ALU.add))
                    dve.wait_ge((s.loaded0, s.loaded1)[u], 16 * (i + 1))
                    dve.tensor_tensor(placed[u][:, 1, :], cn[u][:, :], positions[:, :], ALU.add).then_inc(s.ctx_ready, 1)
                for u in range(SLOTS):
                    dve.wait_ge(s.turned, SLOTS * i + u + 1)
                    norm_columns(chain, [q_bank[u][:, k * P:(k + 1) * P] for k in range(4)],
                                 [norm3[u][:, k // 2, k % 2 * P:(k % 2 + 1) * P] for k in range(4)], s.rows_normed)
                    dve.wait_ge(s.rows_normed, SLOTS * i + u + 1)
                for u in range(SLOTS):
                    dve.wait_ge(s.k_ready, SLOTS * i + u + 1)
                    dve.tensor_tensor(km[u][:, :].rearrange("p (h k) -> p h k", h=HN), spread_over(kn[u][:, :], [P, HN, D], 1),
                                      spread_over(head_of_8[:, :], [P, HN, D], 2), ALU.mult).then_inc(s.spread, 1)
                    dve.wait_ge(s.values, SLOTS * i + u + 1)
                    dve.tensor_copy(vn[u][:, :, :, 0:8], v_bank[u][:, 0:D].rearrange("p (c h e) -> p c h e", c=2, h=HN))\
                       .then_inc(s.v_ready, 1)
                narrow_attention(a3, i, chain, None, take_heads)
                for u in range(SLOTS):
                    dve.wait_ge(s.result, SLOTS * i + u + 1)
                    dve.tensor_tensor(x[:, ds(SLOTS * i + u, 1), :].rearrange("p a d -> p (a d)"), q_bank[u][:, D:2 * D],
                                      ln_t3[u][:, 0, :], ALU.add).then_inc(s.x_added, 1)
            assert chain.steps == steps, (chain.steps, steps)
            dve.wait_ge(s.x_added, B)

        def feed_forward3():
            s = ff3
            steps = SLOTS * (statistics_steps(2) + 1)
            with dve.Fori(0, ROUNDS) as i:
                chain = Chain(dve, s.chain, steps * i)
                for u in range(SLOTS):
                    dve.tensor_scalar(placed[u][:, 0, :], x[:, ds(SLOTS * i + u, 1), :].rearrange("p a d -> p (a d)"), 1.0, None,
                                      ALU.mult).then_inc(s.x_copied, 1)
                for u in range(SLOTS):
                    dve.wait_ge(s.turned, SLOTS * i + u + 1)
                    norm_columns(chain, [bank[u][:, k * P:(k + 1) * P] for k in range(2)],
                                 [norm3[u][:, 0, k * P:(k + 1) * P] for k in range(2)], s.rows_normed)
                    dve.wait_ge(s.rows_normed, SLOTS * i + u + 1)
                for u in range(SLOTS):
                    dve.wait_ge(s.down_ready, SLOTS * i + u + 1)
                    dve.wait_ge(out_stored[u], 16 * (i + 1))
                    dve.scalar_tensor_tensor(result[u][:, :], bank[6 + u][:, 0:D], b3_down[:, 0:1], placed[u][:, 0, :],
                                             ALU.add, ALU.add).then_inc(result_ready, 1)
                dve.wait_ge(result_ready, SLOTS * (i + 1))
            assert chain.steps == steps, (chain.steps, steps)

        dve.sem_inc(x_added, ADD_CREDIT)
        dve.sem_inc(heads_split, GROUP)
        split_context()
        dve.wait_ge(x_loaded, 16 * GROUPS)
        dve.wait_ge(small_loaded, small_count)
        for layer in range(2):
            norm_and_split(layer)
            pairs(layer)
        feed_forward(0, 2)
        layer1()
        layer2(a2s, False)
        layer2(a2c, True)
        feed_forward(2, 5)
        layer3()
        feed_forward3()

    @block.gpsimd
    def _(pool):
        def copy(target, source):
            source, target = (a.rearrange("p a b -> p (a b)") if len(a.shape) == 3 else a for a in (source, target))
            return pool.tensor_tensor(target, source, zero[:, :].broadcast_to([P, source.shape[1]]), ALU.add)

        chain = Chain(pool, ident_ready)
        chain.link(pool.memset(zero[:, :], 0.0))
        chain.link(pool.memset(ident[:, :], 0.0))
        chain.link(pool.affine_select(out=ident[:, :], in_=ident[:, :], compare_op=ALU.not_equal, fill=1.0, base=0,
                                      pattern=[[-1, P]], channel_multiplier=1))
        pool.sem_inc(weights_split, 1)
        steps = 9
        for layer in range(2):
            with pool.Fori(0, PAIRS // 2) as i:
                for slot in range(2):
                    p = PAIRS * layer + 2 * i + slot
                    chain = Chain(pool, split_steps, steps * p)
                    wh, wl = weights_high[slot], weights_low[slot]
                    pool.wait_ge(pair_loaded, 16 * PAIR_LOADS * (p + 1))
                    pool.wait_ge(x_added, 8 * (p - 1) + ADD_CREDIT)
                    chain.mark(copy(columns[slot][:, :, :], pair_columns[:, :, :]))
                    for kind in range(4):
                        chain.link(copy(wh[:, kind, :], pair_weights[:, kind, :]))
                        chain.mark(pool.tensor_tensor(wl[:, kind, :], pair_weights[:, kind, :], wh[:, kind, :].bitcast(F32),
                                                      ALU.subtract))
                    chain.join()
                    pool.tensor_tensor(value_bias[slot][:, 0, :], pair_rows[:, 0, :], pair_rows[:, 1, :], ALU.subtract)\
                        .then_inc(weights_split, 1)
        pool.wait_ge(x_added, 8 * 2 * PAIRS + ADD_CREDIT)
        for size, target in ((8, head_of_8), (16, head_of_16)):
            n = P // size
            chain = Chain(pool, head_steps, 3 * (size // 16))
            chain.link(pool.memset(target[:, :], 1.0))
            chain.link(pool.affine_select(out=target[:, :], in_=target[:, :], compare_op=ALU.is_ge, fill=0.0, base=0,
                                          pattern=[[-size, n]], channel_multiplier=1))
            chain.link(pool.affine_select(out=target[:, :], in_=target[:, :], compare_op=ALU.is_ge, fill=0.0, base=size - 1,
                                          pattern=[[size, n]], channel_multiplier=-1))
        pool.sem_inc(heads_known, 3)
    @block.sync
    def _(sp):
        def load_pair(layer, p, q):
            k = str(layer + 1)
            sp.wait_ge(weights_split, p + 1)
            cols = ds(q * D, D)
            for m, name in enumerate("qkv"):
                sp.dma_start(pair_weights[:, m, :].rearrange("p (c n) -> p c n", c=DC),
                             rows(f"L0_xattn_w{name}{k}")[:, :, cols]).then_inc(pair_loaded, 16)
            sp.dma_start(pair_weights[:, 3, :].rearrange("p (h n) -> p h n", h=2),
                         rows(f"L0_xattn_wo{k}")[:, ds(q * 2, 2), :]).then_inc(pair_loaded, 16)
            for m, name in enumerate(("bq", "bk")):
                sp.dma_start(pair_columns[:, m, :], column(f"L0_xattn_{name}{k}")[:, ds(q * 2, 2)],
                             allow_slow_non_contiguous=True).then_inc(pair_loaded, 16)
            for m, name in enumerate(("bias_k", "bias_v")):
                sp.dma_start(pair_columns[:, 2 + m, :], t[f"L0_xattn_{name}{k}"].rearrange("a b h k -> k (a b h)")[:, ds(q * 2, 2)],
                             allow_slow_non_contiguous=True)\
                  .then_inc(pair_loaded, 16)
            sp.dma_start(pair_rows[:, 0, :], t[f"L0_xattn_bv{k}"][cols].partition_broadcast(P)).then_inc(pair_loaded, 16)
            sp.dma_start(pair_rows[:, 1, :], t[f"L0_xattn_bias_v{k}"].rearrange("a b h k -> (a b h k)")[cols].partition_broadcast(P))\
              .then_inc(pair_loaded, 16)

        ctx = t["ctx_2048"]
        for u in range(SLOTS):
            sp.sem_inc(out_stored[u], 16)
        for g in range(2):
            sp.dma_start(ctx_rows[:, g, :, :], ctx[GROUP * g:GROUP * (g + 1)].rearrange("b p d -> p b d")).then_inc(rows_loaded[g], 16)
        for g in range(GROUPS):
            part = slice(GROUP * g, GROUP * (g + 1))
            sp.dma_start(x[:, part, :], t["x"][part].rearrange("b p d -> p b d")).then_inc(x_loaded, 16)
        for target, source in small_loads:
            sp.dma_start(target, source, allow_slow_non_contiguous=True).then_inc(small_loaded, 16)
        for g in range(2, GROUPS):
            sp.wait_ge(rows_turned, DC * (g - 1))
            sp.dma_start(ctx_rows[:, g % 2, :, :], ctx[GROUP * g:GROUP * (g + 1)].rearrange("b p d -> p b d"))\
              .then_inc(rows_loaded[g % 2], 16)
        for layer in range(2):
            with sp.Fori(0, PAIRS) as q:
                load_pair(layer, PAIRS * layer + q, q)
            if layer == 0:
                sp.dma_start(w_up[:, :, :], rows("L0_xattn_w_fc1")).then_inc(weights0_loaded, 16)
                sp.dma_start(w_down[:, :, :], rows("L0_xattn_w_fc2")).then_inc(weights0_loaded, 16)

        sp.wait_ge(x_added, 8 * 2 * PAIRS + ADD_CREDIT)
        sp.wait_ge(weights_split, 2 * PAIRS + 1)
        for target, source in later_loads:
            sp.dma_start(target, source, allow_slow_non_contiguous=True).then_inc(later_loaded, 16)

        def load_rows(s, u, i, mask):
            b = SLOTS * i + u
            sem = (s.loaded0, s.loaded1)[u]
            sp.dma_start(cn[u][:, :], ctx[ds(b, 1)].rearrange("a p d -> p (a d)")).then_inc(sem, 16)
            if mask:
                sp.dma_start(cross_mask[u][:, 0, :], t["mask_Bx1xSxS2_ff1"][ds(b, 1)].rearrange("b a q k -> q (b a k)"))\
                  .then_inc(sem, 16)

        def load_contexts(s, mask, free, before=0):
            for u in range(SLOTS):
                load_rows(s, u, 0, mask)
            with sp.Fori(1, ROUNDS) as i:
                for u in range(SLOTS):
                    sp.wait_ge(free, before + SLOTS * (i - 1) + u + 1)
                    load_rows(s, u, i, mask)

        load_contexts(n1, False, n1.values)
        sp.dma_start(w_up[:, :, :], rows("L2_xattn_w1")).then_inc(weights2_loaded, 16)
        sp.dma_start(w_down[:, :, :], rows("L2_xattn_w2")).then_inc(weights2_loaded, 16)
        sp.wait_ge(n1.values, B)
        load_contexts(n2, True, n2.x_added, B)
        sp.wait_ge(n2.x_added, 2 * B)
        load_contexts(n3, False, n3.ctx_ready)
        with sp.Fori(0, ROUNDS) as i:
            for u in range(SLOTS):
                b = SLOTS * i + u
                sp.wait_ge(result_ready, b + 1)
                sp.dma_start(out[ds(b, 1)].rearrange("a p d -> p (a d)"), result[u][:, :]).then_inc(out_stored[u], 16)
        for u in range(SLOTS):
            sp.wait_ge(out_stored[u], 16 * (ROUNDS + 1))


def position_code():
    pos = np.arange(D, dtype=np.float32)[:, None]
    div = np.exp(np.arange(0, P, 2, dtype=np.float32) * np.float32(-np.log(10000.0) / P)).astype(np.float32)
    angle = (pos * div).astype(np.float32)
    code = np.zeros((D, P), np.float32)
    code[:, 0::2] = np.sin(angle)
    code[:, 1::2] = np.cos(angle)
    return np.ascontiguousarray(code.T)


def kernel(**inputs):
    import concourse.bacc as bacc
    from concourse.bass_utils import run_bass_kernel_spmd as run

    nc = bacc.Bacc("TRN2", target_bir_lowering=False, num_devices=1)
    arrays, tensors = {}, {}
    for name, value in inputs.items():
        a = np.ascontiguousarray(value)
        if a.dtype == np.bool_:
            a = a.view(np.uint8)
        arrays[f"in_{name}"] = a
        tensors[name] = nc.dram_tensor(f"in_{name}", a.shape, mybir.dt.from_np(a.dtype), kind="ExternalInput").ap()
    arrays["in_positions"] = position_code()
    tensors["positions"] = nc.dram_tensor("in_positions", (P, D), F32, kind="ExternalInput").ap()
    out = nc.dram_tensor("out", (B, P, D), F32, kind="ExternalOutput").ap()
    build(nc, tensors, out)
    return run(nc, [arrays], core_ids=[0]).results[0]["out"]
```

```python
from contextlib import ExitStack

import numpy as np

import concourse.bass as bass
from concourse import mybir
from concourse.alu_op_type import AluOpType as ALU

F32 = mybir.dt.float32
F32R = mybir.dt.float32r
I32 = mybir.dt.int32
U8 = mybir.dt.uint8
ACT = mybir.ActivationFunctionType
X_AXIS = mybir.AxisListType.X

P = 128
B = 16
D = 256
DC = D // P
EPS = 1e-5
BANK = 512

H0 = 16
PAIRS = H0 // 2
GROUP = 4
GROUPS = B // GROUP
TOK = GROUP * P
KEYS0 = P + 1
F0 = 1024
SCALE0 = 1.0 / float(np.sqrt(np.float32(P)))
ADD_CREDIT = 9
PAIR_LOADS = 10

SLOTS = 2
ROUNDS = B // SLOTS
HN = 16
NEG_BIG = 10000.0
SCALE1 = float(np.float32(1.0 / np.sqrt(8.0)))
SCALE2 = 0.25
PACK = 4
PACKS = HN // PACK
QUAD = P // PACK
UNITS = D // P


ds = bass.ds


class Statistics:

    def __init__(self, sums, mean_var, rstd, shifted, work):
        self.sums, self.mean_var, self.rstd, self.shifted, self.work = sums, mean_var, rstd, shifted, work


class FeedForward:

    def __init__(self, sem):
        self.chain = sem("ff_chain")
        self.rows_normed = sem("ff_rows_normed")
        self.turned = sem("ff_turned")
        self.in_ready = sem("ff_in_ready")
        self.up_ready = sem("ff_up_ready")
        self.hidden_ready = sem("ff_hidden_ready")
        self.down_ready = sem("ff_down_ready")
        self.x_added = sem("ff_x_added")


class FeedForward3:

    def __init__(self, sem):
        self.chain = sem("ff3_chain")
        self.x_copied = sem("ff3_x_copied")
        self.turned = sem("ff3_turned")
        self.rows_normed = sem("ff3_rows_normed")
        self.turned_back = sem("ff3_turned_back")
        self.in_ready = sem("ff3_in_ready")
        self.up_ready = sem("ff3_up_ready")
        self.hidden_ready = sem("ff3_hidden_ready")
        self.down_ready = sem("ff3_down_ready")


class Narrow:

    def __init__(self, sem, name, loads, around):
        self.chain = sem(f"{name}_chain")
        self.projected = sem(f"{name}_projected")
        self.values = sem(f"{name}_values")
        self.q_ready = sem(f"{name}_q_ready")
        self.k_ready = sem(f"{name}_k_ready")
        self.spread = sem(f"{name}_spread")
        self.v_ready = sem(f"{name}_v_ready")
        self.scores = sem(f"{name}_scores")
        self.max_ready = sem(f"{name}_max_ready")
        self.exp_ready = sem(f"{name}_exp_ready")
        self.probs_turned = sem(f"{name}_probs_turned")
        self.probs_copied = sem(f"{name}_probs_copied")
        self.heads = sem(f"{name}_heads")
        self.heads_taken = sem(f"{name}_heads_taken")
        self.result = sem(f"{name}_result")
        self.x_added = sem(f"{name}_x_added")
        if loads:
            self.loaded0 = sem(f"{name}_loaded0")
            self.loaded1 = sem(f"{name}_loaded1")
        if around:
            self.setup = sem(f"{name}_setup")
            self.rows_normed = sem(f"{name}_rows_normed")
            self.turned = sem(f"{name}_turned")
            self.in_ready = sem(f"{name}_in_ready")
            self.heads_turned = sem(f"{name}_heads_turned")
            self.heads_copied = sem(f"{name}_heads_copied")


class Packed:

    def __init__(self, sem, name):
        self.prep_chain = sem(f"{name}_prep_chain")
        self.values_chain = sem(f"{name}_values_chain")
        self.heads_chain = sem(f"{name}_heads_chain")
        self.loaded0 = sem(f"{name}_loaded0")
        self.loaded1 = sem(f"{name}_loaded1")
        self.in_ready = sem(f"{name}_in_ready")
        self.q_projected = sem(f"{name}_q_projected")
        self.k_projected = sem(f"{name}_k_projected")
        self.v_projected = sem(f"{name}_v_projected")
        self.q_high = sem(f"{name}_q_high")
        self.k_high = sem(f"{name}_k_high")
        self.q_low = sem(f"{name}_q_low")
        self.k_low = sem(f"{name}_k_low")
        self.spread = sem(f"{name}_spread")
        self.v_ready = sem(f"{name}_v_ready")
        self.scores = sem(f"{name}_scores")
        self.max_ready = sem(f"{name}_max_ready")
        self.exp_ready = sem(f"{name}_exp_ready")
        self.probs_turned = sem(f"{name}_probs_turned")
        self.probs_copied = sem(f"{name}_probs_copied")
        self.sums = sem(f"{name}_sums")
        self.sums_copied = sem(f"{name}_sums_copied")
        self.sums_turned = sem(f"{name}_sums_turned")
        self.heads_taken = sem(f"{name}_heads_taken")
        self.result = sem(f"{name}_result")
        self.x_added = sem(f"{name}_x_added")


class Attention:

    def __init__(self, sems, units, heads, keys, width, mask):
        self.s, self.units, self.heads, self.keys, self.width, self.mask = sems, units, heads, keys, width, mask
        self.blocks = keys // P
        self.steps = HN // heads
        self.per_slot = units * self.steps
        self.per_round = SLOTS * self.per_slot
        self.all_units = SLOTS * units


class Chain:

    def __init__(self, engine, sem, base=0):
        self.engine, self.sem, self.base, self.steps = engine, sem, base, 0

    def mark(self, instruction):
        self.steps += 1
        instruction.then_inc(self.sem, 1)

    def join(self):
        self.engine.wait_ge(self.sem, self.base + self.steps)

    def link(self, instruction):
        self.mark(instruction)
        self.join()


def inverse_root(dve, chain, out, var, shifted, work):
    chain.link(dve.tensor_scalar(shifted, var, EPS, None, ALU.add))
    chain.link(dve.tensor_scalar(out.bitcast(I32), shifted.bitcast(I32), -0.5, 1597463007.0,
                                 ALU.mult, ALU.add))
    for _ in range(3):
        chain.link(dve.scalar_tensor_tensor(work, out, -0.5, out, ALU.mult, ALU.mult))
        chain.link(dve.tensor_tensor(work, work, shifted, ALU.mult))
        chain.link(dve.scalar_tensor_tensor(out, work, 1.5, out, ALU.add, ALU.mult))


def row_statistics(dve, chain, rows, stats, idle):
    n = len(rows)
    for k, row in enumerate(rows):
        chain.mark(dve.bn_stats(stats.sums[:, k, :], row))
    chain.join()
    dve.sem_inc(idle, 1)
    for k in range(n):
        chain.mark(dve.bn_aggr(stats.mean_var[:, k, :], stats.sums[:, k, :]))
    chain.join()
    inverse_root(dve, chain, stats.rstd[:, 0:n], stats.mean_var[:, 0:n, 1], stats.shifted[:, 0:n],
                 stats.work[:, 0:n])


def statistics_steps(n):
    return 2 * n + 11


def pair_number(layer, pair, k):
    return PAIRS * layer + pair + k // GROUPS


def over_groups(engine, window):
    window(-1, -1, 0, False, False, True)
    window(0, 0, 0, True, False, True)
    span = 2 * GROUPS
    with engine.Fori(0, PAIRS // 2 - 1) as i:
        for k in range(1, span + 1):
            window(span * i + k, k, 2 * i, True, True, True)
    last = PAIRS * GROUPS
    for k in range(1, span):
        window(last - span + k, k, PAIRS - 2, True, True, k + 1 < span)
    window(last, span, PAIRS - 2, False, True, False)


def over_windows(engine, window):
    window(-1, 1, False, False, True, 0)
    window(0, 0, True, False, True, 0)
    with engine.Fori(0, B // SLOTS - 1) as i:
        window(SLOTS * i + 1, 1, True, True, True, i + 1)
        window(SLOTS * i + 2, 0, True, True, True, i + 1)
    window(B - 1, 1, True, True, False, 0)
    window(B, 0, False, True, False, 0)


def build(nc, t, out):
    with ExitStack() as outer:
        program(nc, t, out, outer)


def program(nc, t, out, outer):
    def sem(name):
        return outer.enter_context(nc.semaphore(name))

    def sbuf(scope, name, shape, dtype=F32):
        return scope.enter_context(nc.sbuf_tensor(name, shape, dtype))

    bank = [outer.enter_context(nc.psum_tensor(f"bank{k}", [P, BANK], F32)) for k in range(8)]

    x = sbuf(outer, "x", [P, B, D])
    zero = sbuf(outer, "zero", [P, 1])
    ident = sbuf(outer, "ident", [P, P])
    norm_rows = sbuf(outer, "norm_rows", [P, SLOTS, D])
    stats = Statistics(
        sums=sbuf(outer, "stat_sums", [P, 4, 6]), mean_var=sbuf(outer, "mean_var", [P, 4, 2]),
        rstd=sbuf(outer, "rstd", [P, 4]), shifted=sbuf(outer, "stat_shifted", [P, 4]),
        work=sbuf(outer, "stat_work", [P, 4]))
    norms = ["L0_xattn_ln1", "L0_xattn_ln2", "L0_xattn_ln_mlp", "L2_xattn_ln1", "L2_xattn_ln2", "L2_xattn_ln3"]
    norm_scale = sbuf(outer, "norm_scale", [P, len(norms), DC])
    norm_offset = sbuf(outer, "norm_offset", [P, len(norms), DC])
    row_biases = ["L0_xattn_bo1", "L0_xattn_bo2", "L0_xattn_b_fc2", "L2_xattn_b_ao", "L2_xattn_b_co", "L2_xattn_b2"]
    row_bias = sbuf(outer, "row_bias", [P, len(row_biases), D])
    w_up = sbuf(outer, "w_up", [P, DC, F0])
    w_down = sbuf(outer, "w_down", [P, F0 // P, D])
    b_up = sbuf(outer, "b_up", [P, 2, F0 // P])
    hidden_in = sbuf(outer, "hidden_in", [P, DC, SLOTS * P])
    hidden = sbuf(outer, "hidden", [P, F0 // P, SLOTS * P])

    with ExitStack() as scope0:
        normed_high = sbuf(scope0, "wide_normed_high", [P, DC, B * P], F32R)
        normed_low = sbuf(scope0, "wide_normed_low", [P, DC, B * P], F32R)
        ctx_high = sbuf(scope0, "wide_ctx_high", [P, DC, B * P], F32R)
        ctx_low = sbuf(scope0, "wide_ctx_low", [P, DC, B * P], F32R)
        normed = sbuf(scope0, "wide_normed", [P, DC, SLOTS * P])
        pair_weights = sbuf(scope0, "wide_pair_weights", [P, 4, DC * D])
        pair_columns = sbuf(scope0, "wide_pair_columns", [P, 4, 2])
        pair_rows = sbuf(scope0, "wide_pair_rows", [P, 2, D])
        weights_high = [sbuf(scope0, f"wide_weights_high{k}", [P, 4, DC * D], F32R) for k in range(2)]
        weights_low = [sbuf(scope0, f"wide_weights_low{k}", [P, 4, DC * D], F32R) for k in range(2)]
        columns = [sbuf(scope0, f"wide_columns{k}", [P, 4, 2]) for k in range(2)]
        value_bias = [sbuf(scope0, f"wide_value_bias{k}", [P, 1, D]) for k in range(2)]
        q0 = [sbuf(scope0, f"wide_q0{k}", [P, 2, TOK]) for k in range(2)]
        k0 = [sbuf(scope0, f"wide_k0{k}", [P, 2, GROUP, KEYS0]) for k in range(2)]
        v0 = [sbuf(scope0, f"wide_v0{k}", [P, GROUP, D]) for k in range(2)]
        neg_max0 = sbuf(scope0, "wide_neg_max0", [P, GROUP, 2])
        sums0 = sbuf(scope0, "wide_sums0", [P, GROUP, 2])
        inverse0 = sbuf(scope0, "wide_inverse0", [P, GROUP, 2])
        probs0 = sbuf(scope0, "wide_probs0", [P, GROUP, 2, KEYS0])
        probs_t0 = sbuf(scope0, "wide_probs_t0", [P, GROUP, 2, P])
        with ExitStack() as scope_rows:
            ctx_rows = sbuf(scope_rows, "wide_ctx_rows", [P, 2, GROUP, D])
        heads_high = sbuf(scope0, "wide_heads_high", [P, 2, GROUP, P], F32R)
        heads_low = sbuf(scope0, "wide_heads_low", [P, 2, GROUP, P], F32R)

    with ExitStack() as scope1:
        head_of_8 = sbuf(scope1, "head_of_8", [P, HN])
        head_of_16 = sbuf(scope1, "head_of_16", [P, HN // 2])
        vn = [sbuf(scope1, f"vn{u}", [P, UNITS, HN, QUAD]) for u in range(SLOTS)]
        cn = [sbuf(scope1, f"cn{u}", [P, D]) for u in range(SLOTS)]
        neg_max = [sbuf(scope1, f"neg_max{k}", [P, 4]) for k in range(2)]
        probs = [sbuf(scope1, f"probs{k}", [P, BANK]) for k in range(2)]
        probs_t = [sbuf(scope1, f"probs_t{k}", [P, BANK]) for k in range(8)]
        ones = sbuf(scope1, "ones", [P, HN])
        inverse = sbuf(scope1, "inverse", [P, 2, HN])
        heads_out = [sbuf(scope1, f"heads_out{k}", [P, D]) for k in range(2)]
        heads_t = [sbuf(scope1, f"heads_t{u}", [P, D]) for u in range(SLOTS)]
        part_of_head = sbuf(scope1, "part_of_head", [P, PACK])
        wq_packed = sbuf(scope1, "wq_packed", [P, PACKS, PACK, QUAD])
        wk_packed = sbuf(scope1, "wk_packed", [P, PACKS, PACK, QUAD])
        q_packed = [sbuf(scope1, f"q_packed{u}", [P, PACKS, D], F32R) for u in range(SLOTS)]
        k_packed = [sbuf(scope1, f"k_packed{u}", [P, PACKS, D], F32R) for u in range(SLOTS)]
        keys_in = sbuf(scope1, "keys_in", [P, D])
        sums_copy = sbuf(scope1, "sums_copy", [P, PACKS, D])
        wv1 = sbuf(scope1, "wv1", [P, P])
        bias1 = sbuf(scope1, "bias1", [P, 2, PACKS])
        bq1 = sbuf(scope1, "bq1", [P, PACKS])
        bv1 = sbuf(scope1, "bv1", [P, 1, P])
        mask_keys = sbuf(scope1, "mask_keys", [P, B, 2])
        valid = sbuf(scope1, "valid", [P, B])
        key_mean = sbuf(scope1, "key_mean", [P, 1])
        scratch1 = sbuf(scope1, "scratch1", [P, D])
        row_sums = sbuf(scope1, "row_sums", [P, 6, B])
        b_qk2 = sbuf(scope1, "b_qk2", [P, 2, 2, DC])
        b_q2 = sbuf(scope1, "b_q2", [P, 2, DC])
        b_v2 = sbuf(scope1, "b_v2", [P, 2, D])
        self_mask = sbuf(scope1, "self_mask", [P, 2, P])
        positions = sbuf(scope1, "positions", [P, D])
        w3 = sbuf(scope1, "w3", [P, 4, P])
        ln3 = sbuf(scope1, "ln3", [P, 6])
        w3_up = sbuf(scope1, "w3_up", [P, D])
        w3_down = sbuf(scope1, "w3_down", [P, 2, P])
        b3_up = sbuf(scope1, "b3_up", [P, 2])
        b3_down = sbuf(scope1, "b3_down", [P, 1])
        with ExitStack() as scope_raw:
            w_rows1 = sbuf(scope_raw, "w_rows1", [P, 3, P])
            mask_own_bytes = sbuf(scope_raw, "mask_own_bytes", [B, D], U8)
            mask_own = sbuf(scope_raw, "mask_own", [B, D])
            mask_bytes = sbuf(scope_raw, "mask_bytes", [P, B, D], U8)
        with ExitStack() as scope_l2:
            w_qkv = sbuf(scope_l2, "w_qkv", [P, 2, DC, 3 * D])
            w_out2 = sbuf(scope_l2, "w_out2", [P, 2, DC, D])
            km = [sbuf(scope_l2, f"km{u}", [P, HN * P]) for u in range(SLOTS)]
        with ExitStack() as scope_spread:
            q_spread = [sbuf(scope_spread, f"q_spread{u}", [P, HN, D], F32R) for u in range(SLOTS)]
            with ExitStack() as scope_early:
                mask_rows = sbuf(scope_early, "mask_rows", [P, B, D])
                mean_t = sbuf(scope_early, "mean_t", [P, B, D])
                std_t = sbuf(scope_early, "std_t", [P, B, D])
            with ExitStack() as scope_late:
                qn = [sbuf(scope_late, f"qn{u}", [P, D]) for u in range(SLOTS)]
                kn = [sbuf(scope_late, f"kn{u}", [P, D]) for u in range(SLOTS)]
                rows_t = [sbuf(scope_late, f"rows_t{u}", [P, DC, P]) for u in range(SLOTS)]
                cn_t = [sbuf(scope_late, f"cn_t{u}", [P, DC, P]) for u in range(SLOTS)]
                cross_mask = [sbuf(scope_late, f"cross_mask{u}", [P, 2, P]) for u in range(SLOTS)]
                scores_masked = [sbuf(scope_late, f"scores_masked{k}", [P, BANK]) for k in range(2)]
                placed = [sbuf(scope_late, f"placed{u}", [P, 2, D]) for u in range(SLOTS)]
                norm3 = [sbuf(scope_late, f"norm3{u}", [P, 2, D]) for u in range(SLOTS)]
                ln_t3 = [sbuf(scope_late, f"ln_t3{u}", [P, 2, D]) for u in range(SLOTS)]
                norm_packed = sbuf(scope_late, "norm_packed", [P, 2, D])
                placed_packed = sbuf(scope_late, "placed_packed", [P, 2, D])
                hidden3 = [sbuf(scope_late, f"hidden3{u}", [P, 2, D]) for u in range(SLOTS)]
                result = [sbuf(scope_late, f"result{u}", [P, D]) for u in range(SLOTS)]

    idle = sem("idle")
    x_loaded = sem("x_loaded")
    small_loaded = sem("small_loaded")
    weights0_loaded = sem("weights0_loaded")
    heads_known = sem("heads_known")
    ident_ready = sem("ident_ready")
    rows_loaded = [sem(f"rows_loaded{k}") for k in range(2)]
    rows_turned = sem("rows_turned")
    ctx_high_ready = sem("ctx_high_ready")
    ctx_low_ready = sem("ctx_low_ready")
    split_chain = sem("split_chain")
    rows_normed = sem("rows_normed")
    normed_turned = sem("normed_turned")
    normed_ready = sem("normed_ready")
    normed_high_ready = sem("normed_high_ready")
    normed_low_ready = sem("normed_low_ready")
    pair_loaded = sem("pair_loaded")
    split_steps = sem("split_steps")
    weights_split = sem("weights_split")
    qk_ready = sem("qk_ready")
    q_copied = sem("q_copied")
    k_copied = sem("k_copied")
    scores_ready = sem("scores_ready")
    v_ready = sem("v_ready")
    v_copied = sem("v_copied")
    max_ready = sem("max_ready")
    exp_ready = sem("exp_ready")
    softmax_chain = sem("softmax_chain")
    probs_ready = sem("probs_ready")
    probs_turned = sem("probs_turned")
    probs_copied = sem("probs_copied")
    heads_ready = sem("heads_ready")
    heads_high_ready = sem("heads_high_ready")
    heads_split = sem("heads_split")
    out_ready = sem("out_ready")
    x_added = sem("x_added")

    later_loaded = sem("later_loaded")
    weights2_loaded = sem("weights2_loaded")
    attention2_loaded = sem("attention2_loaded")
    masks_ready = sem("masks_ready")
    masks_turned = sem("masks_turned")
    head_steps = sem("head_steps")
    masks_chain = sem("masks_chain")
    std_chain = sem("std_chain")
    std_ready = sem("std_ready")
    out_stored = [sem(f"out_stored{u}") for u in range(SLOTS)]
    result_ready = sem("result_ready")
    ff = FeedForward(sem)
    ff3 = FeedForward3(sem)
    n1 = Packed(sem, "n1")
    n2 = Narrow(sem, "n2", True, True)
    n2.cross_chain = sem("n2_cross_chain")
    n3 = Packed(sem, "n3")
    n3.placed = sem("n3_placed")
    n3.turned = sem("n3_turned")
    n3.rows_normed = sem("n3_rows_normed")
    n3.turned_back = sem("n3_turned_back")
    n3.heads_turned = sem("n3_heads_turned")
    n3.heads_copied = sem("n3_heads_copied")
    packed_ready = sem("packed_ready")

    a2s = Attention(n2, units=1, heads=4, keys=P, width=17, mask=True)
    a2c = Attention(n2, units=1, heads=4, keys=P, width=17, mask=True)
    q_bank = [bank[6], bank[7]]
    v_bank = [bank[4], bank[5]]
    score_bank = [bank[0], bank[1]]
    turn_bank = [bank[2], bank[3]]
    project_bank = [bank[0], bank[1]]
    wide_scores = [bank[2], bank[3]]
    wide_heads = [bank[4], bank[5]]
    wide_turned = bank[6]
    out_bank = bank[7]
    sum_bank = bank[4]
    aux = [bank[5], bank[6], bank[7]]


    def column(name):
        return t[name].rearrange("(c p) -> p c", p=P)

    small_loads = []
    for k, name in enumerate(norms):
        part = ("_scale", "_offset") if name.startswith("L0") else ("_s", "_b")
        small_loads += [(norm_scale[:, k, :], column(name + part[0])), (norm_offset[:, k, :], column(name + part[1]))]
    for k, name in enumerate(row_biases):
        small_loads.append((row_bias[:, k, :], t[name].partition_broadcast(P)))
    small_loads += [(b_up[:, 0, :], column("L0_xattn_b_fc1")), (b_up[:, 1, :], column("L2_xattn_b1"))]
    small_count = 16 * len(small_loads)

    def rows(name):
        return t[name].rearrange("(c p) n -> p c n", p=P)

    def row(name):
        return t[name].partition_broadcast(P)

    later_loads = [(w_rows1[:, k, :], t[f"L1_xattn_W{n}"]) for k, n in enumerate("qkv")]
    later_loads += [(bias1[part * QUAD:(part + 1) * QUAD, k, :], t[f"L1_xattn_b{n}"].rearrange("(g r) -> r g", r=QUAD))
                    for k, n in enumerate("qk") for part in range(PACK)]
    later_loads += [
        (bv1[:, 0, :], row("L1_xattn_bv")),
        (mask_own_bytes[:, :], t["mask_Bx1x2048_bf1"].rearrange("b a k -> (b a) k")),
        (mask_bytes[:, :, :].rearrange("p b k -> p (b k)"), t["mask_Bx1x2048_bf1"].rearrange("b a k -> (b a k)").partition_broadcast(P)),
        (b_qk2[:, 0, :, :].rearrange("p a c -> p (a c)"), column("L2_xattn_b_qkv")[:, 0:2 * DC]),
        (b_qk2[:, 1, 0, :], column("L2_xattn_b_q")),
        (b_qk2[:, 1, 1, :], column("L2_xattn_b_kv")[:, 0:DC]),
        (b_v2[:, 0, :], t["L2_xattn_b_qkv"][2 * D:3 * D].partition_broadcast(P)),
        (b_v2[:, 1, :], t["L2_xattn_b_kv"][D:2 * D].partition_broadcast(P)),
        (self_mask[:, 0, :], t["mask_1x1xSxS2_fc1"].rearrange("a b q k -> (a b q) k")),
        (positions[:, :], t["positions"]),
        (w3_up[:, :], t["L3_xattn_W1"]),
        (w3_down[:, :, :], rows("L3_xattn_W2")),
        (b3_up[:, :], column("L3_xattn_b1")),
        (b3_down[:, :], column("L3_xattn_b2")),
    ]
    later_loads += [(w3[:, k, :], t[f"L3_xattn_W{n}"]) for k, n in enumerate("qkvo")]
    later_loads += [(ln3[:, k:k + 1], column(f"L3_xattn_{n}")) for k, n in enumerate(
        ("ln_q_g", "ln_q_b", "ln_kv_g", "ln_kv_b", "ffn_ln_g", "ffn_ln_b"))]
    later_count = 16 * len(later_loads)
    loads2 = [
        (w_qkv[:, 0, :, :], rows("L2_xattn_w_qkv")),
        (w_qkv[:, 1, :, 0:D], rows("L2_xattn_w_q")),
        (w_qkv[:, 1, :, D:3 * D], rows("L2_xattn_w_kv")),
        (w_out2[:, 0, :, :], rows("L2_xattn_w_ao")),
        (w_out2[:, 1, :, :], rows("L2_xattn_w_co")),
    ]
    loads2_count = 16 * len(loads2)


    block = outer.enter_context(nc.Block())

    @block.tensor
    def _(pe):
        def product3(acc, wh, wl, mh, ml, start, stop):
            pe.matmul(acc, wh, mh, start=start, stop=False)
            pe.matmul(acc, wh, ml, start=False, stop=False)
            return pe.matmul(acc, wl, mh, start=False, stop=stop)

        def turn_context():
            pe.wait_ge(ident_ready, 3)
            for g in range(GROUPS):
                pe.wait_ge(rows_loaded[g % 2], 16 * (g // 2 + 1))
                if g >= 2:
                    pe.wait_ge(ctx_low_ready, DC * (g - 1))
                for c in range(DC):
                    for b in range(GROUP):
                        last = pe.transpose(bank[2 * (g % 2) + c][:, b * P:(b + 1) * P],
                                            ctx_rows[:, g % 2, b, c * P:(c + 1) * P], ident[:, :])
                    last.then_inc(rows_turned, 1)

        def turn_normed(layer):
            with pe.Fori(0, ROUNDS) as i:
                r = ROUNDS * layer + i
                pe.wait_ge(rows_normed, SLOTS * (r + 1))
                for c in range(DC):
                    for u in range(SLOTS):
                        last = pe.transpose(bank[4][:, (SLOTS * c + u) * P:(SLOTS * c + u + 1) * P],
                                            norm_rows[:, u, c * P:(c + 1) * P], ident[:, :])
                last.then_inc(normed_turned, 1)

        def pairs(layer):
            pe.wait_ge(normed_low_ready, DC * ROUNDS * (layer + 1))
            if layer == 0:
                pe.wait_ge(ctx_low_ready, DC * GROUPS)

            def project(gg, k, pair, piece):
                kind, half = piece // 2, piece % 2
                slot, n = k // GROUPS % 2, k % GROUPS
                wh, wl = weights_high[slot], weights_low[slot]
                acc = project_bank[half]
                tok = slice(n * TOK, (n + 1) * TOK)
                if piece == 0 and n == 0:
                    pe.wait_ge(weights_split, pair + 2)
                if kind == 0:
                    if not isinstance(gg, int) or gg > 0:
                        pe.wait_ge(v_copied, 2 * gg - 1 + half)
                else:
                    pe.wait_ge((q_copied, k_copied)[kind - 1], 2 * gg + half + 1)
                if kind < 2:
                    mh, ml = ((normed_high, normed_low), (ctx_high, ctx_low))[kind]
                    for c in range(DC):
                        w = slice(c * D + half * P, c * D + (half + 1) * P)
                        last = product3(acc[:, :], wh[:, kind, w], wl[:, kind, w], mh[:, c, tok], ml[:, c, tok], c == 0, c == DC - 1)
                    last.then_inc(qk_ready, 1)
                else:
                    for m in range(2):
                        b = 2 * half + m
                        keys = slice(n * TOK + b * P, n * TOK + (b + 1) * P)
                        for c in range(DC):
                            w = slice(c * D, (c + 1) * D)
                            last = product3(acc[:, m * D:(m + 1) * D], ctx_high[:, c, keys], ctx_low[:, c, keys],
                                            wh[:, 2, w], wl[:, 2, w], c == 0, c == DC - 1)
                    last.then_inc(v_ready, 1)

            def window(g, k, pair, core, carry, following):
                gg = g + PAIRS * GROUPS * layer
                for b in range(GROUP):
                    ss = GROUP * gg + b
                    if core:
                        if b == 0:
                            pe.wait_ge(q_copied, 2 * gg + 2)
                            pe.wait_ge(k_copied, 2 * gg + 2)
                        if carry or layer or b >= 2:
                            pe.wait_ge(exp_ready, ss - 1)
                        for h in range(2):
                            last = pe.matmul(wide_scores[b % 2][:, h * KEYS0:(h + 1) * KEYS0], q0[k % 2][:, h, b * P:(b + 1) * P],
                                             k0[k % 2][:, h, b, :], start=True, stop=True)
                        last.then_inc(scores_ready, 1)
                    turns = b > 0 and core or b == 0 and carry
                    a, parity = (b - 1) % GROUP, (k if b else k - 1) % 2
                    if turns:
                        pe.wait_ge(probs_ready, ss)
                        if carry or layer or b >= 2:
                            pe.wait_ge(probs_copied, ss - 1)
                        for h in range(2):
                            last = pe.transpose(wide_turned[:, h * P:(h + 1) * P], probs0[:, a, h, 0:P], ident[:, :])
                        last.then_inc(probs_turned, 1)
                    if following and b != 2:
                        project(gg + 1, k + 1, pair_number(layer, pair, k + 1), (0, 2, None, 5)[b])
                    if following and b == 2:
                        project(gg + 1, k + 1, pair_number(layer, pair, k + 1), 3)
                    if turns:
                        pe.wait_ge(probs_copied, ss)
                        pe.wait_ge(v_copied, 2 * gg + (b + 1) // 2)
                        if carry or layer or b >= 3:
                            pe.wait_ge(heads_split, ss - 2 + GROUP)
                        for h in range(2):
                            last = pe.matmul(wide_heads[a % 2][:, h * P:(h + 1) * P], v0[parity][:, a, h * P:(h + 1) * P],
                                             probs_t0[:, a, h, :], start=True, stop=True)
                        last.then_inc(heads_ready, 1)
                    if b >= 2 and core or b < 2 and carry:
                        a = (b - 2) % GROUP
                        slot = (k if b >= 2 else k - 1) // GROUPS % 2
                        pe.wait_ge(heads_split, ss - 1 + GROUP)
                        if a % 2 == 0 and (carry or layer):
                            pe.wait_ge(x_added, 2 * gg + b // 2 - 1 + ADD_CREDIT)
                        for h in range(2):
                            w = slice(h * D, (h + 1) * D)
                            last = product3(out_bank[:, a % 2 * D:(a % 2 + 1) * D], heads_high[:, h, a, :], heads_low[:, h, a, :],
                                            weights_high[slot][:, 3, w], weights_low[slot][:, 3, w], h == 0, h == 1)
                        if a % 2:
                            last.then_inc(out_ready, 1)
                    if following and b in (0, 2):
                        project(gg + 1, k + 1, pair_number(layer, pair, k + 1), (1, None, 4)[b])

            over_groups(pe, window)

        def feed_forward(which, weights_loaded):
            s = ff
            pe.wait_ge(weights_loaded, 32)
            with pe.Fori(0, ROUNDS) as i:
                r = i + ROUNDS * (which == 2)
                pe.wait_ge(s.rows_normed, SLOTS * (r + 1))
                for c in range(DC):
                    for u in range(SLOTS):
                        last = pe.transpose(bank[0][:, (SLOTS * c + u) * P:(SLOTS * c + u + 1) * P],
                                            norm_rows[:, u, c * P:(c + 1) * P], ident[:, :])
                last.then_inc(s.turned, 1)
                pe.wait_ge(s.in_ready, DC * (r + 1))
                for f in range(F0 // P):
                    for c in range(DC):
                        last = pe.matmul(bank[1 + f // 2][:, (f % 2) * D:(f % 2 + 1) * D], w_up[:, c, f * P:(f + 1) * P],
                                         hidden_in[:, c, :], start=c == 0, stop=c == DC - 1)
                    if f % 2:
                        last.then_inc(s.up_ready, 1)
                for u in range(SLOTS):
                    for f in range(F0 // P):
                        if u == 0:
                            pe.wait_ge(s.hidden_ready, F0 // P * r + f + 1)
                        last = pe.matmul(bank[5][:, u * D:(u + 1) * D], hidden[:, f, u * P:(u + 1) * P],
                                         w_down[:, f, :], start=f == 0, stop=f == F0 // P - 1)
                last.then_inc(s.down_ready, 1)

        def narrow_attention(a, i, q_of, k_of):
            s = a.s
            for j in range(a.per_round + 2):
                if j < a.per_round:
                    u, unit, step = j // a.per_slot, j // a.steps % a.units, j % a.steps
                    if j % a.per_slot == 0:
                        pe.wait_ge(s.spread, SLOTS * i + u + 1)
                        pe.wait_ge(s.q_ready, SLOTS * i + u + 1)
                    if j >= 2:
                        pe.wait_ge(s.exp_ready, a.per_round * i + j - 1)
                    pe.matmul(score_bank[j % 2][:, :], q_of(u, unit, step), k_of(u, step),
                              start=True, stop=True).then_inc(s.scores, 1)
                if 1 <= j <= a.per_round:
                    k = j - 1
                    pe.wait_ge(s.exp_ready, a.per_round * i + k + 1)
                    if k >= 2:
                        pe.wait_ge(s.probs_copied, a.per_round * i + k - 1)
                    for n in range(BANK // P):
                        last = pe.transpose(turn_bank[k % 2][:, n * P:(n + 1) * P],
                                            probs[k % 2][:, n * P:(n + 1) * P], ident[:, :])
                    last.then_inc(s.probs_turned, 1)
                if j >= 2:
                    k = j - 2
                    u, w, step = k // a.per_slot, k // a.steps, k % a.steps
                    pe.wait_ge(s.probs_copied, a.per_round * i + k + 1)
                    if k % a.per_slot == 0:
                        pe.wait_ge(s.v_ready, SLOTS * i + u + 1)
                    if w >= 2 and step == 0:
                        pe.wait_ge(s.heads_taken, a.all_units * i + w - 1)
                    for n in range(a.heads):
                        h = step * a.heads + n
                        for c in range(a.blocks):
                            m = n * a.blocks + c
                            last = pe.matmul(v_bank[w % 2][:, h * a.width:(h + 1) * a.width],
                                             probs_t[k % 2][:, m * P:(m + 1) * P], vn[u][:, c, h, 0:a.width],
                                             start=c == 0, stop=c == a.blocks - 1)
                    last.then_inc(s.heads, 1)

        def packed_core(s, b, u, j, core, carry):
            if core:
                if j % (HN // 2) == 0:
                    pe.wait_ge(s.k_low, 2 * b + j // (HN // 2) + 1)
                if j % PACK == 0:
                    pe.wait_ge(s.spread, PACKS * b + j // PACK + 1)
            if j >= 2 and core or j < 2 and carry:
                pe.wait_ge(s.exp_ready, HN * b + j - 1)
            if core:
                for unit in range(UNITS):
                    last = pe.matmul(score_bank[j % 2][:, unit * D:(unit + 1) * D], q_spread[u][:, j, unit * P:(unit + 1) * P],
                                     k_packed[u][:, j // PACK, :], start=True, stop=True)
                last.then_inc(s.scores, 1)
            if j >= 2 and core or j < 2 and carry:
                if carry or j >= 4:
                    pe.wait_ge(s.probs_copied, HN * b + j - 3)
                for c in range(UNITS):
                    for unit in range(UNITS):
                        last = pe.transpose(turn_bank[j % 2][:, (UNITS * c + unit) * P:(UNITS * c + unit + 1) * P],
                                            probs[j % 2][:, unit * D + c * P:unit * D + (c + 1) * P], ident[:, :])
                last.then_inc(s.probs_turned, 1)
            if j % PACK == 2 and (j > 2 and core or j == 2 and carry):
                g = (j - 2) // PACK - 1 if j > 2 else PACKS - 1
                v = vn[u] if j > 2 else vn[1 - u]
                if g == 0:
                    pe.wait_ge(s.v_ready, b + 1)
                pe.wait_ge(s.probs_copied, HN * b + j - 2)
                if carry or j > 6:
                    pe.wait_ge(s.sums_copied, PACKS * b + (j - 2) // PACK - 1)
                for c in range(UNITS):
                    for n in range(PACK):
                        last = pe.matmul(sum_bank[n * QUAD:(n + 1) * QUAD, 0:D], v[:, c, PACK * g + n, :],
                                         probs_t[(PACK * g + n) % 8][:, c * D:(c + 1) * D], start=c == 0, stop=c == UNITS - 1)
                last.then_inc(s.sums, 1)

        def packed_project(s, b, j, core, carry, at):
            n = b + 1
            for half in range(2):
                acc = aux[2 * half]
                if j == at["q"] + half:
                    pe.wait_ge(s.in_ready, n + 1)
                    if core and (half == 0 or not carry):
                        pe.wait_ge(s.k_low, 2 * b + half + 1)
                    for k in range(2):
                        g = 2 * half + k
                        last = pe.matmul(acc[:, k * D:(k + 1) * D], wq_packed[:, g, :, :].rearrange("p a r -> p (a r)"),
                                         x[:, ds(n, 1), :].rearrange("p a d -> p (a d)"), start=True, stop=True)
                    last.then_inc(s.q_projected, 1)
                if j == at["k"] + half:
                    pe.wait_ge(s.q_low, 2 * n + half + 1)
                    for k in range(2):
                        g = 2 * half + k
                        last = pe.matmul(acc[:, k * D:(k + 1) * D], wk_packed[:, g, :, :].rearrange("p a r -> p (a r)"),
                                         keys_in[:, :], start=True, stop=True)
                    last.then_inc(s.k_projected, 1)

        def packed_sums_turned(s, b, core):
            pe.wait_ge(s.sums_copied, PACKS * b)
            if core:
                pe.wait_ge(s.v_ready, b + 1)
                pe.wait_ge(s.k_low, 2 * b + 2)
            else:
                pe.wait_ge(s.x_added, b - 1)
            for unit in range(UNITS):
                for g in range(PACKS):
                    last = pe.transpose(aux[1 + unit][:, g * P:(g + 1) * P], sums_copy[:, g, unit * P:(unit + 1) * P], ident[:, :])
            last.then_inc(s.sums_turned, 1)

        def layer1():
            s = n1
            pe.wait_ge(later_loaded, later_count)
            pe.wait_ge(masks_ready, 1)
            for k in range(3):
                pe.transpose(bank[0][:, k * P:(k + 1) * P], w_rows1[:, k, :], ident[:, :])
            for c in range(2):
                last = pe.transpose(bank[1][:, c * B:(c + 1) * B], mask_own[:, c * P:(c + 1) * P], ident[0:B, 0:B])
            last.then_inc(masks_turned, 1)
            pe.wait_ge(packed_ready, 1)

            def window(b, u, core, carry, following, turn):
                for j in range(HN if core or following else PACK * 2 + 2):
                    if core or carry:
                        packed_core(s, b, u, j, core, carry)
                    if carry and j == 4:
                        packed_sums_turned(s, b, core)
                    if following:
                        packed_project(s, b, j, core, carry, dict(q=7, k=10))
                    if carry and j == 7:
                        pe.wait_ge(s.heads_taken, UNITS * b)
                        for n in range(2):
                            for unit in range(UNITS):
                                last = pe.transpose(aux[1][:, (2 * n + unit) * P:(2 * n + unit + 1) * P],
                                                    heads_out[unit][:, n * P:(n + 1) * P], ident[:, :])
                        last.then_inc(s.result, 1)
                    if following and j == 12:
                        if carry:
                            pe.wait_ge(s.x_added, b)
                        elif core:
                            pe.wait_ge(s.v_ready, b + 1)
                        for c in range(UNITS):
                            last = pe.matmul(aux[1][:, c * P:(c + 1) * P], keys_in[:, c * P:(c + 1) * P], wv1[:, :],
                                             start=True, stop=True)
                        last.then_inc(s.v_projected, 1)

            over_windows(pe, window)

        def layer2(a, cross):
            s = a.s
            pe.wait_ge(attention2_loaded, loads2_count)
            with pe.Fori(0, ROUNDS) as i:
                r = i + ROUNDS * int(cross)
                for u in range(SLOTS):
                    pe.wait_ge(s.rows_normed, SLOTS * r + u + 1)
                    if cross:
                        pe.wait_ge((s.loaded0, s.loaded1)[u], 32 * (i + 1))
                    for c in range(DC):
                        last = pe.transpose(q_bank[u][:, c * P:(c + 1) * P], norm_rows[:, u, c * P:(c + 1) * P], ident[:, :])
                    if cross:
                        for c in range(DC):
                            last = pe.transpose(q_bank[u][:, (DC + c) * P:(DC + c + 1) * P], cn[u][:, c * P:(c + 1) * P],
                                                ident[:, :])
                    last.then_inc(s.turned, 1)
                for u in range(SLOTS):
                    pe.wait_ge(s.in_ready, SLOTS * r + u + 1)
                    keys_in = cn_t[u] if cross else rows_t[u]
                    for m in range(4):
                        src = rows_t[u] if m < 2 else keys_in
                        for c in range(DC):
                            last = pe.matmul(q_bank[u][:, m * P:(m + 1) * P], w_qkv[:, int(cross), c, m * P:(m + 1) * P],
                                             src[:, c, :], start=c == 0, stop=c == DC - 1)
                    last.then_inc(s.projected, 1)
                    for c in range(DC):
                        last = pe.matmul(v_bank[u][:, 0:D], keys_in[:, c, :], w_qkv[:, int(cross), c, 2 * D:3 * D],
                                         start=c == 0, stop=c == DC - 1)
                    last.then_inc(s.values, 1)
                narrow_attention(a, r, lambda u, unit, step: qn[u][:, step // 2 * P:(step // 2 + 1) * P],
                                 lambda u, step: km[u][:, step * BANK:(step + 1) * BANK])
                for u in range(SLOTS):
                    pe.wait_ge(s.heads_taken, SLOTS * r + u + 1)
                    for c in range(DC):
                        last = pe.transpose(q_bank[u][:, c * P:(c + 1) * P], heads_out[u][:, c * P:(c + 1) * P], ident[:, :])
                    last.then_inc(s.heads_turned, 1)
                for u in range(SLOTS):
                    pe.wait_ge(s.heads_copied, SLOTS * r + u + 1)
                    for c in range(DC):
                        last = pe.matmul(q_bank[u][:, D:2 * D], heads_t[u][:, c * P:(c + 1) * P], w_out2[:, int(cross), c, :],
                                         start=c == 0, stop=c == DC - 1)
                    last.then_inc(s.result, 1)

        def layer3():
            s = n3
            pe.wait_ge(packed_ready, 2)

            def window(b, u, core, carry, following, turn):
                for j in range(HN if core or following else PACK * 2 + 2):
                    if core or carry:
                        packed_core(s, b, u, j, core, carry)
                    if following and j == 1:
                        pe.wait_ge(s.placed, b + 2)
                        if core:
                            pe.wait_ge(s.k_low, 2 * b + 1)
                        for n in range(4):
                            last = pe.transpose(aux[0][:, n * P:(n + 1) * P], placed_packed[:, n // 2, n % 2 * P:(n % 2 + 1) * P],
                                                ident[:, :])
                        last.then_inc(s.turned, 1)
                    if carry and j == 4:
                        packed_sums_turned(s, b, core)
                    if following and j == 5:
                        pe.wait_ge(s.rows_normed, b + 2)
                        for n in range(4):
                            last = pe.transpose(aux[0][:, n * P:(n + 1) * P], norm_packed[:, n // 2, n % 2 * P:(n % 2 + 1) * P],
                                                ident[:, :])
                        last.then_inc(s.turned_back, 1)
                    if carry and j == 7:
                        pe.wait_ge(s.heads_taken, UNITS * b)
                        for unit in range(UNITS):
                            last = pe.transpose(aux[1][:, unit * P:(unit + 1) * P], heads_out[unit][:, 0:P], ident[:, :])
                        last.then_inc(s.heads_turned, 1)
                    if following:
                        packed_project(s, b, j, core, carry, dict(q=7, k=10))
                    if carry and j == 9:
                        pe.wait_ge(s.heads_copied, b)
                        pe.matmul(aux[1][:, D:2 * D], w3[:, 3, :], heads_t[0][:, :], start=True, stop=True).then_inc(s.result, 1)
                    if following and j == 12:
                        if carry:
                            pe.wait_ge(s.x_added, b)
                        elif core:
                            pe.wait_ge(s.v_ready, b + 1)
                        for c in range(UNITS):
                            last = pe.matmul(aux[1][:, c * P:(c + 1) * P], keys_in[:, c * P:(c + 1) * P], w3[:, 2, :],
                                             start=True, stop=True)
                        last.then_inc(s.v_projected, 1)

            over_windows(pe, window)

        def feed_forward3():
            s = ff3
            with pe.Fori(0, ROUNDS) as i:
                for u in range(SLOTS):
                    b = SLOTS * i + u
                    pe.wait_ge(s.x_copied, b + 1)
                    for n in range(2):
                        last = pe.transpose(bank[u][:, n * P:(n + 1) * P], placed[u][:, 0, n * P:(n + 1) * P], ident[:, :])
                    last.then_inc(s.turned, 1)
                for u in range(SLOTS):
                    b = SLOTS * i + u
                    pe.wait_ge(s.rows_normed, b + 1)
                    for n in range(2):
                        last = pe.transpose(bank[2 + u][:, n * P:(n + 1) * P], norm3[u][:, 0, n * P:(n + 1) * P], ident[:, :])
                    last.then_inc(s.turned_back, 1)
                for u in range(SLOTS):
                    b = SLOTS * i + u
                    pe.wait_ge(s.in_ready, b + 1)
                    for f in range(2):
                        last = pe.matmul(bank[4 + u][:, f * D:(f + 1) * D], w3_up[:, f * P:(f + 1) * P], ln_t3[u][:, 0, :],
                                         start=True, stop=True)
                    last.then_inc(s.up_ready, 1)
                for u in range(SLOTS):
                    b = SLOTS * i + u
                    pe.wait_ge(s.hidden_ready, 2 * (b + 1))
                    for f in range(2):
                        last = pe.matmul(bank[6 + u][:, 0:D], w3_down[:, f, :], hidden3[u][:, f, :], start=f == 0, stop=f == 1)
                    last.then_inc(s.down_ready, 1)

        turn_context()
        for layer in range(2):
            turn_normed(layer)
            pairs(layer)
        feed_forward(0, weights0_loaded)
        layer1()
        layer2(a2s, False)
        layer2(a2c, True)
        feed_forward(2, weights2_loaded)
        layer3()
        feed_forward3()

    @block.scalar
    def _(act):
        def split_context():
            for g in range(GROUPS):
                for c in range(DC):
                    act.wait_ge(rows_turned, DC * g + c + 1)
                    act.activation(ctx_high[:, c, g * TOK:(g + 1) * TOK], bank[2 * (g % 2) + c][:, :], ACT.Copy)\
                       .then_inc(ctx_high_ready, 1)

        def split_normed(layer):
            with act.Fori(0, ROUNDS) as i:
                for c in range(DC):
                    act.wait_ge(normed_ready, DC * (ROUNDS * layer + i) + c + 1)
                    act.sem_inc(idle, 1)
                    act.activation(normed_high[:, c, ds(i * SLOTS * P, SLOTS * P)], normed[:, c, :], ACT.Copy)\
                       .then_inc(normed_high_ready, 1)

        def pairs(layer):
            def copy_keys(gg, k, h):
                slot, n = k // GROUPS % 2, k % GROUPS
                keys = k0[k % 2]
                act.wait_ge(qk_ready, 4 * gg + 2 + h + 1)
                if n < 2:
                    act.activation(keys[:, h, :, P:P + 1], columns[slot][:, 2:3, h:h + 1].broadcast_to([P, GROUP, 1]), ACT.Copy)
                act.activation(keys[:, h, :, 0:P], project_bank[h][:, :].rearrange("p (b k) -> p b k", b=GROUP), ACT.Identity,
                               bias=columns[slot][:, 1, h:h + 1]).then_inc(k_copied, 1)

            def window(g, k, pair, core, carry, following):
                gg = g + PAIRS * GROUPS * layer
                for b in range(GROUP):
                    ss = GROUP * gg + b
                    turns = b > 0 and core or b == 0 and carry
                    a = (b - 1) % GROUP
                    if turns:
                        act.wait_ge(probs_turned, ss)
                        act.activation(probs_t0[:, a, :, :], wide_turned[:, 0:2 * P].rearrange("p (h q) -> p h q", h=2), ACT.Copy)\
                           .then_inc(probs_copied, 1)
                    if core:
                        act.wait_ge(max_ready, ss + 1)
                        for h in range(2):
                            last = act.activation(probs0[:, b, h, :], wide_scores[b % 2][:, h * KEYS0:(h + 1) * KEYS0], ACT.Exp,
                                                  bias=neg_max0[:, b, h:h + 1], accum_out=sums0[:, b, h:h + 1])
                        last.then_inc(exp_ready, 1)
                    if turns:
                        slot = (k if b else k - 1) // GROUPS % 2
                        act.wait_ge(heads_ready, ss)
                        for h in range(2):
                            last = act.activation(heads_high[:, h, a, :], wide_heads[a % 2][:, h * P:(h + 1) * P], ACT.Identity,
                                                  bias=columns[slot][:, 3, h:h + 1])
                        last.then_inc(heads_high_ready, 1)
                    if following and b in (1, 2):
                        copy_keys(gg + 1, k + 1, b - 1)

            over_groups(act, window)

        def feed_forward(which, norm, function):
            s = ff
            with act.Fori(0, ROUNDS) as i:
                r = i + ROUNDS * (which == 2)
                act.wait_ge(s.turned, r + 1)
                for c in range(DC):
                    act.activation(hidden_in[:, c, :], bank[0][:, c * D:(c + 1) * D], ACT.Identity, bias=norm_offset[:, norm, c:c + 1],
                                   scale=norm_scale[:, norm, c:c + 1]).then_inc(s.in_ready, 1)
                for f in range(F0 // P):
                    act.wait_ge(s.up_ready, F0 // P // 2 * r + f // 2 + 1)
                    act.activation(hidden[:, f, :], bank[1 + f // 2][:, (f % 2) * D:(f % 2 + 1) * D], function,
                                   bias=b_up[:, which // 2, f:f + 1]).then_inc(s.hidden_ready, 1)

        def narrow_attention(a, i):
            s = a.s
            for j in range(a.per_round + 1):
                if j >= 1:
                    k = j - 1
                    act.wait_ge(s.probs_turned, a.per_round * i + k + 1)
                    if k >= 2:
                        act.wait_ge(s.heads, a.per_round * i + k - 1)
                    act.activation(probs_t[k % 2][:, :], turn_bank[k % 2][:, :], ACT.Copy).then_inc(s.probs_copied, 1)
                if j < a.per_round:
                    act.wait_ge(s.max_ready, a.per_round * i + j + 1)
                    if j >= 2:
                        act.wait_ge(s.probs_turned, a.per_round * i + j - 1)
                    source = scores_masked[j % 2] if a.mask else score_bank[j % 2]
                    for h in range(a.heads):
                        part = slice(h * a.keys, (h + 1) * a.keys)
                        last = act.activation(probs[j % 2][:, part], source[:, part], ACT.Exp, bias=neg_max[j % 2][:, h:h + 1])
                    last.then_inc(s.exp_ready, 1)

        def packed_core(s, b, u, j, core, carry):
            if j >= 2 and core or j < 2 and carry:
                act.wait_ge(s.probs_turned, HN * b + j - 1)
                if j % PACK == 2 and (carry or j >= 10):
                    act.wait_ge(s.sums, PACKS * b + (j - 2) // PACK - 1)
                act.activation(probs_t[(j - 2) % 8][:, :], turn_bank[j % 2][:, :], ACT.Copy).then_inc(s.probs_copied, 1)
            if core:
                act.wait_ge(s.max_ready, HN * b + j + 1)
                for unit in range(UNITS):
                    part = slice(unit * D, (unit + 1) * D)
                    last = act.activation(probs[j % 2][:, part], score_bank[j % 2][:, part], ACT.Exp,
                                          bias=neg_max[j % 2][:, unit:unit + 1])
                last.then_inc(s.exp_ready, 1)

        def packed_high(s, b, u, j, at, q_bias, k_bias):
            n = b + 1
            for half in range(2):
                for name, projected, target, bias, ready in (("q", s.q_projected, q_packed[1 - u], q_bias, s.q_high),
                                                             ("k", s.k_projected, k_packed[1 - u], k_bias, s.k_high)):
                    if j == at[name] + half:
                        act.wait_ge(projected, 2 * n + half + 1)
                        if bias is None:
                            last = act.activation(target[:, 2 * half:2 * half + 2, :],
                                                  aux[2 * half][:, :].rearrange("p (g d) -> p g d", g=2), ACT.Copy)
                        else:
                            for k in range(2):
                                g = 2 * half + k
                                last = act.activation(target[:, g, :], aux[2 * half][:, k * D:(k + 1) * D], ACT.Identity,
                                                      bias=bias[:, g:g + 1])
                        last.then_inc(ready, 1)

        def layer1():
            s = n1
            act.wait_ge(packed_ready, 1)

            def window(b, u, core, carry, following, turn):
                for j in range(HN if core or following else PACK * 2 + 2):
                    if core or carry:
                        packed_core(s, b, u, j, core, carry)
                    if following:
                        packed_high(s, b, u, j, dict(q=8, k=11), bq1, bias1[:, 1, :])

            over_windows(act, window)
            act.wait_ge(s.x_added, B)
            act.activation(std_t[:, :, :], std_t[:, :, :], ACT.Sqrt).then_inc(std_ready, 1)

        def layer2(a, cross):
            s = a.s
            norm = 3 + int(cross)
            with act.Fori(0, ROUNDS) as i:
                r = i + ROUNDS * int(cross)
                for u in range(SLOTS):
                    act.wait_ge(s.turned, SLOTS * r + u + 1)
                    for c in range(DC):
                        last = act.activation(rows_t[u][:, c, :], q_bank[u][:, c * P:(c + 1) * P], ACT.Identity,
                                              bias=norm_offset[:, norm, c:c + 1], scale=norm_scale[:, norm, c:c + 1])
                    if cross:
                        last = act.activation(cn_t[u][:, :, :], q_bank[u][:, D:2 * D].rearrange("p (c k) -> p c k", c=DC), ACT.Copy)
                    last.then_inc(s.in_ready, 1)
                for u in range(SLOTS):
                    act.wait_ge(s.projected, SLOTS * r + u + 1)
                    for c in range(DC):
                        last = act.activation(qn[u][:, c * P:(c + 1) * P], q_bank[u][:, c * P:(c + 1) * P], ACT.Identity,
                                              bias=b_q2[:, int(cross), c:c + 1], scale=SCALE2)
                    last.then_inc(s.q_ready, 1)
                    for c in range(DC):
                        last = act.activation(kn[u][:, c * P:(c + 1) * P], q_bank[u][:, (DC + c) * P:(DC + c + 1) * P], ACT.Identity,
                                              bias=b_qk2[:, int(cross), 1, c:c + 1])
                    last.then_inc(s.k_ready, 1)
                narrow_attention(a, r)
                for u in range(SLOTS):
                    act.wait_ge(s.heads_turned, SLOTS * r + u + 1)
                    act.activation(heads_t[u][:, :], q_bank[u][:, 0:D], ACT.Copy).then_inc(s.heads_copied, 1)

        def layer3():
            s = n3

            def window(b, u, core, carry, following, turn):
                for j in range(HN if core or following else PACK * 2 + 2):
                    if core or carry:
                        packed_core(s, b, u, j, core, carry)
                    if following and j == 6:
                        act.wait_ge(s.turned_back, b + 2)
                        act.sem_inc(idle, 1)
                        act.activation(x[:, ds(b + 1, 1), :].rearrange("p a d -> p (a d)"), aux[0][:, 0:D], ACT.Identity,
                                       bias=ln3[:, 1:2], scale=ln3[:, 0:1])
                        act.activation(keys_in[:, :], aux[0][:, D:2 * D], ACT.Identity,
                                       bias=ln3[:, 3:4], scale=ln3[:, 2:3]).then_inc(s.in_ready, 1)
                    if carry and j == 8:
                        act.wait_ge(s.heads_turned, b)
                        act.activation(heads_t[0][:, :], aux[1][:, 0:D], ACT.Copy).then_inc(s.heads_copied, 1)
                    if following:
                        packed_high(s, b, u, j, dict(q=8, k=11), None, None)

            over_windows(act, window)

        def feed_forward3():
            s = ff3
            with act.Fori(0, ROUNDS) as i:
                for u in range(SLOTS):
                    act.wait_ge(s.turned_back, SLOTS * i + u + 1)
                    act.activation(ln_t3[u][:, 0, :], bank[2 + u][:, 0:D], ACT.Identity, bias=ln3[:, 5:6], scale=ln3[:, 4:5])\
                       .then_inc(s.in_ready, 1)
                for u in range(SLOTS):
                    act.wait_ge(s.up_ready, SLOTS * i + u + 1)
                    for f in range(2):
                        act.activation(hidden3[u][:, f, :], bank[4 + u][:, f * D:(f + 1) * D], ACT.Gelu, bias=b3_up[:, f:f + 1])\
                           .then_inc(s.hidden_ready, 1)

        split_context()
        for layer in range(2):
            split_normed(layer)
            pairs(layer)
        feed_forward(0, 2, ACT.Gelu)
        layer1()
        layer2(a2s, False)
        layer2(a2c, True)
        feed_forward(2, 5, ACT.Gelu_apprx_tanh)
        layer3()
        feed_forward3()

    @block.vector
    def _(dve):
        def spread_over(tile, shape, axis):
            return tile.unsqueeze(axis).broadcast_to(shape)

        def split_context():
            for g in range(GROUPS):
                tok = slice(g * TOK, (g + 1) * TOK)
                for c in range(DC):
                    dve.wait_ge(ctx_high_ready, DC * g + c + 1)
                    dve.tensor_tensor(ctx_low[:, c, tok], bank[2 * (g % 2) + c][:, :], ctx_high[:, c, tok].bitcast(F32),
                                      ALU.subtract).then_inc(ctx_low_ready, 1)

        def norm_two(chain, i, sem_ready):
            for u in range(SLOTS):
                chain.mark(dve.bn_stats(stats.sums[:, u, :], x[:, ds(SLOTS * i + u, 1), :].rearrange("p a d -> p (a d)")))
            chain.join()
            dve.sem_inc(idle, 1)
            for u in range(SLOTS):
                chain.mark(dve.bn_aggr(stats.mean_var[:, u, :], stats.sums[:, u, :]))
            chain.join()
            inverse_root(dve, chain, stats.rstd[:, 0:SLOTS], stats.mean_var[:, 0:SLOTS, 1], stats.shifted[:, 0:SLOTS],
                         stats.work[:, 0:SLOTS])
            for u in range(SLOTS):
                dve.tensor_scalar(norm_rows[:, u, :], x[:, ds(SLOTS * i + u, 1), :].rearrange("p a d -> p (a d)"),
                                  stats.mean_var[:, u, 0:1], stats.rstd[:, u:u + 1], ALU.subtract, ALU.mult)\
                   .then_inc(sem_ready, 1)

        NORM_TWO = 2 * SLOTS + 11

        def add_row_bias(chain, i, bias):
            both = x[:, ds(SLOTS * i, SLOTS), :]
            chain.mark(dve.tensor_tensor(both, both, row_bias[:, bias:bias + 1, :].broadcast_to([P, SLOTS, D]), ALU.add))

        def norm_and_split(layer):
            with dve.Fori(0, ROUNDS) as i:
                r = ROUNDS * layer + i
                chain = Chain(dve, split_chain, (NORM_TWO + 1) * r)
                norm_two(chain, i, rows_normed)
                dve.wait_ge(rows_normed, SLOTS * (r + 1))
                add_row_bias(chain, i, layer)
                dve.wait_ge(normed_turned, r + 1)
                tok = ds(i * SLOTS * P, SLOTS * P)
                for c in range(DC):
                    dve.tensor_scalar(normed[:, c, :], bank[4][:, c * D:(c + 1) * D], norm_scale[:, layer, c:c + 1],
                                      norm_offset[:, layer, c:c + 1], ALU.mult, ALU.add).then_inc(normed_ready, 1)
                for c in range(DC):
                    dve.wait_ge(normed_high_ready, DC * r + c + 1)
                    dve.tensor_tensor(normed_low[:, c, tok], normed[:, c, :], normed_high[:, c, tok].bitcast(F32),
                                      ALU.subtract).then_inc(normed_low_ready, 1)
            dve.wait_ge(split_chain, (NORM_TWO + 1) * ROUNDS * (layer + 1))

        def pairs(layer):
            def copy_queries(gg, k, h):
                slot = k // GROUPS % 2
                dve.wait_ge(qk_ready, 4 * gg + h + 1)
                dve.tensor_scalar(q0[k % 2][:, h, :], project_bank[h][:, :], columns[slot][:, 0, h:h + 1], SCALE0, ALU.add, ALU.mult)\
                   .then_inc(q_copied, 1)

            def copy_values(gg, k, half):
                slot = k // GROUPS % 2
                dve.wait_ge(v_ready, 2 * gg + half + 1)
                dve.tensor_tensor(v0[k % 2][:, 2 * half:2 * half + 2, :], project_bank[half][:, :].rearrange("p (b d) -> p b d", b=2),
                                  value_bias[slot][:, :, :].broadcast_to([P, 2, D]), ALU.add).then_inc(v_copied, 1)

            def window(g, k, pair, core, carry, following):
                gg = g + PAIRS * GROUPS * layer
                for b in range(GROUP):
                    ss = GROUP * gg + b
                    if core:
                        dve.wait_ge(scores_ready, ss + 1)
                        dve.tensor_reduce(neg_max0[:, b, :], wide_scores[b % 2][:, 0:2 * KEYS0].rearrange("p (h k) -> p h k", h=2),
                                          X_AXIS, ALU.max, negate=True).then_inc(max_ready, 1)
                        chain = Chain(dve, softmax_chain, ss)
                        dve.wait_ge(exp_ready, ss + 1)
                        chain.link(dve.reciprocal(inverse0[:, b, :], sums0[:, b, :]))
                        for h in range(2):
                            last = dve.tensor_scalar(probs0[:, b, h, 0:P], probs0[:, b, h, 0:P], inverse0[:, b, h:h + 1], None,
                                                     ALU.mult)
                        last.then_inc(probs_ready, 1)
                    if following and b == 0:
                        copy_queries(gg + 1, k + 1, 0)
                    if following and b == 3:
                        copy_values(gg + 1, k + 1, 1)
                    if b > 0 and core or b == 0 and carry:
                        a, slot = (b - 1) % GROUP, (k if b else k - 1) // GROUPS % 2
                        dve.wait_ge(heads_high_ready, ss)
                        for h in range(2):
                            last = dve.scalar_tensor_tensor(heads_low[:, h, a, :], wide_heads[a % 2][:, h * P:(h + 1) * P],
                                                            columns[slot][:, 3, h:h + 1], heads_high[:, h, a, :].bitcast(F32),
                                                            ALU.add, ALU.subtract)
                        last.then_inc(heads_split, 1)
                    if b == 3 and core or b == 1 and carry:
                        done = 2 * gg + b // 2
                        n, half = (k if b == 3 else k - 1) % GROUPS, 1 - b // 2
                        rows = x[:, GROUP * n + 2 * half:GROUP * n + 2 * half + 2, :]
                        dve.wait_ge(out_ready, done)
                        dve.wait_ge(x_added, done - 8 + ADD_CREDIT)
                        dve.tensor_tensor(rows, rows, out_bank[:, :].rearrange("p (b d) -> p b d", b=2), ALU.add).then_inc(x_added, 1)
                    if following and b == 0:
                        copy_queries(gg + 1, k + 1, 1)
                    if following and b == 2:
                        copy_values(gg + 1, k + 1, 0)

            over_groups(dve, window)
            dve.wait_ge(x_added, 8 * PAIRS * (layer + 1) + ADD_CREDIT)

        def feed_forward(which, bias):
            s = ff
            steps = NORM_TWO + 1
            with dve.Fori(0, ROUNDS) as i:
                r = i + ROUNDS * (which == 2)
                chain = Chain(dve, s.chain, steps * r)
                norm_two(chain, i, s.rows_normed)
                dve.wait_ge(s.rows_normed, SLOTS * (r + 1))
                add_row_bias(chain, i, bias)
                dve.wait_ge(s.down_ready, r + 1)
                chain.join()
                both = x[:, ds(SLOTS * i, SLOTS), :]
                dve.tensor_tensor(both, both, bank[5][:, :].rearrange("p (u d) -> p u d", u=SLOTS), ALU.add)\
                   .then_inc(s.x_added, 1)
            dve.wait_ge(s.x_added, ROUNDS * (1 + which // 2))

        def narrow_attention(a, i, chain, masks, take_heads):
            s = a.s
            for j in range(a.per_round + 4):
                if j < a.per_round:
                    u = j // a.per_slot
                    source = score_bank[j % 2][:, :].rearrange("p (h k) -> p h k", h=a.heads)
                    dve.wait_ge(s.scores, a.per_round * i + j + 1)
                    if masks is not None:
                        masked = scores_masked[j % 2][:, :].rearrange("p (h k) -> p h k", h=a.heads)
                        mask = masks(u)
                        wide = [P, a.heads, a.keys]
                        chain.link(dve.tensor_tensor(masked, source, mask[:, 0:1, :].broadcast_to(wide), ALU.mult))
                        chain.link(dve.tensor_tensor(masked, masked, mask[:, 1:2, :].broadcast_to(wide), ALU.add))
                        source = masked
                    dve.tensor_reduce(neg_max[j % 2][:, 0:a.heads], source, X_AXIS, ALU.max, negate=True)\
                       .then_inc(s.max_ready, 1)
                if j > 3 and (j - 3) % a.steps == 0:
                    w = (j - 3) // a.steps - 1
                    dve.wait_ge(s.heads, a.per_round * i + (w + 1) * a.steps)
                    sums = v_bank[w % 2][:, 0:HN * a.width].rearrange("p (h e) -> p h e", h=HN)
                    chain.link(dve.reciprocal(inverse[:, w % 2, :].unsqueeze(2), sums[:, :, a.width - 1:a.width]))
                    take_heads(w, sums)

        def pack_weights(chain, queries, keys):
            for part in range(PACK):
                chain.mark(dve.tensor_scalar(wq_packed[:, :, part, :], queries.rearrange("p (g r) -> p g r", g=PACKS), SCALE1, None,
                                             ALU.mult))
                chain.mark(dve.tensor_copy(wk_packed[:, :, part, :], keys.rearrange("p (g r) -> p g r", g=PACKS)))

        def weighted(w, target, sums):
            return dve.tensor_tensor(target.rearrange("p (h e) -> p h e", h=HN), sums,
                                     inverse[:, w % 2, :].unsqueeze(2).broadcast_to([P, HN, sums.shape[2]]), ALU.mult)

        def packed_core(s, b, u, j, core, carry):
            if core:
                dve.wait_ge(s.scores, HN * b + j + 1)
                dve.tensor_reduce(neg_max[j % 2][:, 0:UNITS], score_bank[j % 2][:, :].rearrange("p (a k) -> p a k", a=UNITS),
                                  X_AXIS, ALU.max, negate=True).then_inc(s.max_ready, 1)
            if j % PACK == 3 and (j > 3 and core or j == 3 and carry):
                g = (j - 3) // PACK - 1 if j > 3 else PACKS - 1
                dve.wait_ge(s.sums, PACKS * b + (j - 3) // PACK)
                dve.tensor_copy(sums_copy[:, g, :], sum_bank[:, 0:D]).then_inc(s.sums_copied, 1)

        def packed_low(s, b, u, j, at, q_bias, k_bias):
            n = b + 1
            for half in range(2):
                for name, high, target, bias, quad, ready in (("q", s.q_high, q_packed[1 - u], q_bias, 2, s.q_low),
                                                              ("k", s.k_high, k_packed[1 - u], k_bias, 1, s.k_low)):
                    if j == at[name] + half:
                        dve.wait_ge(high, 2 * n + half + 1)
                        rows = slice(quad * QUAD, (quad + 1) * QUAD)
                        packs = slice(2 * half, 2 * half + 2)
                        full = aux[2 * half][rows, :].rearrange("p (g d) -> p g d", g=2)
                        if bias is None:
                            last = dve.tensor_tensor(target[rows, packs, :], full, target[rows, packs, :].bitcast(F32), ALU.subtract)
                        else:
                            for k in range(2):
                                g = 2 * half + k
                                last = dve.scalar_tensor_tensor(target[rows, g, :], full[:, k, :], bias[rows, g:g + 1],
                                                                target[rows, g, :].bitcast(F32), ALU.add, ALU.subtract)
                        last.then_inc(ready, 1)

        def layer1():
            s = n1
            dve.wait_ge(later_loaded, later_count)
            chain = Chain(dve, masks_chain)
            chain.mark(dve.tensor_copy(mask_own[:, :], mask_own_bytes[:, :]))
            chain.mark(dve.memset(ones[:, :], 1.0))
            for u in range(SLOTS):
                chain.mark(dve.memset(vn[u][:, :, :, :], 0.0))
            chain.mark(dve.tensor_scalar(bq1[:, :], bias1[:, 0, :], SCALE1, None, ALU.mult))
            chain.mark(dve.tensor_scalar(b_q2[:, :, :], b_qk2[:, :, 0, :], SCALE2, None, ALU.mult))
            chain.mark(dve.tensor_scalar(self_mask[:, 1, :], self_mask[:, 0, :], NEG_BIG, -NEG_BIG, ALU.mult, ALU.add))
            chain.join()
            dve.tensor_copy(mask_rows[:, :, :], mask_bytes[:, :, :]).then_inc(masks_ready, 1)
            dve.wait_ge(masks_ready, 1)
            chain.link(dve.tensor_reduce(valid[:, :], mask_rows[:, :, :], X_AXIS, ALU.add))
            chain.link(dve.reciprocal(valid[:, :], valid[:, :]))
            dve.wait_ge(masks_turned, 1)
            pack_weights(chain, bank[0][:, 0:P], bank[0][:, P:2 * P])
            chain.mark(dve.tensor_copy(wv1[:, :], bank[0][:, 2 * P:3 * P]))
            chain.mark(dve.tensor_copy(mask_keys[:, :, :].rearrange("p b c -> p c b"),
                                       bank[1][:, 0:2 * B].rearrange("p (c b) -> p c b", c=2)))
            dve.wait_ge(heads_known, 3)
            chain.link(dve.tensor_reduce(part_of_head[:, :], head_of_8[:, 0:3 * PACK].rearrange("p (a h) -> p h a", a=3),
                                         X_AXIS, ALU.add))
            dve.sem_inc(packed_ready, 1)

            KEYS, VALUES, HEADS = 4, 6, 9

            def keys_of(b, u, turn, j):
                n = b + 1
                chain = Chain(dve, s.prep_chain, KEYS * n)
                chain.steps = (0, 2, 4)[j]
                mask = mask_rows[:, ds(n, 1), :].rearrange("p a d -> p (a d)")
                source = cn[1 - u][:, :]
                if j == 0:
                    dve.wait_ge((s.loaded0, s.loaded1)[1 - u], 16 * (turn + 1))
                    chain.link(dve.tensor_tensor(scratch1[:, :], source, mask, ALU.mult))
                    chain.link(dve.tensor_reduce(key_mean[:, :], scratch1[:, :], X_AXIS, ALU.add))
                elif j == 1:
                    chain.link(dve.tensor_tensor(key_mean[:, :], key_mean[:, :], valid[:, ds(n, 1)], ALU.mult))
                    chain.link(dve.scalar_tensor_tensor(scratch1[:, :], source, key_mean[:, 0:1], mask, ALU.subtract, ALU.mult))
                else:
                    dve.tensor_scalar(keys_in[:, :], scratch1[:, :], key_mean[:, 0:1], None, ALU.add).then_inc(s.in_ready, 1)

            def values_of(b, u):
                n = b + 1
                chain = Chain(dve, s.values_chain, VALUES * n)
                dve.wait_ge(s.v_projected, n + 1)
                dve.wait_ge(s.in_ready, n + 1)
                v = scratch1[:, :].rearrange("p (c d) -> p c d", c=2)
                chain.link(dve.tensor_tensor(v, aux[1][:, 0:D].rearrange("p (c d) -> p c d", c=2),
                                             bv1[:, :, :].broadcast_to([P, 2, P]), ALU.add))
                for c in range(UNITS):
                    valid_key = mask_keys[:, ds(n, 1), c]
                    heads = v[:, c, :].rearrange("p (h e) -> p h e", h=HN)
                    chain.mark(dve.tensor_scalar(vn[1 - u][:, c, :, 0:8], heads, valid_key, None, ALU.mult))
                    chain.mark(dve.scalar_tensor_tensor(vn[1 - u][:, c, :, 8:16], heads, valid_key, heads, ALU.mult, ALU.mult))
                    ins = dve.tensor_scalar(vn[1 - u][:, c, :, 16], ones[:, :], valid_key, None, ALU.mult)
                    if c:
                        ins.then_inc(s.v_ready, 1)
                    else:
                        chain.mark(ins)

            def moments(b, unit):
                chain = Chain(dve, s.heads_chain, HEADS * (b - 1))
                chain.steps = 4 * unit
                if unit == 0:
                    dve.wait_ge(s.sums_turned, b)
                sums = aux[1 + unit][:, :].rearrange("p (h e) -> p h e", h=HN)
                mean, square = heads_out[unit][:, 0:P], heads_out[unit][:, P:2 * P]
                chain.link(dve.reciprocal(inverse[:, unit, :].unsqueeze(2), sums[:, :, 16:17]))
                chain.mark(weighted(unit, mean, sums[:, :, 0:8]))
                chain.link(weighted(unit, square, sums[:, :, 8:16]))
                chain.link(dve.tensor_tensor(scratch_heads[unit], mean, mean, ALU.mult))
                dve.tensor_tensor(square, square, scratch_heads[unit], ALU.subtract).then_inc(s.heads_taken, 1)

            scratch_heads = [heads_t[u][:, 0:P] for u in range(UNITS)]

            def window(b, u, core, carry, following, turn):
                for j in range(HN if core or following else PACK * 2 + 2):
                    if core or carry:
                        packed_core(s, b, u, j, core, carry)
                    if following and j < 3:
                        if core and j == 0:
                            dve.wait_ge(s.v_ready, b + 1)
                        keys_of(b, u, turn, j)
                    if carry and j in (5, 6):
                        moments(b, j - 5)
                    if carry and j == 8:
                        dve.wait_ge(s.result, b)
                        Chain(dve, s.heads_chain).mark(
                            dve.tensor_scalar(mean_t[:, ds(b - 1, 1), :].rearrange("p a d -> p (a d)"), aux[1][:, 0:D], 1.0, None,
                                              ALU.mult))
                        dve.tensor_scalar(std_t[:, ds(b - 1, 1), :].rearrange("p a d -> p (a d)"), aux[1][:, D:2 * D], 0.0, None,
                                          ALU.max).then_inc(s.x_added, 1)
                    if following:
                        packed_low(s, b, u, j, dict(q=9, k=12), bq1, bias1[:, 1, :])
                        if j == 14:
                            values_of(b, u)

            over_windows(dve, window)
            dve.wait_ge(s.heads_chain, HEADS * B)

            dve.wait_ge(s.x_added, B)
            chain = Chain(dve, std_chain)
            n, mean, var, rstd, shifted, work = (row_sums[:, k, :] for k in range(6))
            chain.link(dve.tensor_tensor(x[:, :, :], x[:, :, :], mask_rows[:, :, :], ALU.mult))
            for half in range(2):
                part = slice(half * B // 2, (half + 1) * B // 2)
                chain.link(dve.tensor_tensor(hidden[:, :, :], x[:, part, :], x[:, part, :], ALU.mult))
                chain.link(dve.tensor_reduce(var[:, part], hidden[:, :, :], X_AXIS, ALU.add))
            chain.link(dve.tensor_reduce(mean, x[:, :, :], X_AXIS, ALU.add))
            chain.link(dve.tensor_tensor(mean, mean, valid[:, :], ALU.mult))
            chain.mark(dve.tensor_tensor(n, mean, mean, ALU.mult))
            chain.link(dve.tensor_tensor(var, var, valid[:, :], ALU.mult))
            chain.link(dve.tensor_tensor(var, var, n, ALU.subtract))
            chain.link(dve.tensor_scalar(var, var, 0.0, None, ALU.max))
            inverse_root(dve, chain, rstd, var, shifted, work)
            for b in range(B):
                chain.mark(dve.tensor_scalar(x[:, b, :], x[:, b, :], mean[:, b:b + 1], rstd[:, b:b + 1], ALU.subtract, ALU.mult))
            chain.join()
            dve.wait_ge(std_ready, 1)
            chain.link(dve.tensor_tensor(x[:, :, :], x[:, :, :], std_t[:, :, :], ALU.mult))
            chain.link(dve.tensor_tensor(x[:, :, :], x[:, :, :], mean_t[:, :, :], ALU.add))
            chain.link(dve.tensor_tensor(x[:, :, :], x[:, :, :], mask_rows[:, :, :], ALU.mult))

        def layer2(a, cross):
            s = a.s
            if not cross:
                chain = Chain(dve, s.setup)
                for u in range(SLOTS):
                    chain.mark(dve.memset(vn[u][:, 0, :, 16], 1.0))
                chain.join()

            def take_heads(w, sums):
                weighted(w, heads_out[w][:, :], sums[:, :, 0:16]).then_inc(s.heads_taken, 1)

            steps = NORM_TWO + 1 + SLOTS * (1 + int(cross)) + a.per_round * 2 + a.all_units
            with dve.Fori(0, ROUNDS) as i:
                r = i + ROUNDS * int(cross)
                chain = Chain(dve, s.cross_chain if cross else s.chain, steps * i)
                norm_two(chain, i, s.rows_normed)
                dve.wait_ge(s.rows_normed, SLOTS * (r + 1))
                add_row_bias(chain, i, 3 + int(cross))
                for u in range(SLOTS):
                    if cross:
                        dve.wait_ge((s.loaded0, s.loaded1)[u], 32 * (i + 1))
                        chain.mark(dve.tensor_scalar(cross_mask[u][:, 1, :], cross_mask[u][:, 0, :], NEG_BIG, -NEG_BIG,
                                                     ALU.mult, ALU.add))
                    dve.wait_ge(s.k_ready, SLOTS * r + u + 1)
                    for c in range(DC):
                        ins = dve.tensor_tensor(km[u][:, c * 8 * P:(c + 1) * 8 * P].rearrange("p (h k) -> p h k", h=8),
                                                spread_over(kn[u][:, c * P:(c + 1) * P], [P, 8, P], 1),
                                                spread_over(head_of_16[:, :], [P, 8, P], 2), ALU.mult)
                        if c:
                            ins.then_inc(s.spread, 1)
                        else:
                            chain.mark(ins)
                    dve.wait_ge(s.values, SLOTS * r + u + 1)
                    dve.tensor_tensor(vn[u][:, 0, :, 0:16], v_bank[u][:, 0:D].rearrange("p (h e) -> p h e", h=HN),
                                      b_v2[:, int(cross), :].rearrange("p (h e) -> p h e", h=HN), ALU.add).then_inc(s.v_ready, 1)
                chain.join()
                narrow_attention(a, r, chain, (lambda u: cross_mask[u]) if cross else (lambda u: self_mask), take_heads)
                for u in range(SLOTS):
                    dve.wait_ge(s.result, SLOTS * r + u + 1)
                    row = x[:, ds(SLOTS * i + u, 1), :].rearrange("p a d -> p (a d)")
                    dve.tensor_tensor(row, row, q_bank[u][:, D:2 * D], ALU.add).then_inc(s.x_added, 1)
            assert chain.steps == steps, (chain.steps, steps)
            dve.wait_ge(s.x_added, B * (1 + int(cross)))

        def norm_columns(chain, tiles, outs, sem_ready):
            row_statistics(dve, chain, tiles, stats, idle)
            for k, (tile, target) in enumerate(zip(tiles, outs)):
                ins = dve.tensor_scalar(target, tile, stats.mean_var[:, k, 0:1], stats.rstd[:, k:k + 1], ALU.subtract, ALU.mult)
                if k < len(tiles) - 1:
                    chain.mark(ins)
            ins.then_inc(sem_ready, 1)
            chain.join()

        def layer3():
            s = n3
            chain = Chain(dve, s.values_chain)
            pack_weights(chain, w3[:, 0, :], w3[:, 1, :])
            for u in range(SLOTS):
                chain.mark(dve.memset(vn[u][:, :, :, :], 0.0))
            chain.join()
            for u in range(SLOTS):
                chain.mark(dve.memset(vn[u][:, :, :, 8], 1.0))
            chain.join()
            dve.sem_inc(packed_ready, 1)

            PREP, HEADS = 1 + 4 + 4 + 11 + 3, 2
            tiles = [aux[0][:, k * P:(k + 1) * P] for k in range(4)]
            targets = [norm_packed[:, k // 2, k % 2 * P:(k % 2 + 1) * P] for k in range(4)]

            def prepare(b, u, turn, j, core):
                n = b + 1
                chain = Chain(dve, s.prep_chain, PREP * n)
                if j == 0:
                    if core:
                        dve.wait_ge(s.prep_chain, PREP * n)
                        dve.wait_ge(s.rows_normed, n)
                    chain.mark(dve.tensor_tensor(placed_packed[:, 0, :], x[:, ds(n, 1), :].rearrange("p a d -> p (a d)"),
                                                 positions[:, :], ALU.add))
                    dve.wait_ge((s.loaded0, s.loaded1)[1 - u], 16 * (turn + 1))
                    dve.tensor_tensor(placed_packed[:, 1, :], cn[1 - u][:, :], positions[:, :], ALU.add).then_inc(s.placed, 1)
                elif j == 2:
                    chain.steps = 1
                    dve.wait_ge(s.turned, n + 1)
                    for k in range(4):
                        chain.mark(dve.bn_stats(stats.sums[:, k, :], tiles[k]))
                    chain.join()
                    dve.sem_inc(idle, 1)
                    for k in range(4):
                        chain.mark(dve.bn_aggr(stats.mean_var[:, k, :], stats.sums[:, k, :]))
                    chain.join()
                elif j == 3:
                    chain.steps = 9
                    inverse_root(dve, chain, stats.rstd[:, :], stats.mean_var[:, :, 1], stats.shifted[:, :], stats.work[:, :])
                elif j == 4:
                    chain.steps = 20
                    for k in range(4):
                        ins = dve.tensor_scalar(targets[k], tiles[k], stats.mean_var[:, k, 0:1], stats.rstd[:, k:k + 1],
                                                ALU.subtract, ALU.mult)
                        if k < 3:
                            chain.mark(ins)
                    ins.then_inc(s.rows_normed, 1)

            def window(b, u, core, carry, following, turn):
                for j in range(HN if core or following else PACK * 2 + 3):
                    if core or carry:
                        packed_core(s, b, u, j, core, carry)
                    if following:
                        prepare(b, u, turn, j, core)
                    if carry and j in (5, 6):
                        unit = j - 5
                        chain = Chain(dve, s.heads_chain, HEADS * (b - 1))
                        chain.steps = unit
                        dve.wait_ge(s.sums_turned, b)
                        sums = aux[1 + unit][:, :].rearrange("p (h e) -> p h e", h=HN)
                        chain.link(dve.reciprocal(inverse[:, unit, :].unsqueeze(2), sums[:, :, 8:9]))
                        weighted(unit, heads_out[unit][:, 0:P], sums[:, :, 0:8]).then_inc(s.heads_taken, 1)
                    if carry and j == 10:
                        dve.wait_ge(s.result, b)
                        row = x[:, ds(b - 1, 1), :].rearrange("p a d -> p (a d)")
                        dve.tensor_tensor(row, row, aux[1][:, D:2 * D], ALU.add).then_inc(s.x_added, 1)
                    if following:
                        packed_low(s, b, u, j, dict(q=9, k=12), None, None)
                        if j == 14:
                            dve.wait_ge(s.v_projected, b + 2)
                            dve.tensor_copy(vn[1 - u][:, :, :, 0:8], aux[1][:, 0:D].rearrange("p (c h e) -> p c h e", c=2, h=HN))\
                               .then_inc(s.v_ready, 1)

            over_windows(dve, window)
            dve.wait_ge(s.x_added, B)

        def feed_forward3():
            s = ff3
            steps = SLOTS * (statistics_steps(2) + 1)
            with dve.Fori(0, ROUNDS) as i:
                chain = Chain(dve, s.chain, steps * i)
                for u in range(SLOTS):
                    dve.tensor_scalar(placed[u][:, 0, :], x[:, ds(SLOTS * i + u, 1), :].rearrange("p a d -> p (a d)"), 1.0, None,
                                      ALU.mult).then_inc(s.x_copied, 1)
                for u in range(SLOTS):
                    dve.wait_ge(s.turned, SLOTS * i + u + 1)
                    norm_columns(chain, [bank[u][:, k * P:(k + 1) * P] for k in range(2)],
                                 [norm3[u][:, 0, k * P:(k + 1) * P] for k in range(2)], s.rows_normed)
                    dve.wait_ge(s.rows_normed, SLOTS * i + u + 1)
                for u in range(SLOTS):
                    dve.wait_ge(s.down_ready, SLOTS * i + u + 1)
                    dve.wait_ge(out_stored[u], 16 * (i + 1))
                    dve.scalar_tensor_tensor(result[u][:, :], bank[6 + u][:, 0:D], b3_down[:, 0:1], placed[u][:, 0, :],
                                             ALU.add, ALU.add).then_inc(result_ready, 1)
                dve.wait_ge(result_ready, SLOTS * (i + 1))
            assert chain.steps == steps, (chain.steps, steps)

        dve.sem_inc(x_added, ADD_CREDIT)
        dve.sem_inc(heads_split, GROUP)
        split_context()
        dve.wait_ge(x_loaded, 16 * GROUPS)
        dve.wait_ge(small_loaded, small_count)
        for layer in range(2):
            norm_and_split(layer)
            pairs(layer)
        feed_forward(0, 2)
        layer1()
        layer2(a2s, False)
        layer2(a2c, True)
        feed_forward(2, 5)
        layer3()
        feed_forward3()

    @block.gpsimd
    def _(pool):
        def copy(target, source):
            source, target = (a.rearrange("p a b -> p (a b)") if len(a.shape) == 3 else a for a in (source, target))
            return pool.tensor_tensor(target, source, zero[:, :].broadcast_to([P, source.shape[1]]), ALU.add)

        chain = Chain(pool, ident_ready)
        chain.link(pool.memset(zero[:, :], 0.0))
        chain.link(pool.memset(ident[:, :], 0.0))
        chain.link(pool.affine_select(out=ident[:, :], in_=ident[:, :], compare_op=ALU.not_equal, fill=1.0, base=0,
                                      pattern=[[-1, P]], channel_multiplier=1))
        pool.sem_inc(weights_split, 1)
        steps = 9
        for layer in range(2):
            with pool.Fori(0, PAIRS // 2) as i:
                for slot in range(2):
                    p = PAIRS * layer + 2 * i + slot
                    chain = Chain(pool, split_steps, steps * p)
                    wh, wl = weights_high[slot], weights_low[slot]
                    pool.wait_ge(pair_loaded, 16 * PAIR_LOADS * (p + 1))
                    pool.wait_ge(x_added, 8 * (p - 1) + ADD_CREDIT)
                    chain.mark(copy(columns[slot][:, :, :], pair_columns[:, :, :]))
                    for kind in range(4):
                        chain.link(copy(wh[:, kind, :], pair_weights[:, kind, :]))
                        chain.mark(pool.tensor_tensor(wl[:, kind, :], pair_weights[:, kind, :], wh[:, kind, :].bitcast(F32),
                                                      ALU.subtract))
                    chain.join()
                    pool.tensor_tensor(value_bias[slot][:, 0, :], pair_rows[:, 0, :], pair_rows[:, 1, :], ALU.subtract)\
                        .then_inc(weights_split, 1)
        pool.wait_ge(x_added, 8 * 2 * PAIRS + ADD_CREDIT)
        for size, target in ((8, head_of_8), (16, head_of_16)):
            n = P // size
            chain = Chain(pool, head_steps, 3 * (size // 16))
            chain.link(pool.memset(target[:, :], 1.0))
            chain.link(pool.affine_select(out=target[:, :], in_=target[:, :], compare_op=ALU.is_ge, fill=0.0, base=0,
                                          pattern=[[-size, n]], channel_multiplier=1))
            chain.link(pool.affine_select(out=target[:, :], in_=target[:, :], compare_op=ALU.is_ge, fill=0.0, base=size - 1,
                                          pattern=[[size, n]], channel_multiplier=-1))
        pool.sem_inc(heads_known, 3)

        def spread_queries(s):
            with pool.Fori(0, ROUNDS) as i:
                for u in range(SLOTS):
                    n = SLOTS * i + u
                    for g in range(PACKS):
                        if g % 2 == 0:
                            pool.wait_ge(s.q_low, 2 * n + g // 2 + 1)
                        wide = [P, PACK, D]
                        pool.tensor_tensor(q_spread[u][:, PACK * g:PACK * (g + 1), :],
                                           q_packed[u][:, g:g + 1, :].bitcast(F32).broadcast_to(wide),
                                           part_of_head[:, :].unsqueeze(2).broadcast_to(wide), ALU.mult).then_inc(s.spread, 1)

        spread_queries(n1)
        spread_queries(n3)

    @block.sync
    def _(sp):
        def load_pair(layer, p, q):
            k = str(layer + 1)
            sp.wait_ge(weights_split, p + 1)
            cols = ds(q * D, D)
            for m, name in enumerate("qkv"):
                sp.dma_start(pair_weights[:, m, :].rearrange("p (c n) -> p c n", c=DC),
                             rows(f"L0_xattn_w{name}{k}")[:, :, cols]).then_inc(pair_loaded, 16)
            sp.dma_start(pair_weights[:, 3, :].rearrange("p (h n) -> p h n", h=2),
                         rows(f"L0_xattn_wo{k}")[:, ds(q * 2, 2), :]).then_inc(pair_loaded, 16)
            for m, name in enumerate(("bq", "bk")):
                sp.dma_start(pair_columns[:, m, :], column(f"L0_xattn_{name}{k}")[:, ds(q * 2, 2)],
                             allow_slow_non_contiguous=True).then_inc(pair_loaded, 16)
            for m, name in enumerate(("bias_k", "bias_v")):
                sp.dma_start(pair_columns[:, 2 + m, :], t[f"L0_xattn_{name}{k}"].rearrange("a b h k -> k (a b h)")[:, ds(q * 2, 2)],
                             allow_slow_non_contiguous=True)\
                  .then_inc(pair_loaded, 16)
            sp.dma_start(pair_rows[:, 0, :], t[f"L0_xattn_bv{k}"][cols].partition_broadcast(P)).then_inc(pair_loaded, 16)
            sp.dma_start(pair_rows[:, 1, :], t[f"L0_xattn_bias_v{k}"].rearrange("a b h k -> (a b h k)")[cols].partition_broadcast(P))\
              .then_inc(pair_loaded, 16)

        ctx = t["ctx_2048"]
        for u in range(SLOTS):
            sp.sem_inc(out_stored[u], 16)
        for g in range(2):
            sp.dma_start(ctx_rows[:, g, :, :], ctx[GROUP * g:GROUP * (g + 1)].rearrange("b p d -> p b d")).then_inc(rows_loaded[g], 16)
        for g in range(GROUPS):
            part = slice(GROUP * g, GROUP * (g + 1))
            sp.dma_start(x[:, part, :], t["x"][part].rearrange("b p d -> p b d")).then_inc(x_loaded, 16)
        for target, source in small_loads:
            sp.dma_start(target, source, allow_slow_non_contiguous=True).then_inc(small_loaded, 16)
        for g in range(2, GROUPS):
            sp.wait_ge(rows_turned, DC * (g - 1))
            sp.dma_start(ctx_rows[:, g % 2, :, :], ctx[GROUP * g:GROUP * (g + 1)].rearrange("b p d -> p b d"))\
              .then_inc(rows_loaded[g % 2], 16)
        for layer in range(2):
            with sp.Fori(0, PAIRS) as q:
                load_pair(layer, PAIRS * layer + q, q)
            if layer == 0:
                sp.dma_start(w_up[:, :, :], rows("L0_xattn_w_fc1")).then_inc(weights0_loaded, 16)
                sp.dma_start(w_down[:, :, :], rows("L0_xattn_w_fc2")).then_inc(weights0_loaded, 16)

        sp.wait_ge(x_added, 8 * 2 * PAIRS + ADD_CREDIT)
        sp.wait_ge(weights_split, 2 * PAIRS + 1)
        for target, source in later_loads:
            sp.dma_start(target, source, allow_slow_non_contiguous=True).then_inc(later_loaded, 16)

        def load_rows(s, u, i, mask):
            b = SLOTS * i + u
            sem = (s.loaded0, s.loaded1)[u]
            sp.dma_start(cn[u][:, :], ctx[ds(b, 1)].rearrange("a p d -> p (a d)")).then_inc(sem, 16)
            if mask:
                sp.dma_start(cross_mask[u][:, 0, :], t["mask_Bx1xSxS2_ff1"][ds(b, 1)].rearrange("b a q k -> q (b a k)"))\
                  .then_inc(sem, 16)

        def load_contexts(s, mask, free, before=0):
            for u in range(SLOTS):
                load_rows(s, u, 0, mask)
            with sp.Fori(1, ROUNDS) as i:
                for u in range(SLOTS):
                    sp.wait_ge(free, before + SLOTS * (i - 1) + u + 1)
                    load_rows(s, u, i, mask)

        load_contexts(n1, False, n1.in_ready)
        sp.dma_start(w_up[:, :, :], rows("L2_xattn_w1")).then_inc(weights2_loaded, 16)
        sp.dma_start(w_down[:, :, :], rows("L2_xattn_w2")).then_inc(weights2_loaded, 16)
        sp.wait_ge(n1.x_added, B)
        for target, source in loads2:
            sp.dma_start(target, source).then_inc(attention2_loaded, 16)
        sp.wait_ge(n2.x_added, 1)
        load_contexts(n2, True, n2.x_added, B)
        sp.wait_ge(n2.x_added, 2 * B)
        load_contexts(n3, False, n3.placed)
        with sp.Fori(0, ROUNDS) as i:
            for u in range(SLOTS):
                b = SLOTS * i + u
                sp.wait_ge(result_ready, b + 1)
                sp.dma_start(out[ds(b, 1)].rearrange("a p d -> p (a d)"), result[u][:, :]).then_inc(out_stored[u], 16)
        for u in range(SLOTS):
            sp.wait_ge(out_stored[u], 16 * (ROUNDS + 1))


def position_code():
    pos = np.arange(D, dtype=np.float32)[:, None]
    div = np.exp(np.arange(0, P, 2, dtype=np.float32) * np.float32(-np.log(10000.0) / P)).astype(np.float32)
    angle = (pos * div).astype(np.float32)
    code = np.zeros((D, P), np.float32)
    code[:, 0::2] = np.sin(angle)
    code[:, 1::2] = np.cos(angle)
    return np.ascontiguousarray(code.T)


def kernel(**inputs):
    import concourse.bacc as bacc
    from concourse.bass_utils import run_bass_kernel_spmd as run

    nc = bacc.Bacc("TRN2", target_bir_lowering=False, num_devices=1)
    arrays, tensors = {}, {}
    for name, value in inputs.items():
        a = np.ascontiguousarray(value)
        if a.dtype == np.bool_:
            a = a.view(np.uint8)
        arrays[f"in_{name}"] = a
        tensors[name] = nc.dram_tensor(f"in_{name}", a.shape, mybir.dt.from_np(a.dtype), kind="ExternalInput").ap()
    arrays["in_positions"] = position_code()
    tensors["positions"] = nc.dram_tensor("in_positions", (P, D), F32, kind="ExternalInput").ap()
    out = nc.dram_tensor("out", (B, P, D), F32, kind="ExternalOutput").ap()
    build(nc, tensors, out)
    return run(nc, [arrays], core_ids=[0]).results[0]["out"]
```

```python
from contextlib import ExitStack

import numpy as np

import concourse.bass as bass
from concourse import mybir
from concourse.alu_op_type import AluOpType as ALU

F32 = mybir.dt.float32
F32R = mybir.dt.float32r
I32 = mybir.dt.int32
U8 = mybir.dt.uint8
ACT = mybir.ActivationFunctionType
X_AXIS = mybir.AxisListType.X

P = 128
B = 16
D = 256
DC = D // P
EPS = 1e-5
BANK = 512

H0 = 16
PAIRS = H0 // 2
GROUP = 4
GROUPS = B // GROUP
TOK = GROUP * P
KEYS0 = P + 1
F0 = 1024
SCALE0 = 1.0 / float(np.sqrt(np.float32(P)))
ADD_CREDIT = 9
PAIR_LOADS = 10

SLOTS = 2
ROUNDS = B // SLOTS
HN = 16
NEG_BIG = 10000.0
SCALE1 = float(np.float32(1.0 / np.sqrt(8.0)))
SCALE2 = 0.25
PACK = 4
PACKS = HN // PACK
STEPS = HN // PACK
QUAD = P // PACK
UNITS = D // P
SHIFT = 3 * QUAD
HALF_HEADS = HN // 2


ds = bass.ds


class Statistics:

    def __init__(self, sums, mean_var, rstd, shifted, work):
        self.sums, self.mean_var, self.rstd, self.shifted, self.work = sums, mean_var, rstd, shifted, work


class FeedForward:

    def __init__(self, sem):
        self.chain = sem("ff_chain")
        self.rows_normed = sem("ff_rows_normed")
        self.turned = sem("ff_turned")
        self.weights_high = sem("ff_weights_high")
        self.weights_low = sem("ff_weights_low")
        self.in_ready = sem("ff_in_ready")
        self.in_high = sem("ff_in_high")
        self.in_low = sem("ff_in_low")
        self.up_ready = sem("ff_up_ready")
        self.hidden_ready = sem("ff_hidden_ready")
        self.hidden_high = sem("ff_hidden_high")
        self.hidden_low = sem("ff_hidden_low")
        self.down_ready = sem("ff_down_ready")
        self.x_added = sem("ff_x_added")


class FeedForward3:

    def __init__(self, sem):
        self.chain = sem("ff3_chain")
        self.x_copied = sem("ff3_x_copied")
        self.turned = sem("ff3_turned")
        self.rows_normed = sem("ff3_rows_normed")
        self.turned_back = sem("ff3_turned_back")
        self.in_ready = sem("ff3_in_ready")
        self.up_ready = sem("ff3_up_ready")
        self.hidden_ready = sem("ff3_hidden_ready")
        self.down_ready = sem("ff3_down_ready")


class Masked:

    def __init__(self, sem, name):
        self.norm_chain = sem(f"{name}_norm_chain")
        self.mask_chain = sem(f"{name}_mask_chain")
        self.heads_chain = sem(f"{name}_heads_chain")
        self.loaded = [sem(f"{name}_loaded{u}") for u in range(SLOTS)]
        self.mask_loaded = [sem(f"{name}_mask_loaded{u}") for u in range(SLOTS)]
        self.rows_normed = sem(f"{name}_rows_normed")
        self.turned = sem(f"{name}_turned")
        self.in_ready = sem(f"{name}_in_ready")
        self.projected = sem(f"{name}_projected")
        self.values = sem(f"{name}_values")
        self.qk_ready = sem(f"{name}_qk_ready")
        self.spread = sem(f"{name}_spread")
        self.v_ready = sem(f"{name}_v_ready")
        self.scores = sem(f"{name}_scores")
        self.masked = sem(f"{name}_masked")
        self.mask_added = sem(f"{name}_mask_added")
        self.max_ready = sem(f"{name}_max_ready")
        self.exp_ready = sem(f"{name}_exp_ready")
        self.probs_turned = sem(f"{name}_probs_turned")
        self.probs_copied = sem(f"{name}_probs_copied")
        self.sums = sem(f"{name}_sums")
        self.sums_copied = sem(f"{name}_sums_copied")
        self.sums_turned = sem(f"{name}_sums_turned")
        self.heads_taken = sem(f"{name}_heads_taken")
        self.heads_turned = sem(f"{name}_heads_turned")
        self.heads_copied = sem(f"{name}_heads_copied")
        self.result = sem(f"{name}_result")
        self.x_added = sem(f"{name}_x_added")


class Packed:

    def __init__(self, sem, name):
        self.prep_chain = [sem(f"{name}_prep_chain{k}") for k in range(2)]
        self.values_chain = sem(f"{name}_values_chain")
        self.heads_chain = [sem(f"{name}_heads_chain{k}") for k in range(2)]
        self.loaded = [sem(f"{name}_loaded{u}") for u in range(SLOTS)]
        self.in_ready = sem(f"{name}_in_ready")
        self.q_projected = sem(f"{name}_q_projected")
        self.k_projected = sem(f"{name}_k_projected")
        self.v_projected = sem(f"{name}_v_projected")
        self.q_high = sem(f"{name}_q_high")
        self.k_high = sem(f"{name}_k_high")
        self.q_low = sem(f"{name}_q_low")
        self.k_low = sem(f"{name}_k_low")
        self.spread = sem(f"{name}_spread")
        self.v_taken = sem(f"{name}_v_taken")
        self.v_ready = sem(f"{name}_v_ready")
        self.scores = sem(f"{name}_scores")
        self.max_ready = sem(f"{name}_max_ready")
        self.max_turned = sem(f"{name}_max_turned")
        self.max_high = sem(f"{name}_max_high")
        self.max_low = sem(f"{name}_max_low")
        self.max_moved = sem(f"{name}_max_moved")
        self.shifted = sem(f"{name}_shifted")
        self.exp_ready = sem(f"{name}_exp_ready")
        self.sums = sem(f"{name}_sums")
        self.sums_copied = sem(f"{name}_sums_copied")
        self.sums_turned = sem(f"{name}_sums_turned")
        self.heads_taken = sem(f"{name}_heads_taken")
        self.result = sem(f"{name}_result")
        self.x_added = sem(f"{name}_x_added")


class Schedule:

    def __init__(self, turned, q, q_side, k, v):
        self.turned, self.q, self.q_side, self.k, self.v = turned, q, q_side, k, v


SCHEDULE1 = Schedule(turned=(3, 3), q=(7, 11), q_side=(0, 1), k=(12, 15), v=10)
SCHEDULE3 = Schedule(turned=(3, 5), q=(12, 14), q_side=(1, 0), k=(11, 15), v=7)
STD_PARTS = 4
PREP3 = 4 + 4 + 3
RSTD_STEPS = 2 + 3 * 4
SPREAD = 2
MAXIMA_TURNED = (11, 3)


class Chain:

    def __init__(self, engine, sem, base=0):
        self.engine, self.sem, self.base, self.steps = engine, sem, base, 0

    def mark(self, instruction):
        self.steps += 1
        instruction.then_inc(self.sem, 1)

    def join(self):
        self.engine.wait_ge(self.sem, self.base + self.steps)

    def link(self, instruction):
        self.mark(instruction)
        self.join()


NEWTON = 3
ROOT_STEPS = 2 + 3 * NEWTON


def inverse_root(dve, chain, out, var, shifted, work):
    chain.link(dve.tensor_scalar(shifted, var, EPS, None, ALU.add))
    chain.link(dve.tensor_scalar(out.bitcast(I32), shifted.bitcast(I32), -0.5, 1597463007.0,
                                 ALU.mult, ALU.add))
    for _ in range(NEWTON):
        chain.link(dve.scalar_tensor_tensor(work, out, -0.5, out, ALU.mult, ALU.mult))
        chain.link(dve.tensor_tensor(work, work, shifted, ALU.mult))
        chain.link(dve.scalar_tensor_tensor(out, work, 1.5, out, ALU.add, ALU.mult))


def row_statistics(dve, chain, rows, stats, idle):
    n = len(rows)
    for k, row in enumerate(rows):
        chain.mark(dve.bn_stats(stats.sums[:, k, :], row))
    chain.join()
    dve.sem_inc(idle, 1)
    for k in range(n):
        chain.mark(dve.bn_aggr(stats.mean_var[:, k, :], stats.sums[:, k, :]))
    chain.join()
    inverse_root(dve, chain, stats.rstd[:, 0:n], stats.mean_var[:, 0:n, 1], stats.shifted[:, 0:n],
                 stats.work[:, 0:n])


def statistics_steps(n):
    return 2 * n + ROOT_STEPS


def pair_number(layer, pair, k):
    return PAIRS * layer + pair + k // GROUPS


def over_groups(engine, window):
    window(-1, -1, 0, False, False, True)
    window(0, 0, 0, True, False, True)
    span = 2 * GROUPS
    with engine.Fori(0, PAIRS // 2 - 1) as i:
        for k in range(1, span + 1):
            window(span * i + k, k, 2 * i, True, True, True)
    last = PAIRS * GROUPS
    for k in range(1, span):
        window(last - span + k, k, PAIRS - 2, True, True, k + 1 < span)
    window(last, span, PAIRS - 2, False, True, False)


def over_steps(engine, window):
    window(-2, 0, False, False, False, True, True, 0, 0)
    window(-1, 1, False, False, True, True, True, 0, 0)
    window(0, 0, True, False, True, True, True, 0, 1)
    with engine.Fori(0, B // SLOTS - 2) as i:
        window(SLOTS * i + 1, 1, True, True, True, True, True, i + 1, i + 1)
        window(SLOTS * i + 2, 0, True, True, True, True, True, i + 1, i + 2)
    window(B - 3, 1, True, True, True, True, False, B // 2 - 1, B // 2 - 1)
    window(B - 2, 0, True, True, True, False, False, B // 2 - 1, 0)
    window(B - 1, 1, True, True, False, False, False, 0, 0)
    window(B, 0, False, True, False, False, False, 0, 0)


def packed_scores(slot, j):
    return (j + slot) % 3


def scores_between(slot, j):
    return 2 if slot == 0 and j < 2 else 3


def after(engine, sem, count):
    if not isinstance(count, int) or count > 0:
        engine.wait_ge(sem, count)


def build(nc, t, out):
    with ExitStack() as outer:
        program(nc, t, out, outer)


def program(nc, t, out, outer):
    def sem(name):
        return outer.enter_context(nc.semaphore(name))

    def sbuf(scope, name, shape, dtype=F32):
        return scope.enter_context(nc.sbuf_tensor(name, shape, dtype))

    bank = [outer.enter_context(nc.psum_tensor(f"bank{k}", [P, BANK], F32)) for k in range(8)]

    x = sbuf(outer, "x", [P, B, D])
    zero = sbuf(outer, "zero", [P, 1])
    ident = sbuf(outer, "ident", [P, P])
    norm_rows = sbuf(outer, "norm_rows", [P, SLOTS, D])
    stats = Statistics(
        sums=sbuf(outer, "stat_sums", [P, 4, 6]), mean_var=sbuf(outer, "mean_var", [P, 4, 2]),
        rstd=sbuf(outer, "rstd", [P, 4]), shifted=sbuf(outer, "stat_shifted", [P, 4]),
        work=sbuf(outer, "stat_work", [P, 4]))
    norms = ["L0_xattn_ln1", "L0_xattn_ln2", "L0_xattn_ln_mlp", "L2_xattn_ln1", "L2_xattn_ln2", "L2_xattn_ln3"]
    norm_scale = sbuf(outer, "norm_scale", [P, len(norms), DC])
    norm_offset = sbuf(outer, "norm_offset", [P, len(norms), DC])
    row_biases = ["L0_xattn_bo1", "L0_xattn_bo2", "L0_xattn_b_fc2", "L2_xattn_b_ao", "L2_xattn_b_co", "L2_xattn_b2"]
    row_bias = sbuf(outer, "row_bias", [P, len(row_biases), D])
    w_up = sbuf(outer, "w_up", [P, DC, F0])
    w_down = sbuf(outer, "w_down", [P, F0 // P, D])
    b_up = sbuf(outer, "b_up", [P, 2, F0 // P])
    hidden_in = sbuf(outer, "hidden_in", [P, DC, SLOTS * P])
    hidden = sbuf(outer, "hidden", [P, F0 // P, SLOTS * P])

    with ExitStack() as scope0:
        normed_high = sbuf(scope0, "wide_normed_high", [P, DC, B * P], F32R)
        normed_low = sbuf(scope0, "wide_normed_low", [P, DC, B * P], F32R)
        ctx_high = sbuf(scope0, "wide_ctx_high", [P, DC, B * P], F32R)
        ctx_low = sbuf(scope0, "wide_ctx_low", [P, DC, B * P], F32R)
        normed = sbuf(scope0, "wide_normed", [P, DC, TOK])
        wide_rows = sbuf(scope0, "wide_rows", [P, GROUP, D])
        pair_weights = sbuf(scope0, "wide_pair_weights", [P, 4, DC * D])
        pair_columns = sbuf(scope0, "wide_pair_columns", [P, 4, 2])
        pair_rows = sbuf(scope0, "wide_pair_rows", [P, 2, D])
        weights_high = [sbuf(scope0, f"wide_weights_high{k}", [P, 4, DC * D], F32R) for k in range(2)]
        weights_low = [sbuf(scope0, f"wide_weights_low{k}", [P, 4, DC * D], F32R) for k in range(2)]
        columns = [sbuf(scope0, f"wide_columns{k}", [P, 4, 2]) for k in range(2)]
        value_bias = [sbuf(scope0, f"wide_value_bias{k}", [P, 1, D]) for k in range(2)]
        q0 = [sbuf(scope0, f"wide_q0{k}", [P, 2, TOK]) for k in range(2)]
        k0 = [sbuf(scope0, f"wide_k0{k}", [P, 2, GROUP, KEYS0]) for k in range(2)]
        v0 = [sbuf(scope0, f"wide_v0{k}", [P, GROUP, D]) for k in range(2)]
        neg_max0 = sbuf(scope0, "wide_neg_max0", [P, GROUP, 2])
        sums0 = sbuf(scope0, "wide_sums0", [P, GROUP, 2])
        inverse0 = sbuf(scope0, "wide_inverse0", [P, GROUP, 2])
        probs0 = sbuf(scope0, "wide_probs0", [P, GROUP, 2, KEYS0])
        probs_t0 = sbuf(scope0, "wide_probs_t0", [P, GROUP, 2, P])
        with ExitStack() as scope_rows:
            ctx_rows = sbuf(scope_rows, "wide_ctx_rows", [P, 2, GROUP, D])
        heads_high = sbuf(scope0, "wide_heads_high", [P, 2, GROUP, P], F32R)
        heads_low = sbuf(scope0, "wide_heads_low", [P, 2, GROUP, P], F32R)

    with ExitStack() as scope1:
        head_of_8 = sbuf(scope1, "head_of_8", [P, HN])
        head_of_16 = sbuf(scope1, "head_of_16", [P, HN // 2])
        vn = [sbuf(scope1, f"vn{u}", [P, UNITS, HN, QUAD]) for u in range(SLOTS)]
        cn = [sbuf(scope1, f"cn{u}", [P, D]) for u in range(SLOTS)]
        maxima = [sbuf(scope1, f"maxima{u}", [P, HN, UNITS]) for u in range(SLOTS)]
        max_high = [sbuf(scope1, f"max_high{k}", [HALF_HEADS * UNITS, P], F32R) for k in range(2)]
        max_low = [sbuf(scope1, f"max_low{k}", [HALF_HEADS * UNITS, P], F32R) for k in range(2)]
        neg_max = [sbuf(scope1, f"neg_max{k}", [P, 4]) for k in range(2)]
        probs = [sbuf(scope1, f"probs{k}", [P, BANK]) for k in range(2)]
        probs_t = [sbuf(scope1, f"probs_t{k}", [P, BANK]) for k in range(8)]
        all_ones = probs[0][:, 0:P]
        ones = sbuf(scope1, "ones", [P, HN])
        inverse = sbuf(scope1, "inverse", [P, 2, HN])
        heads_out = [sbuf(scope1, f"heads_out{k}", [P, D]) for k in range(2)]
        heads_t = [sbuf(scope1, f"heads_t{u}", [P, D]) for u in range(SLOTS)]
        part_of_head = sbuf(scope1, "part_of_head", [P, PACK])
        wq_packed = sbuf(scope1, "wq_packed", [P, PACKS, PACK, QUAD])
        wk_packed = sbuf(scope1, "wk_packed", [P, PACKS, PACK, QUAD])
        q_packed = [sbuf(scope1, f"q_packed{u}", [P, PACKS, D], F32R) for u in range(SLOTS)]
        k_packed = [sbuf(scope1, f"k_packed{u}", [P, PACKS, D], F32R) for u in range(SLOTS)]
        keys_in = [sbuf(scope1, f"keys_in{u}", [P, D]) for u in range(SLOTS)]
        sums_copy = sbuf(scope1, "sums_copy", [P, PACKS, D])
        wv1 = sbuf(scope1, "wv1", [P, P])
        bias1 = sbuf(scope1, "bias1", [P, 2, PACKS])
        bq1 = sbuf(scope1, "bq1", [P, PACKS])
        bv1 = sbuf(scope1, "bv1", [P, 1, P])
        mask_keys = sbuf(scope1, "mask_keys", [P, B, 2])
        valid = sbuf(scope1, "valid", [P, B])
        key_mean = sbuf(scope1, "key_mean", [P, 1])
        scratch1 = sbuf(scope1, "scratch1", [P, D])
        scratch_values = sbuf(scope1, "scratch_values", [P, D])
        row_sums = sbuf(scope1, "row_sums", [P, 6, B])
        x_stats = sbuf(scope1, "x_stats", [P, B, 6])
        x_moments = sbuf(scope1, "x_moments", [P, B, 2])
        b_qk2 = sbuf(scope1, "b_qk2", [P, 2, 2, DC])
        b_q2 = sbuf(scope1, "b_q2", [P, 2, DC])
        b_v2 = sbuf(scope1, "b_v2", [P, 2, D])
        self_mask = sbuf(scope1, "self_mask", [P, 2, P])
        positions = sbuf(scope1, "positions", [P, D])
        w3 = sbuf(scope1, "w3", [P, 4, P])
        ln3 = sbuf(scope1, "ln3", [P, 6])
        w3_up = sbuf(scope1, "w3_up", [P, D])
        w3_down = sbuf(scope1, "w3_down", [P, 2, P])
        b3_up = sbuf(scope1, "b3_up", [P, 2])
        b3_down = sbuf(scope1, "b3_down", [P, 1])
        with ExitStack() as scope_raw:
            w_rows1 = sbuf(scope_raw, "w_rows1", [P, 3, P])
            mask_own_bytes = sbuf(scope_raw, "mask_own_bytes", [B, D], U8)
            mask_own = sbuf(scope_raw, "mask_own", [B, D])
            mask_bytes = sbuf(scope_raw, "mask_bytes", [P, B, D], U8)
            hidden_in_high = sbuf(scope_raw, "hidden_in_high", [P, DC, SLOTS * P], F32R)
            hidden_in_low = sbuf(scope_raw, "hidden_in_low", [P, DC, SLOTS * P], F32R)
        with ExitStack() as scope_l2:
            w_qkv = sbuf(scope_l2, "w_qkv", [P, 2, DC, 3 * D])
            w_out2 = sbuf(scope_l2, "w_out2", [P, 2, DC, D])
            km = [sbuf(scope_l2, f"km{u}", [P, HN * P]) for u in range(SLOTS)]
        with ExitStack() as scope_spread:
            q_spread = [sbuf(scope_spread, f"q_spread{u}", [P, HN, D], F32R) for u in range(SLOTS)]
            with ExitStack() as scope_early:
                mean_t = sbuf(scope_early, "mean_t", [P, B, D])
                std_t = sbuf(scope_early, "std_t", [P, B, D])
                mask_rows = sbuf(scope_early, "mask_rows", [P, B, D])
            with ExitStack() as scope_ff:
                w_up_low = sbuf(scope_ff, "w_up_low", [P, DC, F0], F32R)
                w_down_low = sbuf(scope_ff, "w_down_low", [P, F0 // P, D], F32R)
                hidden_high = sbuf(scope_ff, "hidden_high", [P, F0 // P, SLOTS * P], F32R)
                hidden_low = sbuf(scope_ff, "hidden_low", [P, F0 // P, SLOTS * P], F32R)
            with ExitStack() as scope_late:
                qn = [sbuf(scope_late, f"qn{u}", [P, D]) for u in range(SLOTS)]
                kn = [sbuf(scope_late, f"kn{u}", [P, D]) for u in range(SLOTS)]
                rows_t = [sbuf(scope_late, f"rows_t{u}", [P, DC, P]) for u in range(SLOTS)]
                cn_t = [sbuf(scope_late, f"cn_t{u}", [P, DC, P]) for u in range(SLOTS)]
                cross_mask = [sbuf(scope_late, f"cross_mask{u}", [P, 2, P]) for u in range(SLOTS)]
                scores_masked = [sbuf(scope_late, f"scores_masked{k}", [P, BANK]) for k in range(2)]
                norm_packed = sbuf(scope_late, "norm_packed", [P, 2, D])
                placed_packed = sbuf(scope_late, "placed_packed", [P, 2, D])
                rows3 = sbuf(scope_late, "rows3", [P, SLOTS, D])
                norm3 = sbuf(scope_late, "norm3", [P, SLOTS, D])
                hidden3_in = sbuf(scope_late, "hidden3_in", [P, SLOTS * D])
                hidden3 = sbuf(scope_late, "hidden3", [P, 2, SLOTS * D])
                result = sbuf(scope_late, "result", [P, SLOTS, D])


    w_up_high = q_spread[1][:, 0:HN // 2, :].rearrange("p (c a) d -> p c (a d)", c=DC)
    w_down_high = q_spread[1][:, HN // 2:HN, :]
    hidden_pairs = F0 // P // 2
    weight_quarters = [[w[:, c, :] for w in (w_up, w_up_high, w_up_low)] for c in range(DC)]
    weight_quarters += [[w[:, k * hidden_pairs:(k + 1) * hidden_pairs, :].rearrange("p f d -> p (f d)")
                         for w in (w_down, w_down_high, w_down_low)] for k in range(2)]

    idle = sem("idle")
    x_loaded = [sem(f"x_loaded{g}") for g in range(GROUPS)]
    first_loaded = sem("first_loaded")
    small_loaded = sem("small_loaded")
    weights0_loaded = sem("weights0_loaded")
    ident_ready = sem("ident_ready")
    rows_loaded = [sem(f"rows_loaded{k}") for k in range(2)]
    rows_turned = sem("rows_turned")
    ctx_high_ready = sem("ctx_high_ready")
    ctx_low_ready = sem("ctx_low_ready")
    split_chain = sem("split_chain")
    rows_normed = sem("rows_normed")
    normed_turned = sem("normed_turned")
    normed_ready = sem("normed_ready")
    normed_high_ready = sem("normed_high_ready")
    normed_low_ready = sem("normed_low_ready")
    pair_loaded = sem("pair_loaded")
    split_steps = sem("split_steps")
    weights_split = sem("weights_split")
    qk_ready = sem("qk_ready")
    q_copied = sem("q_copied")
    k_copied = sem("k_copied")
    scores_ready = sem("scores_ready")
    v_ready = sem("v_ready")
    v_copied = sem("v_copied")
    max_ready = sem("max_ready")
    exp_ready = sem("exp_ready")
    softmax_chain = sem("softmax_chain")
    probs_ready = sem("probs_ready")
    probs_turned = sem("probs_turned")
    probs_copied = sem("probs_copied")
    heads_ready = sem("heads_ready")
    heads_high_ready = sem("heads_high_ready")
    heads_split = sem("heads_split")
    out_ready = sem("out_ready")
    x_added = sem("x_added")

    later_loaded = sem("later_loaded")
    weights2_loaded = sem("weights2_loaded")
    attention2_loaded = sem("attention2_loaded")
    masks_ready = sem("masks_ready")
    masks_turned = sem("masks_turned")
    head_steps = sem("head_steps")
    setup_chain = sem("setup_chain")
    x_masked = sem("x_masked")
    moments_masked = sem("moments_masked")
    x_measured = sem("x_measured")
    std_ready = sem("std_ready")
    out_stored = sem("out_stored")
    result_ready = sem("result_ready")
    ff = FeedForward(sem)
    ff3 = FeedForward3(sem)
    pk = Packed(sem, "pk")
    n2 = Masked(sem, "n2")
    pk.placed = sem("pk_placed")
    pk.turned = sem("pk_turned")
    pk.rstd_ready = sem("pk_rstd_ready")
    pk.rows_normed = sem("pk_rows_normed")
    pk.turned_back = sem("pk_turned_back")
    pk.heads_turned = sem("pk_heads_turned")
    pk.heads_copied = sem("pk_heads_copied")
    packed_ready = sem("packed_ready")

    score_bank = [bank[0], bank[1]]
    turn_bank = [bank[2], bank[3]]
    project_bank = [bank[0], bank[1]]
    wide_scores = [bank[2], bank[3]]
    wide_heads = [bank[4], bank[5]]
    wide_turned = bank[6]
    out_bank = bank[7]
    head_scores = [bank[0], bank[1], bank[2]]
    shifted_bank = [bank[3], bank[4]]
    sum_bank = bank[5][:, 0:D]
    spare = bank[5][:, D:2 * D]
    side = [bank[6], bank[7]]
    aux = [bank[5], bank[6], bank[7]]
    step_sums = [bank[3], bank[4]]


    def column(name):
        return t[name].rearrange("(c p) -> p c", p=P)

    small_loads = []
    for k, name in enumerate(norms):
        part = ("_scale", "_offset") if name.startswith("L0") else ("_s", "_b")
        small_loads += [(norm_scale[:, k, :], column(name + part[0])), (norm_offset[:, k, :], column(name + part[1]))]
    for k, name in enumerate(row_biases):
        small_loads.append((row_bias[:, k, :], t[name].partition_broadcast(P)))
    small_loads += [(b_up[:, 0, :], column("L0_xattn_b_fc1")), (b_up[:, 1, :], column("L2_xattn_b1"))]
    first_loads, small_loads = small_loads[:2], small_loads[2:]
    first_count, small_count = 16 * len(first_loads), 16 * len(small_loads)

    def rows(name):
        return t[name].rearrange("(c p) n -> p c n", p=P)

    def row(name):
        return t[name].partition_broadcast(P)

    later_loads = [(w_rows1[:, k, :], t[f"L1_xattn_W{n}"]) for k, n in enumerate("qkv")]
    later_loads += [(bias1[part * QUAD:(part + 1) * QUAD, k, :], t[f"L1_xattn_b{n}"].rearrange("(g r) -> r g", r=QUAD))
                    for k, n in enumerate("qk") for part in range(PACK)]
    later_loads += [
        (bv1[:, 0, :], row("L1_xattn_bv")),
        (mask_own_bytes[:, :], t["mask_Bx1x2048_bf1"].rearrange("b a k -> (b a) k")),
        (mask_bytes[:, :, :].rearrange("p b k -> p (b k)"), t["mask_Bx1x2048_bf1"].rearrange("b a k -> (b a k)").partition_broadcast(P)),
        (b_qk2[:, 0, :, :].rearrange("p a c -> p (a c)"), column("L2_xattn_b_qkv")[:, 0:2 * DC]),
        (b_qk2[:, 1, 0, :], column("L2_xattn_b_q")),
        (b_qk2[:, 1, 1, :], column("L2_xattn_b_kv")[:, 0:DC]),
        (b_v2[:, 0, :], t["L2_xattn_b_qkv"][2 * D:3 * D].partition_broadcast(P)),
        (b_v2[:, 1, :], t["L2_xattn_b_kv"][D:2 * D].partition_broadcast(P)),
        (self_mask[:, 0, :], t["mask_1x1xSxS2_fc1"].rearrange("a b q k -> (a b q) k")),
        (positions[:, :], t["positions"]),
        (w3_up[:, :], t["L3_xattn_W1"]),
        (w3_down[:, :, :], rows("L3_xattn_W2")),
        (b3_up[:, :], column("L3_xattn_b1")),
        (b3_down[:, :], column("L3_xattn_b2")),
    ]
    later_loads += [(w3[:, k, :], t[f"L3_xattn_W{n}"]) for k, n in enumerate("qkvo")]
    later_loads += [(ln3[:, k:k + 1], column(f"L3_xattn_{n}")) for k, n in enumerate(
        ("ln_q_g", "ln_q_b", "ln_kv_g", "ln_kv_b", "ffn_ln_g", "ffn_ln_b"))]
    later_count = 16 * len(later_loads)
    loads2 = [
        (w_qkv[:, 0, :, :], rows("L2_xattn_w_qkv")),
        (w_qkv[:, 1, :, 0:D], rows("L2_xattn_w_q")),
        (w_qkv[:, 1, :, D:3 * D], rows("L2_xattn_w_kv")),
        (w_out2[:, 0, :, :], rows("L2_xattn_w_ao")),
        (w_out2[:, 1, :, :], rows("L2_xattn_w_co")),
    ]
    loads2_count = 16 * len(loads2)


    block = outer.enter_context(nc.Block())

    @block.tensor
    def _(pe):
        def product3(acc, wh, wl, mh, ml, start, stop):
            pe.matmul(acc, wh, mh, start=start, stop=False)
            pe.matmul(acc, wh, ml, start=False, stop=False)
            return pe.matmul(acc, wl, mh, start=False, stop=stop)

        def turn_context(g):
            if g == 0:
                pe.wait_ge(ident_ready, 3)
            pe.wait_ge(rows_loaded[g % 2], 16 * (g // 2 + 1))
            if g >= 2:
                pe.wait_ge(ctx_low_ready, DC * (g - 1))
            for c in range(DC):
                for b in range(GROUP):
                    last = pe.transpose(bank[2 * (g % 2) + c][:, b * P:(b + 1) * P],
                                        ctx_rows[:, g % 2, b, c * P:(c + 1) * P], ident[:, :])
                last.then_inc(rows_turned, 1)

        def turn_normed(layer, g):
            r = GROUPS * layer + g
            pe.wait_ge(rows_normed, GROUP * (r + 1))
            for c in range(DC):
                if g >= 2:
                    pe.wait_ge(normed_ready, DC * (r - 2) + c + 1)
                for b in range(GROUP):
                    last = pe.transpose(bank[4 + 2 * (g % 2) + c][:, b * P:(b + 1) * P], wide_rows[:, b, c * P:(c + 1) * P], ident[:, :])
                last.then_inc(normed_turned, 1)

        def norm_and_split(layer):
            if layer == 0:
                turn_context(0)
            for g in range(GROUPS):
                if layer == 0 and g + 1 < GROUPS:
                    turn_context(g + 1)
                turn_normed(layer, g)

        def pairs(layer):
            pe.wait_ge(normed_low_ready, DC * GROUPS * (layer + 1))
            if layer == 0:
                pe.wait_ge(ctx_low_ready, DC * GROUPS)

            def project(gg, k, pair, piece):
                kind, half = piece // 2, piece % 2
                slot, n = k // GROUPS % 2, k % GROUPS
                wh, wl = weights_high[slot], weights_low[slot]
                acc = project_bank[half]
                tok = slice(n * TOK, (n + 1) * TOK)
                if piece == 0 and n == 0:
                    pe.wait_ge(weights_split, pair + 2)
                if kind == 0:
                    if not isinstance(gg, int) or gg > 0:
                        pe.wait_ge(v_copied, 2 * gg - 1 + half)
                else:
                    pe.wait_ge((q_copied, k_copied)[kind - 1], 2 * gg + half + 1)
                if kind < 2:
                    mh, ml = ((normed_high, normed_low), (ctx_high, ctx_low))[kind]
                    for c in range(DC):
                        w = slice(c * D + half * P, c * D + (half + 1) * P)
                        last = product3(acc[:, :], wh[:, kind, w], wl[:, kind, w], mh[:, c, tok], ml[:, c, tok], c == 0, c == DC - 1)
                    last.then_inc(qk_ready, 1)
                else:
                    for m in range(2):
                        b = 2 * half + m
                        keys = slice(n * TOK + b * P, n * TOK + (b + 1) * P)
                        for c in range(DC):
                            w = slice(c * D, (c + 1) * D)
                            last = product3(acc[:, m * D:(m + 1) * D], ctx_high[:, c, keys], ctx_low[:, c, keys],
                                            wh[:, 2, w], wl[:, 2, w], c == 0, c == DC - 1)
                    last.then_inc(v_ready, 1)

            def window(g, k, pair, core, carry, following):
                gg = g + PAIRS * GROUPS * layer
                for b in range(GROUP):
                    ss = GROUP * gg + b
                    if core:
                        if b == 0:
                            pe.wait_ge(q_copied, 2 * gg + 2)
                            pe.wait_ge(k_copied, 2 * gg + 2)
                        if carry or layer or b >= 2:
                            pe.wait_ge(exp_ready, ss - 1)
                        for h in range(2):
                            last = pe.matmul(wide_scores[b % 2][:, h * KEYS0:(h + 1) * KEYS0], q0[k % 2][:, h, b * P:(b + 1) * P],
                                             k0[k % 2][:, h, b, :], start=True, stop=True)
                        last.then_inc(scores_ready, 1)
                    turns = b > 0 and core or b == 0 and carry
                    a, parity = (b - 1) % GROUP, (k if b else k - 1) % 2
                    if turns:
                        pe.wait_ge(probs_ready, ss)
                        if carry or layer or b >= 2:
                            pe.wait_ge(probs_copied, ss - 1)
                        for h in range(2):
                            last = pe.transpose(wide_turned[:, h * P:(h + 1) * P], probs0[:, a, h, 0:P], ident[:, :])
                        last.then_inc(probs_turned, 1)
                    if following and b != 2:
                        project(gg + 1, k + 1, pair_number(layer, pair, k + 1), (0, 2, None, 5)[b])
                    if following and b == 2:
                        project(gg + 1, k + 1, pair_number(layer, pair, k + 1), 3)
                    if turns:
                        pe.wait_ge(probs_copied, ss)
                        pe.wait_ge(v_copied, 2 * gg + (b + 1) // 2)
                        if carry or layer or b >= 3:
                            pe.wait_ge(heads_split, ss - 2 + GROUP)
                        for h in range(2):
                            last = pe.matmul(wide_heads[a % 2][:, h * P:(h + 1) * P], v0[parity][:, a, h * P:(h + 1) * P],
                                             probs_t0[:, a, h, :], start=True, stop=True)
                        last.then_inc(heads_ready, 1)
                    if b >= 2 and core or b < 2 and carry:
                        a = (b - 2) % GROUP
                        slot = (k if b >= 2 else k - 1) // GROUPS % 2
                        pe.wait_ge(heads_split, ss - 1 + GROUP)
                        if a % 2 == 0 and (carry or layer):
                            pe.wait_ge(x_added, 2 * gg + b // 2 - 1 + ADD_CREDIT)
                        for h in range(2):
                            w = slice(h * D, (h + 1) * D)
                            last = product3(out_bank[:, a % 2 * D:(a % 2 + 1) * D], heads_high[:, h, a, :], heads_low[:, h, a, :],
                                            weights_high[slot][:, 3, w], weights_low[slot][:, 3, w], h == 0, h == 1)
                        if a % 2:
                            last.then_inc(out_ready, 1)
                    if following and b in (0, 2):
                        project(gg + 1, k + 1, pair_number(layer, pair, k + 1), (1, None, 4)[b])

            over_groups(pe, window)

        def feed_forward(which):
            s = ff

            def turn(r):
                pe.wait_ge(s.rows_normed, SLOTS * (r + 1))
                for c in range(DC):
                    for u in range(SLOTS):
                        last = pe.transpose(bank[0][:, (SLOTS * c + u) * P:(SLOTS * c + u + 1) * P],
                                            norm_rows[:, u, c * P:(c + 1) * P], ident[:, :])
                last.then_inc(s.turned, 1)

            def products(r, more, begins=False):
                pe.wait_ge(s.in_low, r + 1)
                if begins:
                    pe.wait_ge(s.weights_low, len(weight_quarters) * which + 2)
                for f in range(F0 // P):
                    for c in range(DC):
                        w = slice(f * P, (f + 1) * P)
                        last = product3(bank[1 + f // 2][:, (f % 2) * D:(f % 2 + 1) * D], w_up_high[:, c, w], w_up_low[:, c, w],
                                        hidden_in_high[:, c, :], hidden_in_low[:, c, :], c == 0, c == DC - 1)
                    if f % 2:
                        last.then_inc(s.up_ready, 1)
                if more:
                    turn(r + 1)
                if begins:
                    pe.wait_ge(s.weights_low, len(weight_quarters) * (which + 1))
                after(pe, s.x_added, r)
                for u in range(SLOTS):
                    for f in range(F0 // P):
                        if u == 0 and f % 2 == 0:
                            pe.wait_ge(s.hidden_low, hidden_pairs * r + f // 2 + 1)
                        tok = slice(u * P, (u + 1) * P)
                        last = product3(bank[5][:, u * D:(u + 1) * D], hidden_high[:, f, tok], hidden_low[:, f, tok],
                                        w_down_high[:, f, :], w_down_low[:, f, :], f == 0, f == F0 // P - 1)
                last.then_inc(s.down_ready, 1)

            first = ROUNDS * which
            turn(first)
            products(first, True, True)
            with pe.Fori(1, ROUNDS - 1) as i:
                products(first + i, True)
            products(first + ROUNDS - 1, False)

        def packed_window(third, prepare, finish, values, at):
            s = pk

            def window(b, u, core, carry, following, ahead, further, next_turn, ahead_turn):
                n = b + B * third

                def turn_maxima(m, half, source):
                    pe.wait_ge(s.max_ready, HN * m + HALF_HEADS * (half + 1))
                    pe.transpose(spare[0:HALF_HEADS * UNITS, half * P:(half + 1) * P],
                                 source[:, half * HALF_HEADS:(half + 1) * HALF_HEADS, :].rearrange("p h a -> p (h a)"), ident[:, :])\
                      .then_inc(s.max_turned, 1)

                def project(name, half, bank):
                    packed = wq_packed if name == "q" else wk_packed
                    source = x[:, ds(b + 2, 1), :].rearrange("p a d -> p (a d)") if name == "q" else keys_in[u][:, :]
                    for k in range(2):
                        last = pe.matmul(side[bank][:, k * D:(k + 1) * D], packed[:, 2 * half + k, :, :].rearrange("p a r -> p (a r)"),
                                         source, start=True, stop=True)
                    last.then_inc(s.q_projected if name == "q" else s.k_projected, 1)

                def turn_sums(unit):
                    pe.wait_ge(s.sums_copied, PACKS * n)
                    if unit and third:
                        pe.wait_ge(s.heads_taken, UNITS * (n - 1) + 1)
                    elif following:
                        pe.wait_ge(s.k_low, 2 * (n + 1) + 1 + max(unit, third))
                    elif unit or third:
                        pe.wait_ge(s.x_added, n - 1)
                    elif core:
                        pe.wait_ge(s.v_ready, n + 1)
                    else:
                        pe.wait_ge(s.heads_taken, UNITS * (n - 1))
                    for g in range(PACKS):
                        last = pe.transpose(side[max(unit, third)][:, g * P:(g + 1) * P], sums_copy[:, g, unit * P:(unit + 1) * P],
                                            ident[:, :])
                    last.then_inc(s.sums_turned, 1)

                for j in range(HN):
                    if core:
                        if j % HALF_HEADS == 0:
                            pe.wait_ge(s.max_moved, 32 * (2 * n + j // HALF_HEADS + 1))
                        after(pe, s.exp_ready, HN * n + j - 1)
                        for c in range(UNITS):
                            last = pe.matmul(shifted_bank[j % 2][:, c * D:(c + 1) * D], k_packed[u][:, j // PACK, c * P:(c + 1) * P],
                                             q_spread[u][:, j, :], start=True, stop=True)
                        last.then_inc(s.shifted, 1)
                    if following:
                        if j % HALF_HEADS == 0:
                            pe.wait_ge(s.k_low, 2 * (n + 1) + j // HALF_HEADS + 1)
                        if j % SPREAD == 0:
                            pe.wait_ge(s.spread, HN // SPREAD * (n + 1) + j // SPREAD + 1)
                        after(pe, s.max_ready, HN * (n + 1) + j + 1 - scores_between(1 - u, j))
                        for unit in range(UNITS):
                            last = pe.matmul(head_scores[packed_scores(1 - u, j)][:, unit * D:(unit + 1) * D],
                                             q_spread[1 - u][:, j, unit * P:(unit + 1) * P], k_packed[1 - u][:, j // PACK, :],
                                             start=True, stop=True)
                        last.then_inc(s.scores, 1)
                    if j % PACK == 1 and (j > 1 and core or j == 1 and carry):
                        g = (j - 5) // PACK if j > 1 else PACKS - 1
                        v = vn[u] if j > 1 else vn[1 - u]
                        if g == 0:
                            pe.wait_ge(s.v_ready, n + 1)
                        pe.wait_ge(s.exp_ready, HN * n + j - 1)
                        after(pe, s.sums_copied, PACKS * n + j // PACK - 1)
                        if j == 5:
                            pe.wait_ge(s.max_low, 2 * n + 2)
                        if j == 9 and third and carry:
                            pe.wait_ge(s.heads_copied, n - B)
                        if j == 13 and following:
                            pe.wait_ge(s.max_low, 2 * (n + 1) + 1)
                        for c in range(UNITS):
                            for m in range(PACK):
                                last = pe.matmul(sum_bank[m * QUAD:(m + 1) * QUAD, :], v[:, c, PACK * g + m, :],
                                                 probs_t[(PACK * g + m) % 8][:, c * D:(c + 1) * D], start=c == 0, stop=c == UNITS - 1)
                        last.then_inc(s.sums, 1)
                    if core and j == MAXIMA_TURNED[1]:
                        if carry:
                            pe.wait_ge(s.sums_copied, PACKS * n)
                        turn_maxima(n, 1, maxima[u])
                    prepare(b, n, j, core, following, ahead)
                    if carry:
                        for unit in range(UNITS):
                            if j == at.turned[unit]:
                                turn_sums(unit)
                        finish(n, j, core, following)
                    if following and j == MAXIMA_TURNED[0]:
                        if core:
                            pe.wait_ge(s.sums_copied, PACKS * n + 2)
                        turn_maxima(n + 1, 0, maxima[1 - u])
                    if ahead and j == at.q[0]:
                        if third and carry:
                            pe.wait_ge(s.x_added, n)
                        elif third and following:
                            pe.wait_ge(s.v_ready, n + 2)
                        elif carry:
                            pe.wait_ge(s.heads_taken, UNITS * (n - 1) + 1)
                        elif following:
                            pe.wait_ge(s.k_low, 2 * (n + 1) + 1)
                        project("q", 0, at.q_side[0])
                    if ahead and j == at.q[1]:
                        if third:
                            pe.wait_ge(s.k_low, 2 * (n + 2) + 1)
                        elif carry:
                            pe.wait_ge(s.x_added, n)
                        elif following:
                            pe.wait_ge(s.k_low, 2 * (n + 1) + 2)
                        project("q", 1, at.q_side[1])
                    if following and j == at.v:
                        if ahead and not third:
                            pe.wait_ge(s.q_low, 2 * (n + 2) + 1)
                        elif carry:
                            pe.wait_ge(s.heads_taken, UNITS * n)
                        else:
                            pe.wait_ge(s.k_low, 2 * (n + 1) + 2)
                        for c in range(UNITS):
                            last = pe.matmul(side[third][:, c * P:(c + 1) * P], keys_in[1 - u][:, c * P:(c + 1) * P], values,
                                             start=True, stop=True)
                        last.then_inc(s.v_projected, 1)
                    if ahead and j == at.k[0]:
                        pe.wait_ge(s.in_ready, n + 3)
                        if following and not third:
                            pe.wait_ge(s.v_taken, n + 2)
                        elif not third:
                            pe.wait_ge(s.q_low, 2 * (n + 2) + 1)
                        project("k", 0, 0)
                    if ahead and j == at.k[1]:
                        pe.wait_ge(s.q_low, 2 * (n + 2) + (1 if third else 2))
                        project("k", 1, 1)

            over_steps(pe, window)

        def layer1():
            s = pk
            pe.wait_ge(later_loaded, later_count)
            pe.wait_ge(masks_ready, 1)
            for k in range(3):
                pe.transpose(bank[0][:, k * P:(k + 1) * P], w_rows1[:, k, :], ident[:, :])
            for c in range(2):
                last = pe.transpose(bank[1][:, c * B:(c + 1) * B], mask_own[:, c * P:(c + 1) * P], ident[0:B, 0:B])
            last.then_inc(masks_turned, 1)
            pe.wait_ge(packed_ready, 1)
            for c in range(2):
                last = pe.matmul(bank[1][:, 0:B], all_ones, mask_keys[:, :, c], start=c == 0, stop=c == 1)
            last.then_inc(masks_turned, 1)

            def prepare(b, n, j, core, following, ahead):
                pass

            def finish(n, j, core, following):
                if j == 9:
                    pe.wait_ge(s.heads_taken, UNITS * n)
                    for m in range(2):
                        for unit in range(UNITS):
                            last = pe.transpose(side[1][:, (2 * m + unit) * P:(2 * m + unit + 1) * P],
                                                heads_out[unit][:, m * P:(m + 1) * P], ident[:, :])
                    last.then_inc(s.result, 1)

            packed_window(0, prepare, finish, wv1[:, :], SCHEDULE1)

        def layer2(cross):
            s = n2
            pe.wait_ge(attention2_loaded, loads2_count)

            def window(b, u, core, carry, following, ahead, further, next_turn, ahead_turn):
                n = b + B * cross
                for j in range(STEPS):
                    g = STEPS * n + j
                    turns = j >= 2 and core or j < 2 and carry
                    if core:
                        if j == 0:
                            pe.wait_ge(s.qk_ready, n + 1)
                        pe.wait_ge(s.spread, g + 1)
                        after(pe, s.masked, g - 1)
                        pe.matmul(score_bank[j % 2][:, :], qn[u][:, j // 2 * P:(j // 2 + 1) * P], km[u][:, j * BANK:(j + 1) * BANK],
                                  start=True, stop=True).then_inc(s.scores, 1)
                    if turns:
                        pe.wait_ge(s.exp_ready, g - 1)
                        after(pe, s.probs_copied, g - 2)
                        for m in range(PACK):
                            last = pe.transpose(turn_bank[0][:, m * P:(m + 1) * P], probs[j % 2][:, m * P:(m + 1) * P], ident[:, :])
                        last.then_inc(s.probs_turned, 1)
                    if following and j == 0:
                        pe.wait_ge(s.in_ready, n + 2)
                        after(pe, s.qk_ready, n + 1)
                        keys_of = cn_t[1 - u] if cross else rows_t[1 - u]
                        for m in range(2 * DC):
                            for c in range(DC):
                                last = pe.matmul(aux[1][:, m * P:(m + 1) * P], w_qkv[:, cross, c, m * P:(m + 1) * P],
                                                 (rows_t[1 - u] if m < DC else keys_of)[:, c, :], start=c == 0, stop=c == DC - 1)
                        last.then_inc(s.projected, 1)
                    if following and j == 1:
                        keys_of = cn_t[1 - u] if cross else rows_t[1 - u]
                        for c in range(DC):
                            last = pe.matmul(aux[0][:, 0:D], keys_of[:, c, :], w_qkv[:, cross, c, 2 * D:3 * D],
                                             start=c == 0, stop=c == DC - 1)
                        last.then_inc(s.values, 1)
                    if carry and j == 2:
                        pe.wait_ge(s.sums_copied, STEPS * n)
                        after(pe, s.x_added, n - 1)
                        for m in range(STEPS):
                            last = pe.transpose(aux[2][:, m * P:(m + 1) * P], sums_copy[:, m, 0:P], ident[:, :])
                        last.then_inc(s.sums_turned, 1)
                    if carry and j == 3:
                        pe.wait_ge(s.heads_taken, n)
                        for c in range(DC):
                            last = pe.transpose(aux[2][:, c * P:(c + 1) * P], heads_out[0][:, c * P:(c + 1) * P], ident[:, :])
                        last.then_inc(s.heads_turned, 1)
                    if ahead and j == 3:
                        pe.wait_ge(s.rows_normed, n + 3)
                        if cross:
                            pe.wait_ge(s.loaded[u], 16 * (ahead_turn + 1))
                        if following:
                            pe.wait_ge(s.v_ready, n + 2)
                        for c in range(DC):
                            last = pe.transpose(aux[0][:, c * P:(c + 1) * P], norm_rows[:, u, c * P:(c + 1) * P], ident[:, :])
                        if cross:
                            for c in range(DC):
                                last = pe.transpose(aux[0][:, (DC + c) * P:(DC + c + 1) * P], cn[u][:, c * P:(c + 1) * P], ident[:, :])
                        last.then_inc(s.turned, 1)
                    if turns:
                        v = vn[u] if j >= 2 else vn[1 - u]
                        if j == 2:
                            pe.wait_ge(s.v_ready, n + 1)
                        pe.wait_ge(s.probs_copied, g - 1)
                        after(pe, s.sums_copied, g - 3)
                        for m in range(PACK):
                            last = pe.matmul(step_sums[j % 2][m * QUAD:(m + 1) * QUAD, 0:P], v[:, 0, (j - 2) % STEPS * PACK + m, :],
                                             probs_t[j % 2][:, m * P:(m + 1) * P], start=True, stop=True)
                        last.then_inc(s.sums, 1)
                    if carry and j == 3:
                        pe.wait_ge(s.heads_copied, n)
                        for c in range(DC):
                            last = pe.matmul(aux[2][:, D:2 * D], heads_t[0][:, c * P:(c + 1) * P], w_out2[:, cross, c, :],
                                             start=c == 0, stop=c == DC - 1)
                        last.then_inc(s.result, 1)

            over_steps(pe, window)

        def layer3():
            s = pk
            pe.wait_ge(packed_ready, 2)

            def prepare(b, n, j, core, following, ahead):
                if ahead and j == 1:
                    pe.wait_ge(s.placed, 2 * (b + 3))
                    if following:
                        pe.wait_ge(s.q_low, 2 * (n + 1) + 2)
                    for k in range(4):
                        last = pe.transpose(side[0][:, k * P:(k + 1) * P], placed_packed[:, k // 2, k % 2 * P:(k % 2 + 1) * P],
                                            ident[:, :])
                    last.then_inc(s.turned, 1)
                if ahead and j == 9:
                    pe.wait_ge(s.rows_normed, b + 3)
                    for k in range(4):
                        last = pe.transpose(side[0][:, k * P:(k + 1) * P], norm_packed[:, k // 2, k % 2 * P:(k % 2 + 1) * P],
                                            ident[:, :])
                    last.then_inc(s.turned_back, 1)

            def finish(n, j, core, following):
                if j == 7:
                    pe.wait_ge(s.heads_taken, UNITS * n)
                    if core:
                        pe.wait_ge(s.sums_copied, PACKS * n + 1)
                    for unit in range(UNITS):
                        last = pe.transpose(spare[:, unit * P:(unit + 1) * P], heads_out[unit][:, 0:P], ident[:, :])
                    last.then_inc(s.heads_turned, 1)
                if j == 9:
                    pe.wait_ge(s.heads_copied, n - B)
                    if following:
                        pe.wait_ge(s.v_ready, n + 2)
                    pe.matmul(side[1][:, 0:D], w3[:, 3, :], heads_t[0][:, :], start=True, stop=True).then_inc(s.result, 1)

            packed_window(1, prepare, finish, w3[:, 2, :], SCHEDULE3)

        def feed_forward3():
            s = ff3

            def turn(i):
                pe.wait_ge(s.x_copied, i + 1)
                for u in range(SLOTS):
                    for n in range(2):
                        last = pe.transpose(bank[0][:, (2 * u + n) * P:(2 * u + n + 1) * P], rows3[:, u, n * P:(n + 1) * P], ident[:, :])
                last.then_inc(s.turned, 1)

            def products(i, more):
                pe.wait_ge(s.rows_normed, i + 1)
                for u in range(SLOTS):
                    for n in range(2):
                        last = pe.transpose(bank[1][:, (2 * u + n) * P:(2 * u + n + 1) * P], norm3[:, u, n * P:(n + 1) * P], ident[:, :])
                last.then_inc(s.turned_back, 1)
                if more:
                    turn(i + 1)
                pe.wait_ge(s.in_ready, i + 1)
                for f in range(2):
                    pe.matmul(bank[2 + f][:, :], w3_up[:, f * P:(f + 1) * P], hidden3_in[:, :], start=True, stop=True)\
                      .then_inc(s.up_ready, 1)
                for f in range(2):
                    pe.wait_ge(s.hidden_ready, 2 * i + f + 1)
                    if f == 0:
                        after(pe, result_ready, i)
                    last = pe.matmul(bank[4][:, :], w3_down[:, f, :], hidden3[:, f, :], start=f == 0, stop=f == 1)
                last.then_inc(s.down_ready, 1)

            turn(0)
            products(0, True)
            with pe.Fori(1, ROUNDS - 1) as i:
                products(i, True)
            products(ROUNDS - 1, False)

        for layer in range(2):
            norm_and_split(layer)
            pairs(layer)
        feed_forward(0)
        layer1()
        layer2(0)
        layer2(1)
        feed_forward(1)
        layer3()
        feed_forward3()

    @block.scalar
    def _(act):
        def split_context(g):
            for c in range(DC):
                act.wait_ge(rows_turned, DC * g + c + 1)
                act.activation(ctx_high[:, c, g * TOK:(g + 1) * TOK], bank[2 * (g % 2) + c][:, :], ACT.Copy)\
                   .then_inc(ctx_high_ready, 1)

        def split_normed(layer, g):
            r = GROUPS * layer + g
            if g == 0:
                act.wait_ge(first_loaded, first_count)
                if layer:
                    act.wait_ge(small_loaded, small_count)
            for c in range(DC):
                act.wait_ge(normed_turned, DC * r + c + 1)
                after(act, normed_low_ready, DC * (r - 1) + c + 1)
                act.activation(normed[:, c, :], bank[4 + 2 * (g % 2) + c][:, :], ACT.Identity, bias=norm_offset[:, layer, c:c + 1],
                               scale=norm_scale[:, layer, c:c + 1]).then_inc(normed_ready, 1)
            for c in range(DC):
                act.wait_ge(normed_ready, DC * r + c + 1)
                act.activation(normed_high[:, c, g * TOK:(g + 1) * TOK], normed[:, c, :], ACT.Copy).then_inc(normed_high_ready, 1)

        def norm_and_split(layer):
            if layer == 0:
                split_context(0)
            for g in range(GROUPS):
                if layer == 0 and g + 1 < GROUPS:
                    split_context(g + 1)
                split_normed(layer, g)

        def pairs(layer):
            def copy_keys(gg, k, h):
                slot, n = k // GROUPS % 2, k % GROUPS
                keys = k0[k % 2]
                act.wait_ge(qk_ready, 4 * gg + 2 + h + 1)
                if n < 2:
                    act.activation(keys[:, h, :, P:P + 1], columns[slot][:, 2:3, h:h + 1].broadcast_to([P, GROUP, 1]), ACT.Copy)
                act.activation(keys[:, h, :, 0:P], project_bank[h][:, :].rearrange("p (b k) -> p b k", b=GROUP), ACT.Identity,
                               bias=columns[slot][:, 1, h:h + 1]).then_inc(k_copied, 1)

            def window(g, k, pair, core, carry, following):
                gg = g + PAIRS * GROUPS * layer
                for b in range(GROUP):
                    ss = GROUP * gg + b
                    turns = b > 0 and core or b == 0 and carry
                    a = (b - 1) % GROUP
                    if turns:
                        act.wait_ge(probs_turned, ss)
                        act.activation(probs_t0[:, a, :, :], wide_turned[:, 0:2 * P].rearrange("p (h q) -> p h q", h=2), ACT.Copy)\
                           .then_inc(probs_copied, 1)
                    if core:
                        act.wait_ge(max_ready, ss + 1)
                        for h in range(2):
                            last = act.activation(probs0[:, b, h, :], wide_scores[b % 2][:, h * KEYS0:(h + 1) * KEYS0], ACT.Exp,
                                                  bias=neg_max0[:, b, h:h + 1], accum_out=sums0[:, b, h:h + 1])
                        last.then_inc(exp_ready, 1)
                    if turns:
                        slot = (k if b else k - 1) // GROUPS % 2
                        act.wait_ge(heads_ready, ss)
                        for h in range(2):
                            last = act.activation(heads_high[:, h, a, :], wide_heads[a % 2][:, h * P:(h + 1) * P], ACT.Identity,
                                                  bias=columns[slot][:, 3, h:h + 1])
                        last.then_inc(heads_high_ready, 1)
                    if following and b in (1, 2):
                        copy_keys(gg + 1, k + 1, b - 1)

            over_groups(act, window)

        def feed_forward(which, norm, function, weights_loaded, left, left_count):
            s = ff

            def split_weights(quarters):
                for whole, high, _ in quarters:
                    act.activation(high, whole, ACT.Copy).then_inc(s.weights_high, 1)

            def scale(r):
                act.wait_ge(s.turned, r + 1)
                for c in range(DC):
                    act.activation(hidden_in[:, c, :], bank[0][:, c * D:(c + 1) * D], ACT.Identity, bias=norm_offset[:, norm, c:c + 1],
                                   scale=norm_scale[:, norm, c:c + 1]).then_inc(s.in_ready, 1)
                act.wait_ge(s.in_ready, DC * (r + 1))
                act.activation(hidden_in_high[:, :, :], hidden_in[:, :, :], ACT.Copy).then_inc(s.in_high, 1)

            def gelus(r, more):
                for f in range(F0 // P):
                    act.wait_ge(s.up_ready, F0 // P // 2 * r + f // 2 + 1)
                    act.activation(hidden[:, f, :], bank[1 + f // 2][:, (f % 2) * D:(f % 2 + 1) * D], function,
                                   bias=b_up[:, which, f:f + 1]).then_inc(s.hidden_ready, 1)
                    if f % 2:
                        act.wait_ge(s.hidden_ready, F0 // P * r + f + 1)
                        act.activation(hidden_high[:, f - 1:f + 1, :], hidden[:, f - 1:f + 1, :], ACT.Copy)\
                           .then_inc(s.hidden_high, 1)
                if more:
                    scale(r + 1)

            first = ROUNDS * which
            act.wait_ge(weights_loaded, 32)
            act.wait_ge(left, left_count)
            split_weights(weight_quarters)
            scale(first)
            with act.Fori(0, ROUNDS - 1) as i:
                gelus(first + i, True)
            gelus(first + ROUNDS - 1, False)

        def packed_window(third, prepare, finish, q_bias, k_bias, at):
            s = pk

            def high(name, m, half, slot):
                projected, target, bias, ready = ((s.q_projected, q_packed[slot], q_bias, s.q_high) if name == "q" else
                                                  (s.k_projected, k_packed[slot], k_bias, s.k_high))
                bank = at.q_side[half] if name == "q" else half
                act.wait_ge(projected, 2 * m + half + 1)
                if bias is None:
                    last = act.activation(target[0:SHIFT, 2 * half:2 * half + 2, :],
                                          side[bank][0:SHIFT, :].rearrange("p (g d) -> p g d", g=2), ACT.Copy)
                else:
                    for k in range(2):
                        g = 2 * half + k
                        last = act.activation(target[0:SHIFT, g, :], side[bank][0:SHIFT, k * D:(k + 1) * D], ACT.Identity,
                                              bias=bias[0:SHIFT, g:g + 1])
                last.then_inc(ready, 1)

            def window(b, u, core, carry, following, ahead, further, next_turn, ahead_turn):
                n = b + B * third
                for j in range(HN):
                    if following and j == 0:
                        high("k", n + 1, 1, 1 - u)
                    if j % PACK == 2 and (j > 2 and core or j == 2 and carry):
                        g = (j - 6) // PACK if j > 2 else PACKS - 1
                        act.wait_ge(s.sums, PACKS * n + j // PACK)
                        if j == 6 and carry:
                            act.wait_ge(s.sums_turned, UNITS * n)
                        act.activation(sums_copy[:, g, :], sum_bank[:, :], ACT.Copy).then_inc(s.sums_copied, 1)
                    if ahead:
                        prepare(b, u, j)
                    if carry:
                        finish(b, n, j)
                    if core:
                        act.wait_ge(s.shifted, HN * n + j + 1)
                        if j % PACK == 0:
                            after(act, s.sums, PACKS * n + j // PACK - 1)
                        act.activation(probs_t[j % 8][:, :], shifted_bank[j % 2][:, :], ACT.Exp, bias=zero[:, 0:1]).then_inc(s.exp_ready, 1)
                    if ahead and j == at.q[0] + 1:
                        high("q", n + 2, 0, u)
                    if ahead and j == at.q[1] + 1:
                        high("q", n + 2, 1, u)
                    if ahead and j == at.k[0] + 1:
                        high("k", n + 2, 0, u)

            over_steps(act, window)

        def layer1():
            s = pk
            act.wait_ge(packed_ready, 1)

            def prepare(b, u, j):
                pass

            def finish(b, n, j):
                if j == 10:
                    act.wait_ge(s.result, n)
                    act.sem_inc(idle, 1)
                    act.activation(mean_t[:, ds(b - 1, 1), :].rearrange("p a d -> p (a d)"), side[1][:, 0:D], ACT.Copy)
                    act.activation(std_t[:, ds(b - 1, 1), :].rearrange("p a d -> p (a d)"), side[1][:, D:2 * D], ACT.Relu)\
                       .then_inc(s.x_added, 1)

            packed_window(0, prepare, finish, bq1, bias1[:, 1, :], SCHEDULE1)
            for part in range(STD_PARTS):
                first, end = (B * k // STD_PARTS for k in (part, part + 1))
                act.wait_ge(moments_masked, end)
                act.activation(std_t[:, first:end, :], std_t[:, first:end, :], ACT.Sqrt).then_inc(std_ready, 1)

        def layer2(cross):
            s = n2
            norm = 3 + cross

            def window(b, u, core, carry, following, ahead, further, next_turn, ahead_turn):
                n = b + B * cross
                for j in range(STEPS):
                    g = STEPS * n + j
                    turns = j >= 2 and core or j < 2 and carry
                    if following and j == 1:
                        act.wait_ge(s.projected, n + 2)
                        for c in range(DC):
                            act.activation(qn[1 - u][:, c * P:(c + 1) * P], aux[1][:, c * P:(c + 1) * P], ACT.Identity,
                                           bias=b_q2[:, cross, c:c + 1], scale=SCALE2)
                        for c in range(DC):
                            last = act.activation(kn[1 - u][:, c * P:(c + 1) * P], aux[1][:, (DC + c) * P:(DC + c + 1) * P],
                                                  ACT.Identity, bias=b_qk2[:, cross, 1, c:c + 1])
                        last.then_inc(s.qk_ready, 1)
                    if turns:
                        act.wait_ge(s.probs_turned, g - 1)
                        after(act, s.sums, g - 3)
                        act.activation(probs_t[j % 2][:, :], turn_bank[0][:, :], ACT.Copy).then_inc(s.probs_copied, 1)
                    if carry and j == 3:
                        act.wait_ge(s.heads_turned, n)
                        act.activation(heads_t[0][:, :], aux[2][:, 0:D], ACT.Copy).then_inc(s.heads_copied, 1)
                    if j >= 1 and core or j == 0 and carry:
                        act.wait_ge(s.max_ready, g)
                        k = (j - 1) % 2
                        for h in range(PACK):
                            part = slice(h * P, (h + 1) * P)
                            last = act.activation(probs[k][:, part], scores_masked[k][:, part], ACT.Exp, bias=neg_max[k][:, h:h + 1])
                        last.then_inc(s.exp_ready, 1)
                    if turns:
                        act.wait_ge(s.sums, g - 1)
                        act.activation(sums_copy[:, (j - 2) % STEPS, 0:P], step_sums[j % 2][:, 0:P], ACT.Copy).then_inc(s.sums_copied, 1)
                    if ahead and j == 3:
                        act.wait_ge(s.turned, n + 3)
                        for c in range(DC):
                            last = act.activation(rows_t[u][:, c, :], aux[0][:, c * P:(c + 1) * P], ACT.Identity,
                                                  bias=norm_offset[:, norm, c:c + 1], scale=norm_scale[:, norm, c:c + 1])
                        if cross:
                            last = act.activation(cn_t[u][:, :, :], aux[0][:, D:2 * D].rearrange("p (c k) -> p c k", c=DC), ACT.Copy)
                        last.then_inc(s.in_ready, 1)

            over_steps(act, window)

        def layer3():
            s = pk

            def prepare(b, u, j):
                if j == 10:
                    act.wait_ge(s.turned_back, b + 3)
                    act.sem_inc(idle, 1)
                    act.activation(x[:, ds(b + 2, 1), :].rearrange("p a d -> p (a d)"), side[0][:, 0:D], ACT.Identity,
                                   bias=ln3[:, 1:2], scale=ln3[:, 0:1])
                    act.activation(keys_in[u][:, :], side[0][:, D:2 * D], ACT.Identity,
                                   bias=ln3[:, 3:4], scale=ln3[:, 2:3]).then_inc(s.in_ready, 1)

            def finish(b, n, j):
                if j == 8:
                    act.wait_ge(s.heads_turned, b)
                    act.activation(heads_t[0][:, :], spare[:, :], ACT.Copy).then_inc(s.heads_copied, 1)

            packed_window(1, prepare, finish, None, None, SCHEDULE3)

        def feed_forward3():
            s = ff3

            def copy(i):
                after(act, s.turned, i)
                act.sem_inc(idle, 1)
                act.activation(rows3[:, :, :], x[:, ds(SLOTS * i, SLOTS), :], ACT.Copy).then_inc(s.x_copied, 1)

            def hidden_layer(i, more):
                if more:
                    copy(i + 1)
                act.wait_ge(s.turned_back, i + 1)
                act.activation(hidden3_in[:, :], bank[1][:, :], ACT.Identity, bias=ln3[:, 5:6], scale=ln3[:, 4:5]).then_inc(s.in_ready, 1)
                for f in range(2):
                    act.wait_ge(s.up_ready, 2 * i + f + 1)
                    act.activation(hidden3[:, f, :], bank[2 + f][:, :], ACT.Gelu, bias=b3_up[:, f:f + 1]).then_inc(s.hidden_ready, 1)

            act.wait_ge(pk.x_added, 2 * B)
            copy(0)
            with act.Fori(0, ROUNDS - 1) as i:
                hidden_layer(i, True)
            hidden_layer(ROUNDS - 1, False)

        for layer in range(2):
            norm_and_split(layer)
            pairs(layer)
        feed_forward(0, 2, ACT.Gelu, weights0_loaded, x_added, 8 * 2 * PAIRS + ADD_CREDIT)
        layer1()
        layer2(0)
        layer2(1)
        feed_forward(1, 5, ACT.Gelu_apprx_tanh, weights2_loaded, n2.x_added, 2 * B)
        layer3()
        feed_forward3()

    @block.vector
    def _(dve):
        def split_context(g):
            tok = slice(g * TOK, (g + 1) * TOK)
            for c in range(DC):
                dve.wait_ge(ctx_high_ready, DC * g + c + 1)
                dve.tensor_tensor(ctx_low[:, c, tok], bank[2 * (g % 2) + c][:, :], ctx_high[:, c, tok].bitcast(F32),
                                  ALU.subtract).then_inc(ctx_low_ready, 1)

        def norm_two(chain, i, sem_ready):
            for u in range(SLOTS):
                chain.mark(dve.bn_stats(stats.sums[:, u, :], x[:, ds(SLOTS * i + u, 1), :].rearrange("p a d -> p (a d)")))
            chain.join()
            dve.sem_inc(idle, 1)
            for u in range(SLOTS):
                chain.mark(dve.bn_aggr(stats.mean_var[:, u, :], stats.sums[:, u, :]))
            chain.join()
            inverse_root(dve, chain, stats.rstd[:, 0:SLOTS], stats.mean_var[:, 0:SLOTS, 1], stats.shifted[:, 0:SLOTS],
                         stats.work[:, 0:SLOTS])
            for u in range(SLOTS):
                dve.tensor_scalar(norm_rows[:, u, :], x[:, ds(SLOTS * i + u, 1), :].rearrange("p a d -> p (a d)"),
                                  stats.mean_var[:, u, 0:1], stats.rstd[:, u:u + 1], ALU.subtract, ALU.mult)\
                   .then_inc(sem_ready, 1)

        NORM_TWO = 2 * SLOTS + ROOT_STEPS

        def add_row_bias(chain, i, bias):
            both = x[:, ds(SLOTS * i, SLOTS), :]
            chain.mark(dve.tensor_tensor(both, both, row_bias[:, bias:bias + 1, :].broadcast_to([P, SLOTS, D]), ALU.add))

        NORM_GROUP = statistics_steps(GROUP)

        def norm_group(layer, g):
            r = GROUPS * layer + g
            if layer == 0:
                dve.wait_ge(x_loaded[g], 16)
            after(dve, rows_normed, GROUP * r)
            row_statistics(dve, Chain(dve, split_chain, NORM_GROUP * r + layer), [x[:, GROUP * g + b, :] for b in range(GROUP)], stats, idle)
            after(dve, normed_turned, DC * r)
            for b in range(GROUP):
                dve.tensor_scalar(wide_rows[:, b, :], x[:, GROUP * g + b, :], stats.mean_var[:, b, 0:1], stats.rstd[:, b:b + 1],
                                  ALU.subtract, ALU.mult).then_inc(rows_normed, 1)

        def split_normed(layer, g):
            r = GROUPS * layer + g
            tok = slice(g * TOK, (g + 1) * TOK)
            for c in range(DC):
                dve.wait_ge(normed_high_ready, DC * r + c + 1)
                dve.tensor_tensor(normed_low[:, c, tok], normed[:, c, :], normed_high[:, c, tok].bitcast(F32),
                                  ALU.subtract).then_inc(normed_low_ready, 1)

        def norm_and_split(layer):
            if layer == 0:
                split_context(0)
            for g in range(GROUPS):
                norm_group(layer, g)
                if layer == 0 and g + 1 < GROUPS:
                    split_context(g + 1)
                if g:
                    split_normed(layer, g - 1)
            split_normed(layer, GROUPS - 1)
            if layer == 0:
                dve.wait_ge(small_loaded, small_count)
            dve.wait_ge(rows_normed, B * (layer + 1))
            Chain(dve, split_chain, NORM_GROUP * GROUPS * (layer + 1) + layer).link(
                dve.tensor_tensor(x[:, :, :], x[:, :, :], row_bias[:, layer:layer + 1, :].broadcast_to([P, B, D]), ALU.add))

        def pairs(layer):
            def copy_queries(gg, k, h):
                slot = k // GROUPS % 2
                dve.wait_ge(qk_ready, 4 * gg + h + 1)
                dve.tensor_scalar(q0[k % 2][:, h, :], project_bank[h][:, :], columns[slot][:, 0, h:h + 1], SCALE0, ALU.add, ALU.mult)\
                   .then_inc(q_copied, 1)

            def copy_values(gg, k, half):
                slot = k // GROUPS % 2
                dve.wait_ge(v_ready, 2 * gg + half + 1)
                dve.tensor_tensor(v0[k % 2][:, 2 * half:2 * half + 2, :], project_bank[half][:, :].rearrange("p (b d) -> p b d", b=2),
                                  value_bias[slot][:, :, :].broadcast_to([P, 2, D]), ALU.add).then_inc(v_copied, 1)

            def window(g, k, pair, core, carry, following):
                gg = g + PAIRS * GROUPS * layer
                for b in range(GROUP):
                    ss = GROUP * gg + b
                    if core:
                        dve.wait_ge(scores_ready, ss + 1)
                        dve.tensor_reduce(neg_max0[:, b, :], wide_scores[b % 2][:, 0:2 * KEYS0].rearrange("p (h k) -> p h k", h=2),
                                          X_AXIS, ALU.max, negate=True).then_inc(max_ready, 1)
                        chain = Chain(dve, softmax_chain, ss)
                        dve.wait_ge(exp_ready, ss + 1)
                        chain.link(dve.reciprocal(inverse0[:, b, :], sums0[:, b, :]))
                        for h in range(2):
                            last = dve.tensor_scalar(probs0[:, b, h, 0:P], probs0[:, b, h, 0:P], inverse0[:, b, h:h + 1], None,
                                                     ALU.mult)
                        last.then_inc(probs_ready, 1)
                    if following and b == 0:
                        copy_queries(gg + 1, k + 1, 0)
                    if following and b == 3:
                        copy_values(gg + 1, k + 1, 1)
                    if b > 0 and core or b == 0 and carry:
                        a, slot = (b - 1) % GROUP, (k if b else k - 1) // GROUPS % 2
                        dve.wait_ge(heads_high_ready, ss)
                        for h in range(2):
                            last = dve.scalar_tensor_tensor(heads_low[:, h, a, :], wide_heads[a % 2][:, h * P:(h + 1) * P],
                                                            columns[slot][:, 3, h:h + 1], heads_high[:, h, a, :].bitcast(F32),
                                                            ALU.add, ALU.subtract)
                        last.then_inc(heads_split, 1)
                    if b == 3 and core or b == 1 and carry:
                        done = 2 * gg + b // 2
                        n, half = (k if b == 3 else k - 1) % GROUPS, 1 - b // 2
                        rows = x[:, GROUP * n + 2 * half:GROUP * n + 2 * half + 2, :]
                        dve.wait_ge(out_ready, done)
                        dve.wait_ge(x_added, done - 8 + ADD_CREDIT)
                        dve.tensor_tensor(rows, rows, out_bank[:, :].rearrange("p (b d) -> p b d", b=2), ALU.add).then_inc(x_added, 1)
                    if following and b == 0:
                        copy_queries(gg + 1, k + 1, 1)
                    if following and b == 2:
                        copy_values(gg + 1, k + 1, 0)

            over_groups(dve, window)
            dve.wait_ge(x_added, 8 * PAIRS * (layer + 1) + ADD_CREDIT)

        def feed_forward(which, bias):
            s = ff
            steps = NORM_TWO + 1
            first = ROUNDS * which

            def norm(i):
                r = first + i
                chain = Chain(dve, s.chain, steps * r)
                after(dve, s.turned, r)
                dve.sem_inc(idle, 1)
                norm_two(chain, i, s.rows_normed)
                dve.wait_ge(s.rows_normed, SLOTS * (r + 1))
                add_row_bias(chain, i, bias)
                chain.join()

            def add(i):
                dve.wait_ge(s.down_ready, first + i + 1)
                both = x[:, ds(SLOTS * i, SLOTS), :]
                dve.tensor_tensor(both, both, bank[5][:, :].rearrange("p (u d) -> p u d", u=SLOTS), ALU.add)\
                   .then_inc(s.x_added, 1)

            def input_low(i):
                dve.wait_ge(s.in_high, first + i + 1)
                dve.tensor_tensor(hidden_in_low[:, :, :], hidden_in[:, :, :], hidden_in_high[:, :, :].bitcast(F32), ALU.subtract).then_inc(s.in_low, 1)

            def hidden_lows(i):
                for k in range(hidden_pairs):
                    dve.wait_ge(s.hidden_high, hidden_pairs * (first + i) + k + 1)
                    pair = slice(2 * k, 2 * k + 2)
                    dve.tensor_tensor(hidden_low[:, pair, :], hidden[:, pair, :], hidden_high[:, pair, :].bitcast(F32), ALU.subtract).then_inc(s.hidden_low, 1)

            norm(0)
            input_low(0)
            norm(1)
            with dve.Fori(0, ROUNDS - 2) as i:
                hidden_lows(i)
                input_low(i + 1)
                norm(i + 2)
                add(i)
            hidden_lows(ROUNDS - 2)
            input_low(ROUNDS - 1)
            add(ROUNDS - 2)
            hidden_lows(ROUNDS - 1)
            add(ROUNDS - 1)
            dve.wait_ge(s.x_added, first + ROUNDS)

        def pack_weights(chain, queries, keys):
            for part in range(PACK):
                chain.mark(dve.tensor_scalar(wq_packed[:, :, part, :], queries.rearrange("p (g r) -> p g r", g=PACKS), SCALE1, None,
                                             ALU.mult))
                chain.mark(dve.tensor_copy(wk_packed[:, :, part, :], keys.rearrange("p (g r) -> p g r", g=PACKS)))

        def weighted(w, target, sums):
            return dve.tensor_tensor(target.rearrange("p (h e) -> p h e", h=HN), sums,
                                     inverse[:, w % 2, :].unsqueeze(2).broadcast_to([P, HN, sums.shape[2]]), ALU.mult)

        def packed_window(third, prepare, finish, values, q_bias, k_bias, at, conclude):
            s = pk

            def low(name, m, half, slot):
                high, target, bias, quad, ready = ((s.q_high, q_packed[slot], q_bias, 2, s.q_low) if name == "q" else
                                                   (s.k_high, k_packed[slot], k_bias, 1, s.k_low))
                dve.wait_ge(high, 2 * m + half + 1)
                rows = slice(quad * QUAD, (quad + 1) * QUAD)
                packs = slice(2 * half, 2 * half + 2)
                full = side[at.q_side[half] if name == "q" else half][rows, :].rearrange("p (g d) -> p g d", g=2)
                if bias is None:
                    last = dve.tensor_tensor(target[rows, packs, :], full, target[rows, packs, :].bitcast(F32), ALU.subtract)
                else:
                    for k in range(2):
                        g = 2 * half + k
                        last = dve.scalar_tensor_tensor(target[rows, g, :], full[:, k, :], bias[rows, g:g + 1],
                                                        target[rows, g, :].bitcast(F32), ALU.add, ALU.subtract)
                last.then_inc(ready, 1)

            def split_maxima(m, half, early):
                k = 2 * m + half + 1
                turned = spare[0:HALF_HEADS * UNITS, half * P:(half + 1) * P]
                if early:
                    dve.wait_ge(s.max_turned, k)
                    dve.tensor_copy(max_high[half][:, :], turned).then_inc(s.max_high, 1)
                else:
                    dve.wait_ge(s.max_high, k)
                    dve.tensor_tensor(max_low[half][:, :], turned, max_high[half][:, :].bitcast(F32), ALU.subtract).then_inc(s.max_low, 1)

            def window(b, u, core, carry, following, ahead, further, next_turn, ahead_turn):
                n = b + B * third
                for j in range(HN):
                    if core and j == MAXIMA_TURNED[1] + 1:
                        split_maxima(n, 1, False)
                    if following and j == MAXIMA_TURNED[0] + 1:
                        split_maxima(n + 1, 0, False)
                    if ahead and j == at.q[0] + 2:
                        low("q", n + 2, 0, u)
                    if ahead and j == at.q[1] + 2:
                        low("q", n + 2, 1, u)
                    if ahead and j == at.k[0] + 2:
                        low("k", n + 2, 0, u)
                    if following and j == at.q[1] + 2 - HN:
                        low("q", n + 1, 1, 1 - u)
                    if following and j == 1:
                        low("k", n + 1, 1, 1 - u)
                    if carry:
                        finish(b, n, j, True)
                    if ahead:
                        prepare(b + 2, n + 2, u, j, ahead_turn, following, True)
                    if following:
                        dve.wait_ge(s.scores, HN * (n + 1) + j + 1)
                        dve.tensor_reduce(maxima[1 - u][:, j, :],
                                          head_scores[packed_scores(1 - u, j)][:, :].rearrange("p (a k) -> p a k", a=UNITS),
                                          X_AXIS, ALU.max, negate=True).then_inc(s.max_ready, 1)
                    if core and j == MAXIMA_TURNED[1]:
                        split_maxima(n, 1, True)
                    if following and j == MAXIMA_TURNED[0]:
                        split_maxima(n + 1, 0, True)
                    if following and j > at.v:
                        values(b + 1, n + 1, 1 - u, j - at.v)
                    if carry:
                        finish(b, n, j, False)
                    if ahead:
                        prepare(b + 2, n + 2, u, j, ahead_turn, following, False)
                    if core and not following and conclude and j == HALF_HEADS:
                        conclude()
                    if following and not third and j == HN - 1:
                        dve.wait_ge(x_masked, b + 2)
                        dve.bn_stats(x_stats[:, ds(b + 1, 1), :].rearrange("p a k -> p (a k)"),
                                     x[:, ds(b + 1, 1), :].rearrange("p a d -> p (a d)")).then_inc(x_measured, 1)

            over_steps(dve, window)

        def layer1():
            s = pk
            dve.wait_ge(later_loaded, later_count)
            chain = setup
            chain.mark(dve.tensor_scalar(bq1[:, :], bias1[:, 0, :], SCALE1, None, ALU.mult))
            chain.mark(dve.tensor_scalar(b_q2[:, :, :], b_qk2[:, :, 0, :], SCALE2, None, ALU.mult))
            chain.mark(dve.tensor_scalar(self_mask[:, 1, :], self_mask[:, 0, :], NEG_BIG, -NEG_BIG, ALU.mult, ALU.add))
            dve.wait_ge(head_steps, 6)
            chain.mark(dve.tensor_reduce(part_of_head[:, :], head_of_8[:, 0:3 * PACK].rearrange("p (a h) -> p h a", a=3),
                                         X_AXIS, ALU.add))
            dve.wait_ge(masks_ready, 1)
            dve.wait_ge(masks_turned, 1)
            pack_weights(chain, bank[0][:, 0:P], bank[0][:, P:2 * P])
            chain.mark(dve.tensor_copy(wv1[:, :], bank[0][:, 2 * P:3 * P]))
            chain.mark(dve.tensor_copy(mask_keys[:, :, :].rearrange("p b c -> p c b"),
                                       bank[1][:, 0:2 * B].rearrange("p (c b) -> p c b", c=2)))
            chain.join()
            dve.sem_inc(packed_ready, 1)
            dve.wait_ge(masks_turned, 2)
            chain.link(dve.reciprocal(valid[:, :], bank[1][:, 0:B]))

            KEYS, VALUES, HEADS = 4, 5, 8

            def keys_of(b, n, u, j, turn, following, early):
                if early or j not in (2, 3, 4, 9, 10):
                    return
                chain = Chain(dve, s.prep_chain[0], KEYS * n)
                mask = mask_rows[:, ds(b, 1), :].rearrange("p a d -> p (a d)")
                source = cn[u][:, :]
                if j == 2:
                    if following:
                        dve.wait_ge(s.in_ready, n)
                    dve.wait_ge(s.loaded[u], 16 * (turn + 1))
                    chain.mark(dve.tensor_tensor(scratch1[:, :], source, mask, ALU.mult))
                elif j == 3:
                    chain.steps = 1
                    chain.join()
                    chain.mark(dve.tensor_reduce(key_mean[:, :], scratch1[:, :], X_AXIS, ALU.add))
                elif j == 4:
                    chain.steps = 2
                    chain.join()
                    chain.mark(dve.tensor_tensor(key_mean[:, :], key_mean[:, :], valid[:, ds(b, 1)], ALU.mult))
                elif j == 9:
                    chain.steps = 3
                    chain.join()
                    chain.mark(dve.scalar_tensor_tensor(scratch1[:, :], source, key_mean[:, 0:1], mask, ALU.subtract, ALU.mult))
                else:
                    chain.steps = 4
                    chain.join()
                    dve.tensor_scalar(keys_in[u][:, :], scratch1[:, :], key_mean[:, 0:1], None, ALU.add).then_inc(s.in_ready, 1)

            def values_of(b, n, u, step):
                chain = Chain(dve, s.values_chain, VALUES * n)
                v = scratch_values[:, :].rearrange("p (c d) -> p c d", c=2)
                if step == 1:
                    dve.wait_ge(s.v_projected, n + 1)
                    after(dve, s.v_ready, n)
                    after(dve, s.values_chain, VALUES * n)
                    dve.tensor_tensor(v, side[0][:, 0:D].rearrange("p (c d) -> p c d", c=2),
                                      bv1[:, :, :].broadcast_to([P, 2, P]), ALU.add).then_inc(s.v_taken, 1)
                if step in (2, 3):
                    dve.wait_ge(s.v_taken, n + 1)
                    c = step - 2
                    valid_key = mask_keys[:, ds(b, 1), c]
                    heads = v[:, c, :].rearrange("p (h e) -> p h e", h=HN)
                    chain.mark(dve.tensor_scalar(vn[u][:, c, :, 0:8], heads, valid_key, None, ALU.mult))
                    chain.mark(dve.scalar_tensor_tensor(vn[u][:, c, :, 8:16], heads, valid_key, heads, ALU.mult, ALU.mult))
                    ins = dve.tensor_scalar(vn[u][:, c, :, 16], ones[:, :], valid_key, None, ALU.mult)
                    if c:
                        ins.then_inc(s.v_ready, 1)
                    else:
                        chain.mark(ins)

            scratch_heads = [heads_t[u][:, 0:P] for u in range(UNITS)]

            def moments(b, n, j, early):
                if j not in (4, 5, 6, 7):
                    return
                unit = (j - 4) // 2
                chain = Chain(dve, s.heads_chain[0], HEADS * (n - 1))
                sums = side[unit][:, :].rearrange("p (h e) -> p h e", h=HN)
                mean, square = heads_out[unit][:, 0:P], heads_out[unit][:, P:2 * P]
                chain.steps = 4 * unit + (0, 1, 2, 4)[2 * (j % 2) + (not early)]
                if j % 2 == 0 and early:
                    dve.wait_ge(s.sums_turned, UNITS * (n - 1) + unit + 1)
                    chain.mark(dve.reciprocal(inverse[:, unit, :].unsqueeze(2), sums[:, :, 16:17]))
                elif j % 2 == 0:
                    chain.join()
                    chain.mark(weighted(unit, mean, sums[:, :, 0:8]))
                elif early:
                    chain.join()
                    chain.mark(weighted(unit, square, sums[:, :, 8:16]))
                    chain.mark(dve.tensor_tensor(scratch_heads[unit], mean, mean, ALU.mult))
                else:
                    chain.join()
                    dve.tensor_tensor(square, square, scratch_heads[unit], ALU.subtract).then_inc(s.heads_taken, 1)

            scale, mean, var, rstd, shifted, work = (row_sums[:, k, :] for k in range(6))

            def measure():
                chain = setup
                dve.wait_ge(x_measured, B)
                for b in range(B):
                    chain.mark(dve.bn_aggr(x_moments[:, b, :], x_stats[:, b, :]))
                chain.join()
                chain.mark(dve.tensor_scalar(scale, valid[:, :], float(D), None, ALU.mult))
                chain.link(dve.tensor_tensor(var, x_moments[:, :, 0], x_moments[:, :, 0], ALU.mult))
                chain.link(dve.tensor_tensor(var, var, x_moments[:, :, 1], ALU.add))
                chain.mark(dve.tensor_tensor(mean, x_moments[:, :, 0], scale, ALU.mult))
                chain.link(dve.tensor_tensor(var, var, scale, ALU.mult))
                chain.link(dve.tensor_tensor(work, mean, mean, ALU.mult))
                chain.link(dve.tensor_tensor(var, var, work, ALU.subtract))
                chain.link(dve.tensor_scalar(var, var, 0.0, None, ALU.max))
                inverse_root(dve, chain, rstd, var, shifted, work)

            packed_window(0, keys_of, moments, values_of, bq1, bias1[:, 1, :], SCHEDULE1, measure)

            chain = setup
            for part in range(STD_PARTS):
                dve.wait_ge(std_ready, part + 1)
                rows = range(part * B // STD_PARTS, (part + 1) * B // STD_PARTS)
                for b in rows:
                    chain.mark(dve.scalar_tensor_tensor(x[:, b, :], x[:, b, :], mean[:, b:b + 1], std_t[:, b, :],
                                                        ALU.subtract, ALU.mult))
                chain.join()
                for b in rows:
                    chain.mark(dve.scalar_tensor_tensor(x[:, b, :], x[:, b, :], rstd[:, b:b + 1], mean_t[:, b, :],
                                                        ALU.mult, ALU.add))
            chain.join()

        def layer2(cross):
            s = n2
            if not cross:
                chain = setup
                for u in range(SLOTS):
                    chain.mark(dve.memset(vn[u][:, 0, :, 16], 1.0))
                chain.join()
            NORM = 1 + 1 + ROOT_STEPS + 1

            def norm_row(n, b, u, j):
                chain = Chain(dve, s.norm_chain, NORM * n)
                row = x[:, ds(b, 1), :].rearrange("p a d -> p (a d)")
                if j == 0:
                    chain.mark(dve.bn_stats(stats.sums[:, 0, :], row))
                    chain.join()
                    dve.sem_inc(idle, 1)
                    chain.mark(dve.bn_aggr(stats.mean_var[:, 0, :], stats.sums[:, 0, :]))
                    chain.join()
                elif j == 1:
                    chain.steps = 2
                    inverse_root(dve, chain, stats.rstd[:, 0:1], stats.mean_var[:, 0:1, 1], stats.shifted[:, 0:1], stats.work[:, 0:1])
                elif j == 2:
                    chain.steps = 13
                    dve.tensor_scalar(norm_rows[:, u, :], row, stats.mean_var[:, 0, 0:1], stats.rstd[:, 0:1], ALU.subtract, ALU.mult)\
                       .then_inc(s.rows_normed, 1)
                    dve.wait_ge(s.rows_normed, n + 1)
                    chain.link(dve.tensor_tensor(row, row, row_bias[:, 3 + cross, :], ALU.add))

            def window(b, u, core, carry, following, ahead, further, next_turn, ahead_turn):
                n = b + B * cross
                mask = cross_mask[u] if cross else self_mask
                for j in range(STEPS):
                    g = STEPS * n + j
                    if j >= 1 and core or j == 0 and carry:
                        k = (j - 1) % 2
                        dve.wait_ge(s.mask_added, g)
                        dve.tensor_reduce(neg_max[k][:, 0:PACK], scores_masked[k][:, :].rearrange("p (h k) -> p h k", h=PACK),
                                          X_AXIS, ALU.max, negate=True).then_inc(s.max_ready, 1)
                    if core:
                        wide = [P, PACK, P]
                        after(dve, s.exp_ready, g - 1)
                        dve.wait_ge(s.scores, g + 1)
                        dve.tensor_tensor(scores_masked[j % 2][:, :].rearrange("p (h k) -> p h k", h=PACK),
                                          score_bank[j % 2][:, :].rearrange("p (h k) -> p h k", h=PACK),
                                          mask[:, 0:1, :].broadcast_to(wide), ALU.mult).then_inc(s.masked, 1)
                    if ahead:
                        norm_row(n + 2, b + 2, u, j)
                    if following and j == 2:
                        dve.wait_ge(s.values, n + 2)
                        after(dve, s.sums, STEPS * n)
                        dve.tensor_tensor(vn[1 - u][:, 0, :, 0:16], aux[0][:, 0:D].rearrange("p (h e) -> p h e", h=HN),
                                          b_v2[:, cross, :].rearrange("p (h e) -> p h e", h=HN), ALU.add).then_inc(s.v_ready, 1)
                    if carry and j == 2:
                        dve.wait_ge(s.sums_turned, n)
                        sums = aux[2][:, :].rearrange("p (h e) -> p h e", h=HN)
                        Chain(dve, s.heads_chain, n - 1).link(dve.reciprocal(inverse[:, 0, :].unsqueeze(2), sums[:, :, 16:17]))
                        weighted(0, heads_out[0][:, :], sums[:, :, 0:16]).then_inc(s.heads_taken, 1)
                    if following and cross and j == 3:
                        dve.wait_ge(s.mask_loaded[1 - u], 16 * (next_turn + 1))
                        Chain(dve, s.mask_chain, b + 1).link(
                            dve.tensor_scalar(cross_mask[1 - u][:, 1, :], cross_mask[1 - u][:, 0, :], NEG_BIG, -NEG_BIG,
                                              ALU.mult, ALU.add))
                    if carry and j == 3:
                        dve.wait_ge(s.result, n)
                        row = x[:, ds(b - 1, 1), :].rearrange("p a d -> p (a d)")
                        dve.tensor_tensor(row, row, aux[2][:, D:2 * D], ALU.add).then_inc(s.x_added, 1)

            over_steps(dve, window)
            dve.wait_ge(s.x_added, B * (1 + cross))

        def norm_columns(chain, tiles, outs, sem_ready):
            row_statistics(dve, chain, tiles, stats, idle)
            for k, (tile, target) in enumerate(zip(tiles, outs)):
                ins = dve.tensor_scalar(target, tile, stats.mean_var[:, k, 0:1], stats.rstd[:, k:k + 1], ALU.subtract, ALU.mult)
                if k < len(tiles) - 1:
                    chain.mark(ins)
            ins.then_inc(sem_ready, 1)
            chain.join()

        def layer3():
            s = pk
            chain = setup
            pack_weights(chain, w3[:, 0, :], w3[:, 1, :])
            for u in range(SLOTS):
                chain.mark(dve.memset(vn[u][:, :, :, :], 0.0))
            chain.join()
            for u in range(SLOTS):
                chain.mark(dve.memset(vn[u][:, :, :, 8], 1.0))
            chain.join()
            dve.sem_inc(packed_ready, 1)

            PREP, HEADS = PREP3, 2
            tiles = [side[0][:, k * P:(k + 1) * P] for k in range(4)]
            targets = [norm_packed[:, k // 2, k % 2 * P:(k % 2 + 1) * P] for k in range(4)]

            def inputs_of(b, n, u, j, turn, following, early):
                chain = Chain(dve, s.prep_chain[1], PREP * b)

                if j == 2 and early:
                    if following:
                        dve.wait_ge(s.prep_chain[1], PREP * b)
                        dve.wait_ge(s.rows_normed, b)
                    dve.wait_ge(s.turned, b + 1)
                    for k in range(4):
                        chain.mark(dve.bn_stats(stats.sums[:, k, :], tiles[k]))
                elif j == 3 and early:
                    chain.steps = 4
                    chain.join()
                    dve.sem_inc(idle, 1)
                    for k in range(4):
                        chain.mark(dve.bn_aggr(stats.mean_var[:, k, :], stats.sums[:, k, :]))
                elif j in (7, 8) and early:
                    if j == 7:
                        dve.wait_ge(s.rstd_ready, RSTD_STEPS * (b + 1))
                    chain.steps = 8 + 2 * (j - 7)
                    for k in (2 * (j - 7), 2 * (j - 7) + 1):
                        ins = dve.tensor_scalar(targets[k], tiles[k], stats.mean_var[:, k, 0:1], stats.rstd[:, k:k + 1],
                                                ALU.subtract, ALU.mult)
                        if k < 3:
                            chain.mark(ins)
                        else:
                            ins.then_inc(s.rows_normed, 1)

            def values_of(b, n, u, step):
                if step > 1:
                    return
                dve.wait_ge(s.v_projected, n + 1)
                dve.tensor_copy(vn[u][:, :, :, 0:8], side[1][:, 0:D].rearrange("p (c h e) -> p c h e", c=2, h=HN)).then_inc(s.v_ready, 1)

            def heads_of(b, n, j, early):
                if j in (4, 6) and early:
                    unit = (j - 4) // 2
                    chain = Chain(dve, s.heads_chain[1], HEADS * (b - 1))
                    sums = side[1][:, :].rearrange("p (h e) -> p h e", h=HN)
                    chain.steps = unit
                    dve.wait_ge(s.sums_turned, UNITS * (n - 1) + unit + 1)
                    chain.link(dve.reciprocal(inverse[:, unit, :].unsqueeze(2), sums[:, :, 8:9]))
                    weighted(unit, heads_out[unit][:, 0:P], sums[:, :, 0:8]).then_inc(s.heads_taken, 1)
                elif j == 10 and not early:
                    dve.wait_ge(s.result, n)
                    row = x[:, ds(b - 1, 1), :].rearrange("p a d -> p (a d)")
                    dve.tensor_tensor(row, row, side[1][:, 0:D], ALU.add).then_inc(s.x_added, 1)

            packed_window(1, inputs_of, heads_of, values_of, None, None, SCHEDULE3, None)
            dve.wait_ge(s.x_added, 2 * B)

        def feed_forward3():
            s = ff3
            steps = statistics_steps(4) + 3

            def norm(i):
                chain = Chain(dve, s.chain, steps * i)
                dve.wait_ge(s.turned, i + 1)
                after(dve, s.turned_back, i)
                dve.sem_inc(idle, 1)
                norm_columns(chain, [bank[0][:, k * P:(k + 1) * P] for k in range(4)],
                             [norm3[:, k // 2, k % 2 * P:(k % 2 + 1) * P] for k in range(4)], s.rows_normed)
                dve.wait_ge(s.rows_normed, i + 1)
                assert chain.steps == steps, (chain.steps, steps)

            def add(i):
                dve.wait_ge(s.down_ready, i + 1)
                dve.wait_ge(out_stored, 16 * (i + 1))
                dve.scalar_tensor_tensor(result[:, :, :], bank[4][:, :].rearrange("p (u d) -> p u d", u=SLOTS), b3_down[:, 0:1],
                                         x[:, ds(SLOTS * i, SLOTS), :], ALU.add, ALU.add).then_inc(result_ready, 1)

            norm(0)
            with dve.Fori(0, ROUNDS - 1) as i:
                norm(i + 1)
                add(i)
            add(ROUNDS - 1)

        setup = Chain(dve, setup_chain)
        dve.sem_inc(x_added, ADD_CREDIT)
        dve.sem_inc(heads_split, GROUP)
        for layer in range(2):
            norm_and_split(layer)
            pairs(layer)
        feed_forward(0, 2)
        layer1()
        layer2(0)
        layer2(1)
        feed_forward(1, 5)
        layer3()
        feed_forward3()

    @block.gpsimd
    def _(pool):
        def copy(target, source):
            source, target = (a.rearrange("p a b -> p (a b)") if len(a.shape) == 3 else a for a in (source, target))
            return pool.tensor_tensor(target, source, zero[:, :].broadcast_to([P, source.shape[1]]), ALU.add)

        chain = Chain(pool, ident_ready)
        chain.link(pool.memset(zero[:, :], 0.0))
        chain.link(pool.memset(ident[:, :], 0.0))
        chain.link(pool.affine_select(out=ident[:, :], in_=ident[:, :], compare_op=ALU.not_equal, fill=1.0, base=0,
                                      pattern=[[-1, P]], channel_multiplier=1))
        pool.sem_inc(weights_split, 1)
        steps = 9
        for layer in range(2):
            with pool.Fori(0, PAIRS // 2) as i:
                for slot in range(2):
                    p = PAIRS * layer + 2 * i + slot
                    chain = Chain(pool, split_steps, steps * p)
                    wh, wl = weights_high[slot], weights_low[slot]
                    pool.wait_ge(pair_loaded, 16 * PAIR_LOADS * (p + 1))
                    pool.wait_ge(x_added, 8 * (p - 1) + ADD_CREDIT)
                    chain.mark(copy(columns[slot][:, :, :], pair_columns[:, :, :]))
                    for kind in range(4):
                        chain.link(copy(wh[:, kind, :], pair_weights[:, kind, :]))
                        chain.mark(pool.tensor_tensor(wl[:, kind, :], pair_weights[:, kind, :], wh[:, kind, :].bitcast(F32),
                                                      ALU.subtract))
                    chain.join()
                    pool.tensor_tensor(value_bias[slot][:, 0, :], pair_rows[:, 0, :], pair_rows[:, 1, :], ALU.subtract)\
                        .then_inc(weights_split, 1)
        def feed_forward_low(which):
            for k, (whole, high, low) in enumerate(weight_quarters):
                pool.wait_ge(ff.weights_high, len(weight_quarters) * which + k + 1)
                pool.tensor_tensor(low, whole, high.bitcast(F32), ALU.subtract).then_inc(ff.weights_low, 1)

        feed_forward_low(0)
        pool.wait_ge(x_added, 8 * 2 * PAIRS + ADD_CREDIT)
        for size, target in ((8, head_of_8), (16, head_of_16)):
            n = P // size
            chain = Chain(pool, head_steps, 3 * (size // 16))
            chain.link(pool.memset(target[:, :], 1.0))
            chain.link(pool.affine_select(out=target[:, :], in_=target[:, :], compare_op=ALU.is_ge, fill=0.0, base=0,
                                          pattern=[[-size, n]], channel_multiplier=1))
            chain.link(pool.affine_select(out=target[:, :], in_=target[:, :], compare_op=ALU.is_ge, fill=0.0, base=size - 1,
                                          pattern=[[size, n]], channel_multiplier=-1))

        def constants1():
            pool.wait_ge(later_loaded, later_count)
            pool.wait_ge(ff.up_ready, 1)
            chain = Chain(pool, head_steps, 6)
            chain.link(pool.memset(ones[:, :], 1.0))
            chain.link(pool.memset(all_ones, 1.0))
            for u in range(SLOTS):
                chain.link(pool.memset(vn[u][:, :, :, :], 0.0))
                chain.link(pool.memset(q_packed[u][SHIFT:P, :, :].bitcast(F32), 0.0))
                chain.link(pool.memset(k_packed[u][SHIFT:P, :, :].bitcast(F32), 1.0))
            chain.link(pool.tensor_copy(mask_own[:, :], mask_own_bytes[:, :]))
            pool.tensor_copy(mask_rows[:, :, :], mask_bytes[:, :, :]).then_inc(masks_ready, 1)
            pool.wait_ge(masks_ready, 1)

        def spread_queries(third):
            s = pk

            def place(m, slot, turn):
                pool.wait_ge(s.loaded[slot], 16 * (ROUNDS + turn + 1))
                pool.sem_inc(idle, 1)
                pool.tensor_tensor(placed_packed[:, 0, :], x[:, ds(m, 1), :].rearrange("p a d -> p (a d)"),
                                   positions[:, :], ALU.add).then_inc(s.placed, 1)
                pool.tensor_tensor(placed_packed[:, 1, :], cn[slot][:, :], positions[:, :], ALU.add).then_inc(s.placed, 1)

            if third:
                place(0, 0, 0)

            def inverse_roots(m):
                chain = Chain(pool, s.rstd_ready, RSTD_STEPS * m)
                rstd, shifted, work = stats.rstd[:, :], stats.shifted[:, :], stats.work[:, :]

                def step(instruction):
                    chain.link(instruction)
                    pool.sem_inc(idle, 1)

                pool.wait_ge(s.prep_chain[1], PREP3 * m + 8)
                pool.sem_inc(idle, 1)
                step(pool.tensor_scalar(shifted, stats.mean_var[:, :, 1], EPS, None, ALU.add))
                step(pool.tensor_scalar(rstd.bitcast(I32), shifted.bitcast(I32), -0.5, 1597463007.0, ALU.mult, ALU.add))
                for _ in range(3):
                    step(pool.tensor_tensor(work, rstd, rstd, ALU.mult))
                    step(pool.tensor_tensor(work, work, shifted, ALU.mult))
                    step(pool.tensor_scalar(work, work, -0.5, 1.5, ALU.mult, ALU.add))
                    step(pool.tensor_tensor(rstd, rstd, work, ALU.mult))

            def window(b, u, core, carry, following, ahead, further, next_turn, ahead_turn):
                n = b + B * third

                def spread(m, slot, pack):
                    pool.wait_ge(s.q_low, 2 * m + pack // 2 + 1)
                    for first in range(PACK * pack, PACK * (pack + 1), SPREAD):
                        heads = slice(first - PACK * pack, first - PACK * pack + SPREAD)
                        wide = [P, SPREAD, D]
                        pool.tensor_tensor(q_spread[slot][:, first:first + SPREAD, :],
                                           q_packed[slot][:, pack:pack + 1, :].bitcast(F32).broadcast_to(wide),
                                           part_of_head[:, heads].unsqueeze(2).broadcast_to(wide), ALU.mult).then_inc(s.spread, 1)

                def spread_ahead(packs):
                    for pack in packs:
                        if core:
                            pool.wait_ge(s.shifted, HN * n + PACK * (pack + 1))
                        spread(n + 2, u, pack)

                if third:
                    if following:
                        if carry:
                            pool.wait_ge(s.shifted, HN * n)
                        spread(n + 1, 1 - u, 2)
                    if ahead:
                        inverse_roots(b + 2)
                    if following:
                        spread(n + 1, 1 - u, 3)
                    if further:
                        pool.wait_ge(s.turned, b + 3)
                        place(b + 3, 1 - u, ahead_turn + u)
                    if ahead:
                        spread_ahead((0, 1))
                else:
                    if following:
                        pool.wait_ge(s.q_projected, 2 * (n + 2))
                        row = x[:, ds(b + 1, 1), :].rearrange("p a d -> p (a d)")
                        pool.tensor_tensor(row, row, mask_rows[:, ds(b + 1, 1), :].rearrange("p a d -> p (a d)"), ALU.mult)\
                            .then_inc(x_masked, 1)
                    if ahead:
                        spread_ahead(range(PACKS))
                    if carry:
                        pool.wait_ge(s.x_added, n)
                        for k, moment in enumerate((mean_t, std_t)):
                            row = moment[:, ds(b - 1, 1), :].rearrange("p a d -> p (a d)")
                            ins = pool.tensor_tensor(row, row, mask_rows[:, ds(b - 1, 1), :].rearrange("p a d -> p (a d)"), ALU.mult)
                        ins.then_inc(moments_masked, 1)

            over_steps(pool, window)

        def layer2(cross):
            s = n2

            def window(b, u, core, carry, following, ahead, further, next_turn, ahead_turn):
                n = b + B * cross
                mask = cross_mask[u] if cross else self_mask
                wide = [P, PACK, P]

                def spread(m):
                    c, first = m // 2, PACK * m % 8
                    pool.tensor_tensor(km[1 - u][:, m * BANK:(m + 1) * BANK].rearrange("p (h k) -> p h k", h=PACK),
                                       kn[1 - u][:, c * P:(c + 1) * P].unsqueeze(1).broadcast_to(wide),
                                       head_of_16[:, first:first + PACK].unsqueeze(2).broadcast_to(wide), ALU.mult)\
                        .then_inc(s.spread, 1)

                for j in range(STEPS):
                    if core:
                        pool.wait_ge(s.masked, STEPS * n + j + 1)
                        scores = scores_masked[j % 2][:, :].rearrange("p (h k) -> p h k", h=PACK)
                        pool.tensor_tensor(scores, scores, mask[:, 1:2, :].broadcast_to(wide), ALU.add).then_inc(s.mask_added, 1)
                    if following and j == 1:
                        pool.wait_ge(s.qk_ready, n + 2)
                        spread(0)
                    elif following and j == 2:
                        spread(1)
                        spread(2)
                    elif following and j == 3:
                        spread(3)

            over_steps(pool, window)

        constants1()
        spread_queries(0)
        layer2(0)
        layer2(1)
        feed_forward_low(1)
        pool.wait_ge(ff.x_added, 2 * ROUNDS)
        spread_queries(1)

    @block.sync
    def _(sp):
        def load_pair(layer, p, q):
            k = str(layer + 1)
            sp.wait_ge(weights_split, p + 1)
            cols = ds(q * D, D)
            for m, name in enumerate("qkv"):
                sp.dma_start(pair_weights[:, m, :].rearrange("p (c n) -> p c n", c=DC),
                             rows(f"L0_xattn_w{name}{k}")[:, :, cols]).then_inc(pair_loaded, 16)
            sp.dma_start(pair_weights[:, 3, :].rearrange("p (h n) -> p h n", h=2),
                         rows(f"L0_xattn_wo{k}")[:, ds(q * 2, 2), :]).then_inc(pair_loaded, 16)
            for m, name in enumerate(("bq", "bk")):
                sp.dma_start(pair_columns[:, m, :], column(f"L0_xattn_{name}{k}")[:, ds(q * 2, 2)],
                             allow_slow_non_contiguous=True).then_inc(pair_loaded, 16)
            for m, name in enumerate(("bias_k", "bias_v")):
                sp.dma_start(pair_columns[:, 2 + m, :], t[f"L0_xattn_{name}{k}"].rearrange("a b h k -> k (a b h)")[:, ds(q * 2, 2)],
                             allow_slow_non_contiguous=True)\
                  .then_inc(pair_loaded, 16)
            sp.dma_start(pair_rows[:, 0, :], t[f"L0_xattn_bv{k}"][cols].partition_broadcast(P)).then_inc(pair_loaded, 16)
            sp.dma_start(pair_rows[:, 1, :], t[f"L0_xattn_bias_v{k}"].rearrange("a b h k -> (a b h k)")[cols].partition_broadcast(P))\
              .then_inc(pair_loaded, 16)

        ctx = t["ctx_2048"]
        sp.sem_inc(out_stored, 16)
        def load_x(g):
            part = slice(GROUP * g, GROUP * (g + 1))
            sp.dma_start(x[:, part, :], t["x"][part].rearrange("b p d -> p b d")).then_inc(x_loaded[g], 16)

        def load_context(g):
            sp.dma_start(ctx_rows[:, g % 2, :, :], ctx[GROUP * g:GROUP * (g + 1)].rearrange("b p d -> p b d"))\
              .then_inc(rows_loaded[g % 2], 16)

        load_context(0)
        load_x(0)
        for target, source in first_loads:
            sp.dma_start(target, source, allow_slow_non_contiguous=True).then_inc(first_loaded, 16)
        load_context(1)
        load_x(1)
        for g in range(2, GROUPS):
            sp.wait_ge(rows_turned, DC * (g - 1))
            load_context(g)
            load_x(g)
        for target, source in small_loads:
            sp.dma_start(target, source, allow_slow_non_contiguous=True).then_inc(small_loaded, 16)
        for layer in range(2):
            with sp.Fori(0, PAIRS) as q:
                load_pair(layer, PAIRS * layer + q, q)
            if layer == 0:
                sp.dma_start(w_up[:, :, :], rows("L0_xattn_w_fc1")).then_inc(weights0_loaded, 16)
                sp.dma_start(w_down[:, :, :], rows("L0_xattn_w_fc2")).then_inc(weights0_loaded, 16)

        sp.wait_ge(x_added, 8 * 2 * PAIRS + ADD_CREDIT)
        sp.wait_ge(weights_split, 2 * PAIRS + 1)
        for target, source in later_loads:
            sp.dma_start(target, source, allow_slow_non_contiguous=True).then_inc(later_loaded, 16)

        def load_rows(sem, u, b):
            sp.dma_start(cn[u][:, :], ctx[ds(b, 1)].rearrange("a p d -> p (a d)")).then_inc(sem, 16)

        def attend(third, free):
            s = pk

            def move_maxima(n, half, slot):
                sp.wait_ge(s.max_low, 2 * n + half + 1)
                for k, source in enumerate((max_high, max_low)):
                    target = q_spread[slot][SHIFT + k:SHIFT + k + 1, half * HALF_HEADS:(half + 1) * HALF_HEADS, :]
                    sp.dma_start(target.bitcast(F32).rearrange("p h (a q) -> p (h a) q", a=UNITS), source[half][:, :].bitcast(F32))\
                      .then_inc(s.max_moved, 16)

            def window(b, u, core, carry, following, ahead, further, next_turn, ahead_turn):
                n = b + B * third
                if third and further:
                    if ahead and following:
                        sp.wait_ge(free, 2 * (b + 2))
                    load_rows(s.loaded[1 - u], 1 - u, b + 3)
                if not third and ahead:
                    if core:
                        sp.wait_ge(free, n + 1)
                    load_rows(s.loaded[u], u, b + 2)
                if core:
                    move_maxima(n, 1, u)
                if following:
                    move_maxima(n + 1, 0, 1 - u)

            if third:
                load_rows(s.loaded[0], 0, 0)
            over_steps(sp, window)

        def load_masked():
            def load_mask(u, b):
                sp.dma_start(cross_mask[u][:, 0, :], t["mask_Bx1xSxS2_ff1"][ds(b, 1)].rearrange("b a q k -> q (b a k)"))\
                  .then_inc(n2.mask_loaded[u], 16)

            for u in range(SLOTS):
                load_rows(n2.loaded[u], u, u)
                load_mask(u, u)
            with sp.Fori(1, ROUNDS) as i:
                for u in range(SLOTS):
                    last = B + SLOTS * (i - 1) + u + 1
                    sp.wait_ge(n2.turned, last)
                    load_rows(n2.loaded[u], u, SLOTS * i + u)
                    sp.wait_ge(n2.mask_added, STEPS * last)
                    load_mask(u, SLOTS * i + u)

        attend(0, pk.in_ready)
        sp.dma_start(w_up[:, :, :], rows("L2_xattn_w1")).then_inc(weights2_loaded, 16)
        sp.dma_start(w_down[:, :, :], rows("L2_xattn_w2")).then_inc(weights2_loaded, 16)
        sp.wait_ge(pk.x_added, B)
        for target, source in loads2:
            sp.dma_start(target, source).then_inc(attention2_loaded, 16)
        sp.wait_ge(n2.x_added, 1)
        load_masked()
        sp.wait_ge(n2.x_added, 2 * B)
        attend(1, pk.placed)
        with sp.Fori(0, ROUNDS) as i:
            sp.wait_ge(result_ready, i + 1)
            sp.dma_start(out[ds(SLOTS * i, SLOTS)].rearrange("b p d -> p b d"), result[:, :, :]).then_inc(out_stored, 16)
        sp.wait_ge(out_stored, 16 * (ROUNDS + 1))


def position_code():
    pos = np.arange(D, dtype=np.float32)[:, None]
    div = np.exp(np.arange(0, P, 2, dtype=np.float32) * np.float32(-np.log(10000.0) / P)).astype(np.float32)
    angle = (pos * div).astype(np.float32)
    code = np.zeros((D, P), np.float32)
    code[:, 0::2] = np.sin(angle)
    code[:, 1::2] = np.cos(angle)
    return np.ascontiguousarray(code.T)


def kernel(**inputs):
    import concourse.bacc as bacc
    from concourse.bass_utils import run_bass_kernel_spmd as run

    nc = bacc.Bacc("TRN2", target_bir_lowering=False, num_devices=1)
    arrays, tensors = {}, {}
    for name, value in inputs.items():
        a = np.ascontiguousarray(value)
        if a.dtype == np.bool_:
            a = a.view(np.uint8)
        arrays[f"in_{name}"] = a
        tensors[name] = nc.dram_tensor(f"in_{name}", a.shape, mybir.dt.from_np(a.dtype), kind="ExternalInput").ap()
    arrays["in_positions"] = position_code()
    tensors["positions"] = nc.dram_tensor("in_positions", (P, D), F32, kind="ExternalInput").ap()
    out = nc.dram_tensor("out", (B, P, D), F32, kind="ExternalOutput").ap()
    build(nc, tensors, out)
    return run(nc, [arrays], core_ids=[0]).results[0]["out"]
```
